# Optimizing a Trainium2 kernel written in Bass

```python
import numpy as np
import jax
import jax.numpy as jnp

def _softmax(x, axis=-1):
    return jax.nn.softmax(x, axis=axis)

def _gelu(x):
    return jax.nn.gelu(x, approximate=True)

def _silu(x):
    return jax.nn.silu(x)

def _sigmoid(x):
    return jax.nn.sigmoid(x)

def _layernorm(x, axis=-1, eps=1e-05):
    m = jnp.mean(x, axis=axis, keepdims=True)
    v = jnp.var(x, axis=axis, keepdims=True)
    return (x - m) / jnp.sqrt(v + eps)

def _scatter_add(tgt, idx, src, axis=0):
    return tgt.at[idx].add(src)

def _segment_sum(src, seg, n):
    return jax.ops.segment_sum(src, seg, n)
kernel_name = 'mk_decoder_preln_d2_seqx_r8_4beb38'

def setup_inputs(seed: int=0):
    np.random.seed(seed)
    _w = jnp.asarray

    def _rec_inputs():
        import jax
        import jax.numpy as jnp
        _rk = jax.random.key(seed)
        x = -0.0002928 + 1 * jax.random.normal(jax.random.fold_in(_rk, 1), (4, 256, 256), jnp.float32)
        _lenS = 256 - jax.random.randint(jax.random.fold_in(_rk, 7), (4,), 0, max(1, 256 // 4) + 1, jnp.int32)
        _lenS2 = 1601 - jax.random.randint(jax.random.fold_in(_rk, 8), (4,), 0, max(1, 1601 // 4) + 1, jnp.int32)
        _ctx_512P = jax.random.normal(jax.random.fold_in(_rk, 11), (4, 16, 64), jnp.float32)
        _ctx_512c = jax.random.dirichlet(jax.random.fold_in(_rk, 511), 0.3 * jnp.ones((16,), jnp.float32), (4, 1601))
        _ctx_512t = jnp.einsum('bsk,bkd->bsd', _ctx_512c, _ctx_512P)
        _ctx_512t = _ctx_512t * jax.lax.rsqrt(jnp.mean(jnp.square(_ctx_512t)) + 1e-12) * 0.953939
        ctx_512 = 0.000227908 + 0.99994 * (_ctx_512t + 0.3 * jax.random.normal(jax.random.fold_in(_rk, 611), (4, 1601, 64), jnp.float32))
        return (x, ctx_512)
    x, ctx_512 = _rec_inputs()

    def _L0_attn_setup():
        import jax, jax.numpy as jnp
        import numpy as np
        H = 16

        def _wkv(k, v, time_decay, time_first):
            decay = jnp.exp(-jnp.exp(time_decay.astype(jnp.float32)))
            first = jnp.exp(time_first.astype(jnp.float32))
            w = jnp.exp(jnp.clip(k.astype(jnp.float32), -10.0, 10.0))
            w = w.at[:, 0].multiply(first)
            wt = jnp.swapaxes(w, 0, 1)
            vt = jnp.swapaxes(v.astype(jnp.float32), 0, 1)

            def step(carry, inp):
                num, den = carry
                w_t, v_t = inp
                num = decay * num + w_t * v_t
                den = decay * den + w_t
                return ((num, den), num / (den + 1e-06))
            B, _, _, S = k.shape
            init = (jnp.zeros((B, H, S), jnp.float32), jnp.zeros((B, H, S), jnp.float32))
            _, wkv = jax.lax.scan(step, init, (wt, vt))
            return jnp.swapaxes(wkv, 0, 1).astype(k.dtype)
        key = jax.random.key(seed)
        ks = jax.random.split(key, 5)
        B, T, C = (4, 256, 256)
        S = C // H
        g = 0.5 * (6.0 / (C + C)) ** 0.5 * 3.0 ** 0.5
        x = jax.random.normal(ks[0], (B, T, C), dtype=jnp.float32)
        Wk = jax.random.uniform(ks[1], (C, C), jnp.float32, -g, g)
        Wv = jax.random.uniform(ks[2], (C, C), jnp.float32, -g, g)
        Wr = jax.random.uniform(ks[3], (C, C), jnp.float32, -g, g)
        Wo = jax.random.uniform(ks[4], (C, C), jnp.float32, -g, g)
        time_decay = jnp.full((H, S), -5.0, dtype=jnp.float32)
        time_first = jnp.zeros((H, S), dtype=jnp.float32)
        return {'x': x, 'Wk': Wk, 'Wv': Wv, 'Wr': Wr, 'Wo': Wo, 'time_decay': time_decay, 'time_first': time_first}
    _L0_attn_all = _L0_attn_setup()
    _L0_attn_in = {k: v for k, v in _L0_attn_all.items() if k in ('Wk', 'Wv', 'Wr', 'Wo', 'time_decay', 'time_first')}
    del _L0_attn_all

    def _L0_xattn_setup():
        import jax, jax.numpy as jnp
        import numpy as np
        B, S, L = (2, 128, 128)
        DIM_Q, H, K, D_C, D_CQ, R = (256, 16, 128, 64, 192, 64)

        def _rope_tables(length, dim):
            inv = 1.0 / 10000.0 ** (jnp.arange(0, dim, 2, dtype=jnp.float32) / dim)
            f = jnp.arange(length, dtype=jnp.float32)[:, None] * inv[None, :]
            sin = jnp.repeat(jnp.sin(f), 2, axis=-1)
            cos = jnp.repeat(jnp.cos(f), 2, axis=-1)
            return (sin, cos)

        def _rotate_half(x):
            half = x.shape[-1] // 2
            return jnp.concatenate([-x[..., half:], x[..., :half]], axis=-1)

        def _apply_rope(x, sin, cos):
            return x * cos + _rotate_half(x) * sin
        key = jax.random.key(seed)
        ks = jax.random.split(key, 8)
        return {'hidden_q': jax.random.normal(ks[0], (B, S, DIM_Q), jnp.float32), 'kv_c': jax.random.normal(ks[1], (B, L, D_C), jnp.float32), 'Wq': jax.random.normal(ks[2], (H * K, DIM_Q), jnp.float32) / np.sqrt(DIM_Q).astype(np.float32), 'w_kc_q': jax.random.normal(ks[3], (H, K, D_CQ), jnp.float32) / np.sqrt(K).astype(np.float32), 'w_kc_kv': jax.random.normal(ks[4], (H, K, D_C), jnp.float32) / np.sqrt(K).astype(np.float32), 'W_qr': jax.random.normal(ks[5], (H, D_CQ, R), jnp.float32) / np.float32(np.sqrt(D_CQ) * np.sqrt(R)), 'W_kr': jax.random.normal(ks[6], (H, D_C, R), jnp.float32) / np.sqrt(D_C).astype(np.float32), 'Wo': jax.random.normal(ks[7], (DIM_Q, H * K), jnp.float32) / np.sqrt(H * K).astype(np.float32)}
    _L0_xattn_all = _L0_xattn_setup()
    _L0_xattn_in = {k: v for k, v in _L0_xattn_all.items() if k in ('Wq', 'w_kc_q', 'w_kc_kv', 'W_qr', 'W_kr', 'Wo')}
    del _L0_xattn_all

    def _L0_ffn_setup():
        import math
        import jax, jax.numpy as jnp
        import numpy as np
        CAPACITY_FACTOR = 1.25
        MIN_CAPACITY = 4

        def _capacity(num_tokens: int, num_experts: int) -> int:
            cap = math.floor(CAPACITY_FACTOR * num_tokens / num_experts)
            cap += cap % 2
            return max(cap, MIN_CAPACITY)
        key = jax.random.key(seed)
        k1, k2, k3, k4 = jax.random.split(key, 4)
        B, S, H, I, E = (2, 512, 256, 256, 8)
        inputs = jax.random.normal(k1, (B, S, H), dtype=jnp.float32)
        gate_weight = jax.random.normal(k2, (E, H), dtype=jnp.float32) * math.sqrt(0.1 / H)
        w1 = jax.random.normal(k3, (E, H, I), dtype=jnp.float32) * 0.02
        w2 = jax.random.normal(k4, (E, I, H), dtype=jnp.float32) * 0.02
        return {'inputs': inputs, 'gate_weight': gate_weight, 'w1': w1, 'w2': w2}
    _L0_ffn_all = _L0_ffn_setup()
    _L0_ffn_in = {k: v for k, v in _L0_ffn_all.items() if k in ('gate_weight', 'w1', 'w2')}
    del _L0_ffn_all

    def _L1_attn_setup():
        import jax, jax.numpy as jnp
        import numpy as np
        B, S, HID = (2, 256, 256)
        H, HKV, D = (16, 4, 128)
        ROPE_BASE = 1000000.0
        EPS = 1e-05

        def _layernorm(x, g, b):
            mu = jnp.mean(x, axis=-1, keepdims=True)
            var = jnp.mean(jnp.square(x - mu), axis=-1, keepdims=True)
            return (x - mu) * jax.lax.rsqrt(var + EPS) * g + b

        def _rope_tables(seq_len, dim, base):
            inv_freq = 1.0 / base ** (jnp.arange(0, dim, 2, dtype=jnp.float32) / dim)
            t = jnp.arange(seq_len, dtype=jnp.float32)
            freqs = jnp.outer(t, inv_freq)
            cos = jnp.concatenate([jnp.cos(freqs), jnp.cos(freqs)], axis=-1)
            sin = jnp.concatenate([jnp.sin(freqs), jnp.sin(freqs)], axis=-1)
            return (cos, sin)

        def _rotate_half(x):
            x1, x2 = jnp.split(x, 2, axis=-1)
            return jnp.concatenate([-x2, x1], axis=-1)
        key = jax.random.key(seed)
        k1, k2, k3 = jax.random.split(key, 3)
        return {'x': jax.random.normal(k1, (B, S, HID), dtype=jnp.float32), 'w_qkv': jax.random.normal(k2, ((H + 2 * HKV) * D, HID), dtype=jnp.float32) * 0.02, 'w_o': jax.random.normal(k3, (HID, H * D), dtype=jnp.float32) * 0.02, 'qn_g': jnp.ones((D,), jnp.float32), 'qn_b': jnp.zeros((D,), jnp.float32), 'kn_g': jnp.ones((D,), jnp.float32), 'kn_b': jnp.zeros((D,), jnp.float32)}
    _L1_attn_all = _L1_attn_setup()
    _L1_attn_in = {k: v for k, v in _L1_attn_all.items() if k in ('w_qkv', 'w_o', 'qn_g', 'qn_b', 'kn_g', 'kn_b')}
    del _L1_attn_all

    def _L1_xattn_setup():
        import jax, jax.numpy as jnp
        import numpy as np
        B, S, H, NH, L = (2, 256, 256, 16, 64)
        HD = H // NH
        key = jax.random.key(seed)
        k1, k2, k3, k4, k5 = jax.random.split(key, 5)
        scale = 0.02
        return {'q': jax.random.normal(k1, (B, S, H), dtype=jnp.float32), 'latent_kv': jax.random.normal(k2, (B, S, L), dtype=jnp.float32), 'Wq': jax.random.normal(k3, (H, H), dtype=jnp.float32) * scale, 'Wkv_expand': jax.random.normal(k4, (2 * H, L), dtype=jnp.float32) * scale, 'Wout': jax.random.normal(k5, (H, H), dtype=jnp.float32) * scale}
    _L1_xattn_all = _L1_xattn_setup()
    _L1_xattn_in = {k: v for k, v in _L1_xattn_all.items() if k in ('Wq', 'Wkv_expand', 'Wout')}
    del _L1_xattn_all

    def _L1_ffn_setup():
        import jax, jax.numpy as jnp
        import numpy as np
        DIM = 256
        EXPERT_DIM = 128
        N_EXPERTS = 16
        TOPK = 2
        N_SHARED = 1
        B, T = (4, 256)
        key = jax.random.key(seed)
        ks = jax.random.split(key, 9)
        s = 0.02
        return {'x': jax.random.normal(ks[0], (B, T, DIM), jnp.float32), 'router_w': jax.random.normal(ks[1], (N_EXPERTS, DIM), jnp.float32) * s, 'router_bias': jnp.zeros((N_EXPERTS,), jnp.float32), 'Wu': jax.random.normal(ks[2], (N_EXPERTS, DIM, EXPERT_DIM), jnp.float32) * s, 'Wg': jax.random.normal(ks[3], (N_EXPERTS, DIM, EXPERT_DIM), jnp.float32) * s, 'Wd': jax.random.normal(ks[4], (N_EXPERTS, EXPERT_DIM, DIM), jnp.float32) * s, 'Su': jax.random.normal(ks[5], (N_SHARED, DIM, EXPERT_DIM * TOPK), jnp.float32) * s, 'Sg': jax.random.normal(ks[6], (N_SHARED, DIM, EXPERT_DIM * TOPK), jnp.float32) * s, 'Sd': jax.random.normal(ks[7], (N_SHARED, EXPERT_DIM * TOPK, DIM), jnp.float32) * s}
    _L1_ffn_all = _L1_ffn_setup()
    _L1_ffn_in = {k: v for k, v in _L1_ffn_all.items() if k in ('router_w', 'router_bias', 'Wu', 'Wg', 'Wd', 'Su', 'Sg', 'Sd')}
    del _L1_ffn_all
    return {'x': x, 'ctx_512': ctx_512, 'L0_attn_Wk': _L0_attn_in['Wk'], 'L0_attn_Wv': _L0_attn_in['Wv'], 'L0_attn_Wr': _L0_attn_in['Wr'], 'L0_attn_Wo': _L0_attn_in['Wo'], 'L0_attn_time_decay': _L0_attn_in['time_decay'], 'L0_attn_time_first': _L0_attn_in['time_first'], 'L0_xattn_Wq': _L0_xattn_in['Wq'], 'L0_xattn_w_kc_q': _L0_xattn_in['w_kc_q'], 'L0_xattn_w_kc_kv': _L0_xattn_in['w_kc_kv'], 'L0_xattn_W_qr': _L0_xattn_in['W_qr'], 'L0_xattn_W_kr': _L0_xattn_in['W_kr'], 'L0_xattn_Wo': _L0_xattn_in['Wo'], 'L0_ffn_gate_weight': _L0_ffn_in['gate_weight'], 'L0_ffn_w1': _L0_ffn_in['w1'], 'L0_ffn_w2': _L0_ffn_in['w2'], 'L1_attn_w_qkv': _L1_attn_in['w_qkv'], 'L1_attn_w_o': _L1_attn_in['w_o'], 'L1_attn_qn_g': _L1_attn_in['qn_g'], 'L1_attn_qn_b': _L1_attn_in['qn_b'], 'L1_attn_kn_g': _L1_attn_in['kn_g'], 'L1_attn_kn_b': _L1_attn_in['kn_b'], 'L1_xattn_Wq': _L1_xattn_in['Wq'], 'L1_xattn_Wkv_expand': _L1_xattn_in['Wkv_expand'], 'L1_xattn_Wout': _L1_xattn_in['Wout'], 'L1_ffn_router_w': _L1_ffn_in['router_w'], 'L1_ffn_router_bias': _L1_ffn_in['router_bias'], 'L1_ffn_Wu': _L1_ffn_in['Wu'], 'L1_ffn_Wg': _L1_ffn_in['Wg'], 'L1_ffn_Wd': _L1_ffn_in['Wd'], 'L1_ffn_Su': _L1_ffn_in['Su'], 'L1_ffn_Sg': _L1_ffn_in['Sg'], 'L1_ffn_Sd': _L1_ffn_in['Sd']}

def reference(x, ctx_512, L0_attn_Wk, L0_attn_Wv, L0_attn_Wr, L0_attn_Wo, L0_attn_time_decay, L0_attn_time_first, L0_xattn_Wq, L0_xattn_w_kc_q, L0_xattn_w_kc_kv, L0_xattn_W_qr, L0_xattn_W_kr, L0_xattn_Wo, L0_ffn_gate_weight, L0_ffn_w1, L0_ffn_w2, L1_attn_w_qkv, L1_attn_w_o, L1_attn_qn_g, L1_attn_qn_b, L1_attn_kn_g, L1_attn_kn_b, L1_xattn_Wq, L1_xattn_Wkv_expand, L1_xattn_Wout, L1_ffn_router_w, L1_ffn_router_bias, L1_ffn_Wu, L1_ffn_Wg, L1_ffn_Wd, L1_ffn_Su, L1_ffn_Sg, L1_ffn_Sd):
    import jax
    import jax.numpy as jnp

    def _L0_attn_ref(x, Wk, Wv, Wr, Wo, time_decay, time_first):
        import jax, jax.numpy as jnp
        import numpy as np
        H = 16

        def _wkv(k, v, time_decay, time_first):
            decay = jnp.exp(-jnp.exp(time_decay.astype(jnp.float32)))
            first = jnp.exp(time_first.astype(jnp.float32))
            w = jnp.exp(jnp.clip(k.astype(jnp.float32), -10.0, 10.0))
            w = w.at[:, 0].multiply(first)
            wt = jnp.swapaxes(w, 0, 1)
            vt = jnp.swapaxes(v.astype(jnp.float32), 0, 1)

            def step(carry, inp):
                num, den = carry
                w_t, v_t = inp
                num = decay * num + w_t * v_t
                den = decay * den + w_t
                return ((num, den), num / (den + 1e-06))
            B, _, _, S = k.shape
            init = (jnp.zeros((B, H, S), jnp.float32), jnp.zeros((B, H, S), jnp.float32))
            _, wkv = jax.lax.scan(step, init, (wt, vt))
            return jnp.swapaxes(wkv, 0, 1).astype(k.dtype)
        B, T, C = x.shape
        S = C // H
        k = (x @ Wk.T).reshape(B, T, H, S)
        v = (x @ Wv.T).reshape(B, T, H, S)
        r = (x @ Wr.T).reshape(B, T, H, S)
        wkv = _wkv(k, v, time_decay, time_first)
        rwkv = (jax.nn.sigmoid(r) * wkv).reshape(B, T, C)
        return rwkv @ Wo.T

    def _L0_xattn_ref(hidden_q, kv_c, Wq, w_kc_q, w_kc_kv, W_qr, W_kr, Wo):
        import jax, jax.numpy as jnp
        import numpy as np
        B, S, L = (2, 128, 128)
        DIM_Q, H, K, D_C, D_CQ, R = (256, 16, 128, 64, 192, 64)

        def _rope_tables(length, dim):
            inv = 1.0 / 10000.0 ** (jnp.arange(0, dim, 2, dtype=jnp.float32) / dim)
            f = jnp.arange(length, dtype=jnp.float32)[:, None] * inv[None, :]
            sin = jnp.repeat(jnp.sin(f), 2, axis=-1)
            cos = jnp.repeat(jnp.cos(f), 2, axis=-1)
            return (sin, cos)

        def _rotate_half(x):
            half = x.shape[-1] // 2
            return jnp.concatenate([-x[..., half:], x[..., :half]], axis=-1)

        def _apply_rope(x, sin, cos):
            return x * cos + _rotate_half(x) * sin
        Bv, Sv, _ = hidden_q.shape
        _, Lv, _ = kv_c.shape
        q_hk = (hidden_q @ Wq.T).reshape(Bv, Sv, H, K)
        q_big = jnp.einsum('bshk,hkq->bshq', q_hk, w_kc_q)
        sin_q, cos_q = _rope_tables(Sv, D_CQ)
        q_big = _apply_rope(q_big, sin_q[None, :, None, :], cos_q[None, :, None, :])
        sin_k, cos_k = _rope_tables(Lv, D_C)
        kv_r = _apply_rope(kv_c, sin_k[None], cos_k[None])
        q_r = jnp.einsum('bshq,hqr->bhsr', q_big, W_qr)
        k_r = jnp.einsum('bld,hdr->bhlr', kv_r, W_kr)
        scores = jnp.einsum('bhsr,bhlr->bhsl', q_r, k_r)
        attn = jax.nn.softmax(scores, axis=-1)
        ctx_c = jnp.einsum('bhsl,bld->bhsd', attn, kv_r)
        ctx_lat = jnp.einsum('bhsd,hkd->bhsk', ctx_c, w_kc_kv)
        ctx = ctx_lat.transpose(0, 2, 1, 3).reshape(Bv, Sv, H * K)
        return ctx @ Wo.T

    def _L0_ffn_ref(inputs, gate_weight, w1, w2):
        import math
        import jax, jax.numpy as jnp
        import numpy as np
        CAPACITY_FACTOR = 1.25
        MIN_CAPACITY = 4

        def _capacity(num_tokens: int, num_experts: int) -> int:
            cap = math.floor(CAPACITY_FACTOR * num_tokens / num_experts)
            cap += cap % 2
            return max(cap, MIN_CAPACITY)
        B, S, H = inputs.shape
        E = gate_weight.shape[0]
        tokens = inputs.reshape(-1, H)
        T = tokens.shape[0]
        C = _capacity(T, E)
        logits = tokens.astype(jnp.float32) @ gate_weight.astype(jnp.float32).T
        probs = jax.nn.softmax(logits, axis=-1)
        top1 = jnp.argmax(logits, axis=-1)
        mask = jax.nn.one_hot(top1, E, dtype=jnp.int32)
        ranks = jnp.cumsum(mask, axis=0) - 1
        mask = mask * (ranks < C).astype(jnp.int32)
        rank1 = jnp.sum(mask * ranks, axis=-1)
        weight = mask.astype(probs.dtype) * probs
        rank_oh = jax.nn.one_hot(rank1, C, dtype=probs.dtype)
        combine_weights = weight[:, :, None] * rank_oh[:, None, :]
        sec_mask = (combine_weights != 0).astype(inputs.dtype)
        dispatch = jnp.einsum('tec,th->ech', sec_mask, tokens)
        hmid = jax.nn.gelu(jnp.einsum('ech,ehi->eci', dispatch, w1), approximate=False)
        expert_out = jnp.einsum('eci,eih->ech', hmid, w2)
        out = jnp.einsum('tec,ech->th', combine_weights.astype(inputs.dtype), expert_out)
        return out.reshape(B, S, H)

    def _L1_attn_ref(x, w_qkv, w_o, qn_g, qn_b, kn_g, kn_b):
        import jax, jax.numpy as jnp
        import numpy as np
        B, S, HID = (2, 256, 256)
        H, HKV, D = (16, 4, 128)
        ROPE_BASE = 1000000.0
        EPS = 1e-05

        def _layernorm(x, g, b):
            mu = jnp.mean(x, axis=-1, keepdims=True)
            var = jnp.mean(jnp.square(x - mu), axis=-1, keepdims=True)
            return (x - mu) * jax.lax.rsqrt(var + EPS) * g + b

        def _rope_tables(seq_len, dim, base):
            inv_freq = 1.0 / base ** (jnp.arange(0, dim, 2, dtype=jnp.float32) / dim)
            t = jnp.arange(seq_len, dtype=jnp.float32)
            freqs = jnp.outer(t, inv_freq)
            cos = jnp.concatenate([jnp.cos(freqs), jnp.cos(freqs)], axis=-1)
            sin = jnp.concatenate([jnp.sin(freqs), jnp.sin(freqs)], axis=-1)
            return (cos, sin)

        def _rotate_half(x):
            x1, x2 = jnp.split(x, 2, axis=-1)
            return jnp.concatenate([-x2, x1], axis=-1)
        b, s, _ = x.shape
        qkv = jnp.einsum('bsh,oh->bso', x, w_qkv)
        q, k, v = jnp.split(qkv, [H * D, (H + HKV) * D], axis=-1)
        q = q.reshape(b, s, H, D).transpose(0, 2, 1, 3)
        k = k.reshape(b, s, HKV, D).transpose(0, 2, 1, 3)
        v = v.reshape(b, s, HKV, D).transpose(0, 2, 1, 3)
        q = _layernorm(q, qn_g, qn_b)
        k = _layernorm(k, kn_g, kn_b)
        cos, sin = _rope_tables(s, D, ROPE_BASE)
        q = q * cos + _rotate_half(q) * sin
        k = k * cos + _rotate_half(k) * sin
        rep = H // HKV
        k = jnp.repeat(k, rep, axis=1)
        v = jnp.repeat(v, rep, axis=1)
        scores = jnp.einsum('bhqd,bhkd->bhqk', q, k) / jnp.sqrt(jnp.float32(D))
        causal = jnp.triu(jnp.ones((s, s), dtype=bool), k=1)
        scores = jnp.where(causal, -jnp.inf, scores)
        weights = jax.nn.softmax(scores, axis=-1)
        attn = jnp.einsum('bhqk,bhkd->bhqd', weights, v)
        attn = attn.transpose(0, 2, 1, 3).reshape(b, s, H * D)
        return jnp.einsum('bsd,od->bso', attn, w_o)

    def _L1_xattn_ref(q, latent_kv, Wq, Wkv_expand, Wout):
        import jax, jax.numpy as jnp
        import numpy as np
        B, S, H, NH, L = (2, 256, 256, 16, 64)
        HD = H // NH
        b, sq, _ = q.shape
        sk = latent_kv.shape[1]
        qp = q @ Wq.T
        kv = latent_kv @ Wkv_expand.T
        k, v = jnp.split(kv, 2, axis=-1)
        qh = qp.reshape(b, sq, NH, HD).transpose(0, 2, 1, 3)
        kh = k.reshape(b, sk, NH, HD).transpose(0, 2, 1, 3)
        vh = v.reshape(b, sk, NH, HD).transpose(0, 2, 1, 3)
        inv_sqrt_d = 1.0 / jnp.sqrt(jnp.float32(HD))
        scores = jnp.einsum('bhqd,bhkd->bhqk', qh, kh) * inv_sqrt_d
        causal = jnp.tril(jnp.ones((sq, sk), dtype=bool))
        scores = jnp.where(causal, scores, jnp.finfo(scores.dtype).min)
        attn = jax.nn.softmax(scores, axis=-1)
        out = jnp.einsum('bhqk,bhkd->bhqd', attn, vh)
        out = out.transpose(0, 2, 1, 3).reshape(b, sq, H)
        return out @ Wout.T

    def _L1_ffn_ref(x, router_w, router_bias, Wu, Wg, Wd, Su, Sg, Sd):
        import jax, jax.numpy as jnp
        import numpy as np
        DIM = 256
        EXPERT_DIM = 128
        N_EXPERTS = 16
        TOPK = 2
        N_SHARED = 1
        B, T = (4, 256)
        Bx, Tx, D = x.shape
        flat = x.reshape(Bx * Tx, D)
        logits = flat @ router_w.T
        scores = jax.nn.softmax(logits, axis=-1)
        _, topk_idx = jax.lax.top_k(logits + router_bias, TOPK)
        topk_scores = jnp.take_along_axis(scores, topk_idx, axis=-1)
        topk_scores = topk_scores / topk_scores.sum(-1, keepdims=True)
        combine = jnp.einsum('nk,nke->ne', topk_scores, jax.nn.one_hot(topk_idx, N_EXPERTS, dtype=scores.dtype))
        out = jnp.zeros_like(flat)
        for e in range(N_EXPERTS):
            h = jax.nn.silu(flat @ Wu[e]) * (flat @ Wg[e])
            out = out + combine[:, e:e + 1] * (h @ Wd[e])
        for s in range(N_SHARED):
            out = out + jax.nn.silu(flat @ Su[s]) * (flat @ Sg[s]) @ Sd[s]
        return out.reshape(Bx, Tx, D)
    x = x + _L0_attn_ref(_layernorm(x, axis=-1), L0_attn_Wk, L0_attn_Wv, L0_attn_Wr, L0_attn_Wo, L0_attn_time_decay, L0_attn_time_first)
    x = x + _L0_xattn_ref(_layernorm(x, axis=-1), ctx_512, L0_xattn_Wq, L0_xattn_w_kc_q, L0_xattn_w_kc_kv, L0_xattn_W_qr, L0_xattn_W_kr, L0_xattn_Wo)
    x = x + _L0_ffn_ref(_layernorm(x, axis=-1), L0_ffn_gate_weight, L0_ffn_w1, L0_ffn_w2)
    x = x + _L1_attn_ref(_layernorm(x, axis=-1), L1_attn_w_qkv, L1_attn_w_o, L1_attn_qn_g, L1_attn_qn_b, L1_attn_kn_g, L1_attn_kn_b)
    x = x + _L1_xattn_ref(_layernorm(x, axis=-1), ctx_512, L1_xattn_Wq, L1_xattn_Wkv_expand, L1_xattn_Wout)
    x = x + _L1_ffn_ref(_layernorm(x, axis=-1), L1_ffn_router_w, L1_ffn_router_bias, L1_ffn_Wu, L1_ffn_Wg, L1_ffn_Wd, L1_ffn_Su, L1_ffn_Sg, L1_ffn_Sd)
    return x

_drawn_inputs = setup_inputs


def setup_inputs(seed=0):
    import zlib

    import numpy as np

    out = dict(_drawn_inputs(seed))
    spreads = {'L0_attn_time_decay': (-5.0, 0.6),
     'L0_attn_time_first': (0.0, 0.8),
     'L1_attn_qn_g': (1.0, 0.6),
     'L1_attn_qn_b': (0.0, 0.8),
     'L1_attn_kn_g': (1.0, 0.6),
     'L1_attn_kn_b': (0.0, 0.8),
     'L1_ffn_router_bias': (0.0, 0.8)}
    factors = {'L0_ffn_gate_weight': 5.539,
     'L0_ffn_w1': 5.104,
     'L0_ffn_w2': 5.001,
     'L1_xattn_Wq': 8.0,
     'L1_ffn_router_w': 7.414,
     'L1_ffn_Wu': 6.924,
     'L1_ffn_Wg': 6.839,
     'L1_ffn_Wd': 6.829,
     'L1_ffn_Su': 3.535,
     'L1_ffn_Sg': 3.474,
     'L1_ffn_Sd': 3.491}
    for name, (base, spread) in spreads.items():
        noise = np.random.default_rng([zlib.crc32(name.encode()), seed]).standard_normal(out[name].shape)
        drawn = base * np.exp(spread * noise) if base else spread * noise
        out[name] = jnp.asarray(drawn.astype(out[name].dtype))
    for name, factor in factors.items():
        out[name] = (out[name] * factor).astype(out[name].dtype)
    return out
```

```python
from contextlib import ExitStack

import numpy as np

import concourse.bass as bass
from concourse import mybir

P = 128
F32 = mybir.dt.float32
F32R = mybir.dt.float32r
ALU = mybir.AluOpType
ACT = mybir.ActivationFunctionType
AX = mybir.AxisListType.X
LN_EPS = 1e-5
LAST = 6

B, T, C = 4, 256, 256
NT = B * T // P
KC = C // P
HALF = 512
L = 1601
LT = (L + P - 1) // P
LREST = L - (LT - 1) * P
D = 64
H = 16
PAIRS = H // 2
QW = 192
E0, E1 = 8, 16
CAP0 = 160
E1X = E1 + 2
HKV = 4
NEG = -1e30


class PsumBanks:

    def __init__(self, psum, filled, emptied):
        self.psum, self.filled_sem, self.emptied_sem = psum, filled, emptied
        self.jobs, self.order, self.count = {}, [], {e: 0 for e in emptied}
        self.taken = {e: 0 for e in emptied}

    def claim(self, key, by):
        assert key not in self.jobs, key
        self.count[by] += 1
        self.jobs[key] = (len(self.order), by, self.count[by])
        self.order.append(key)
        return self.bank(key)

    def bank(self, key):
        n = self.jobs[key][0] % 8
        return self.psum[:, n * 512:(n + 1) * 512]

    def earlier(self, key):
        n = self.jobs[key][0]
        return self.order[n - 8] if n >= 8 else None

    def filled(self, key):
        return self.filled_sem, self.jobs[key][0] + 1

    def emptied(self, key):
        _, by, n = self.jobs[key]
        return self.emptied_sem[by], n

    def take(self, key, by):
        self.taken[by] += 1
        assert self.jobs[key][1:] == (by, self.taken[by]), (key, self.jobs[key], self.taken)
        return self.bank(key)


def decoder(nc, x, ctx_512, L0_attn_Wk, L0_attn_Wv, L0_attn_Wr, L0_attn_Wo, L0_attn_time_decay, L0_attn_time_first,
            L0_xattn_Wq, L0_xattn_w_kc_q, L0_xattn_w_kc_kv, L0_xattn_W_qr, L0_xattn_W_kr, L0_xattn_Wo,
            L0_ffn_gate_weight, L0_ffn_w1, L0_ffn_w2, L1_attn_w_qkv, L1_attn_w_o, L1_attn_qn_g, L1_attn_qn_b,
            L1_attn_kn_g, L1_attn_kn_b, L1_xattn_Wq, L1_xattn_Wkv_expand, L1_xattn_Wout, L1_ffn_router_w,
            L1_ffn_router_bias, L1_ffn_Wu, L1_ffn_Wg, L1_ffn_Wd, L1_ffn_Su, L1_ffn_Sg, L1_ffn_Sd,
            ident_c, cosq_c, sinq_c, cosk_c, sink_c, rev_c, tri_c, cos1_c, sin1_c, mask0_c, mask1_c, hmask_c, out):
    with ExitStack() as ctx:
        base = [nc.sbuf_base]

        def sb(name, shape, dt=F32):
            return ctx.enter_context(nc.sbuf_tensor(name, shape, dt))

        def sem(name):
            return ctx.enter_context(nc.semaphore(name))

        X = sb("X", [P, NT, C])
        ident = sb("ident", [P, P])
        stats = sb("stats", [P, NT, 6])
        mv = sb("mv", [P, NT, 2])
        rstd = sb("rstd", [P, NT])
        ones = sb("ones", [P, P])
        pool_tick = sb("pool_tick", [P, 8])
        arena = nc.sbuf_base
        room = nc.sbuf_usable_end - arena

        def at(name, offset, shape, dt=F32):
            size = int(np.prod(shape[1:])) * 4
            assert offset + size <= room, (name, offset + size, room)
            return nc.alloc_sbuf_tensor_at(name, shape, dt, offset=arena + offset)

        HN = at("HN", 168192, [P, NT, C])
        HT = at("HT", 176384, [P, KC, NT * P])
        PS = ctx.enter_context(nc.psum_tensor("PS", [P, 8 * 512], F32))

        r_nat = at("r_nat", 112672, [P, 4, KC, C])
        r_wt = at("r_wt", 120864, [P, 4, KC, C])
        r_w = at("r_w", 0, [P, KC, B * T])
        r_wv = at("r_wv", 8192, [P, KC, B * T])
        r_sig = at("r_sig", 16384, [P, KC, B * T])
        r_num = at("r_num", 24576, [P, KC, B * T])
        r_den = at("r_den", 32768, [P, KC, B * T])
        r_decay = at("r_decay", 40960, [P, KC, B * T])
        r_ones = at("r_ones", 49152, [P, B * T])
        r_td = at("r_td", 53248, [P, KC])
        r_tf = at("r_tf", 53280, [P, KC])
        r_dec = at("r_dec", 53312, [P, KC])

        KVR = at("KVR", 91168, [P, B, LT, D])
        U = at("U", 184576, [P, PAIRS, C])
        cosk = at("cosk", 192768, [P, LT, D])
        sink = at("sink", 196096, [P, LT, D])
        DUP = at("DUP", 192768, [P, LT, 2 * D])
        kt1 = at("kt1", 138304, [P, LT, D])
        kt2 = at("kt2", 141632, [P, LT, D])
        x_wq = at("x_wq", 112672, [P, H, C])
        x_kcq = at("x_kcq", 129056, [P, H, QW])
        x_wqr = at("x_wqr", 141344, [P, 24, D])
        x_wkr = at("x_wkr", 147488, [P, 8, D])
        x_wo = at("x_wo", 149536, [P, KC, H * P])
        x_kckv = at("x_kckv", 192768, [P, H, D])
        WqrT = at("WqrT", 0, [D, H * QW])
        WqrS = at("WqrS", 12288, [D, H * QW])
        WkrT = at("WkrT", 24576, [D, H * D])
        x_woT = at("x_woT", 28672, [P, H, C])
        W1 = at("W1", 65536, [P, KC, H * QW])
        W2 = at("W2", 112672, [P, PAIRS, 2, 256])
        cosq = at("cosq", 129056, [P, 3, HALF])
        sinq = at("sinq", 135200, [P, 3, HALF])
        zc = at("zc", 141344, [P, 2, 3, HALF])
        zs = at("zs", 153632, [P, 2, 3, HALF])
        qlo = at("qlo", 165920, [P, 2, HALF], F32R)
        QALL = at("QALL", 0, [P, B, PAIRS, 2, T], F32R)
        KH = at("KH", 65536, [P, L + 1], F32R)
        KL = at("KL", 71968, [P, L + 1], F32R)
        SC = [[at(f"S{s}{h}", 112672 + 6432 * (2 * s + h), [P, L]) for h in range(2)] for s in range(2)]
        PT = at("PT", 138432, [P, LT, 2, P])
        CTX = at("CTX", 151744, [P, PAIRS, B * T])
        QC = [at(f"QC{s}", 78400 + 1024 * s, [P, 2, P], F32R) for s in range(2)]
        mx = at("mx", 80448, [P, 2, 2, 2])
        sm = at("sm", 80512, [P, 2, 2])
        ri = at("ri", 80544, [P, 2, 2])

        g_nat = at("g_nat", 34816, [E0, C])
        g_T = at("g_T", 35840, [P, KC, E0])
        f_w1 = at("f_w1", 0, [P, E0, KC, C])
        f_w2 = at("f_w2", 16384, [P, E0, KC, C])
        f_rev = at("f_rev", 36352, [P, NT, E1])
        f_tri = at("f_tri", 37376, [P, P])
        f_l = at("f_l", 38400, [P, NT, E1])
        f_e = at("f_e", 39424, [P, NT, E1])
        f_b = at("f_b", 40448, [P, NT, E1])
        f_v = at("f_v", 41472, [P, NT, E1])
        f_oh = at("f_oh", 42496, [P, NT, E1])
        f_oh2 = at("f_oh2", 43520, [P, NT, E1])
        f_pre = at("f_pre", 44544, [P, NT, E1])
        f_mx = at("f_mx", 45568, [P, 4, NT])
        f_comb = at("f_comb", 45824, [P, NT, E1X])
        f_h = at("f_h", 47104, [P, 2, 2, HALF])

        a_nat = at("a_nat", 61440, [P, 24, C])
        a_wo = at("a_wo", 86016, [P, KC, H * P])
        QKT = at("QKT", 0, [P, 20, B * T])
        a_wT = at("a_wT", 102400, [P, KC, 24 * P])
        a_woT = at("a_woT", 126976, [P, H, C])
        a_v = at("a_v", 143360, [P, NT, HKV * P])
        a_sq = at("a_sq", 86016, [P, 2, HALF])
        a_m1 = at("a_m1", 186624, [P, 2, HALF])
        a_m2 = at("a_m2", 190720, [P, 2, HALF])
        a_mu = at("a_mu", 194816, [P, KC, 20])
        a_ss = at("a_ss", 194976, [P, 2, 4])
        a_gc = at("a_gc", 195072, [P, 2, 2, P])
        a_gs = at("a_gs", 197120, [P, 2, 2, P])
        a_bt = at("a_bt", 199168, [P, 2, 2, P])
        a_cos = at("a_cos", 184576, [P, 2, P])
        a_sin = at("a_sin", 185600, [P, 2, P])
        a_gb = at("a_gb", 186624, [P, 4, P])
        a_tmp = at("a_tmp", 188672, [P, 2, P])
        s_sc = at("s_sc", 102400, [P, 2, 4, 2 * P])
        s_pt = at("s_pt", 110592, [P, 2, 2, HALF])
        s_mask0 = at("s_mask0", 118784, [P, HALF])
        s_mask1 = at("s_mask1", 120832, [P, HALF])
        s_mx = at("s_mx", 122880, [P, 2, 4])
        s_sm = at("s_sm", 122912, [P, 2, 4])
        s_ri = at("s_ri", 122944, [P, 2, 4])

        y_lat = at("y_lat", 123008, [P, B * 2, D])
        y_wq = at("y_wq", 143360, [P, KC, C])
        y_wo = at("y_wo", 145408, [P, KC, C])
        y_wkv = at("y_wkv", 147456, [P, 4, D])
        y_wT = at("y_wT", 148480, [P, 2, KC, C])
        y_kvT = at("y_kvT", 152576, [D, 4 * P])
        y_latT = at("y_latT", 154624, [D, B, T])
        y_hm = at("y_hm", 158720, [P, 8])
        y_q = at("y_q", 184576, [P, KC, B * T])
        y_ax = at("y_ax", 192768, [P, KC, B * T])
        y_km = at("y_km", 0, [P, B, KC, 8, T], F32)
        VP = 1152
        y_vm = at("y_vm", 65536, [P, B, 2, VP])
        y_v = at("y_v", 126976, [P, B, 2, C])

        m_wu = at("m_wu", 0, [P, E1X, KC, P])
        m_wg = at("m_wg", 65536, [P, E1X, KC, P])
        m_wd = at("m_wd", 84480, [P, E1X, C])
        m_rw = at("m_rw", 102944, [E1, C])
        m_rT = at("m_rT", 104000, [P, KC, E1])
        m_rb = at("m_rb", 104128, [P, E1])
        m_su = at("m_su", 104416, [P, 2, HALF])
        m_h = at("m_h", 108512, [P, 2, HALF])

        filled = sem("bank_filled")
        emptied = {"act": sem("bank_emptied_by_act"), "dve": sem("bank_emptied_by_dve")}
        banks = PsumBanks(PS, filled, emptied)
        x_loaded = sem("x_loaded")
        consts_loaded = sem("consts_loaded")
        rwkv_loaded = sem("rwkv_weights_loaded")
        xattn_loaded = sem("xattn_weights_loaded")
        kv_cleared = sem("kv_tail_cleared")
        kv_loaded = sem("kv_loaded")
        rope_loaded = sem("query_rope_loaded")
        q_moved = [sem("query_low_parts_moved_even"), sem("query_low_parts_moved_odd")]
        moe0_loaded = sem("moe0_weights_loaded")
        gqa_loaded = sem("gqa_weights_loaded")
        gqa_bcast = sem("gqa_tables_loaded")
        masks_loaded = sem("masks_loaded")
        lat_loaded = sem("latent_weights_loaded")
        moe1_loaded = sem("moe1_weights_loaded")
        stored = sem("output_stored")
        phase_ended = sem("phase_ended")
        var_ready = sem("variances_ready")
        std_ready = sem("deviations_ready")
        hvar_ready = sem("head_variances_ready")
        hstd_ready = sem("head_deviations_ready")
        hn_ready = sem("normalised_tiles")
        dve_step = sem("dve_step")
        act_step = sem("act_step")
        pool_step = sem("pool_step")
        ones_set = sem("ones_set")
        w_exp = sem("rwkv_exp_ready")
        decay_exp = sem("decay_exp_ready")
        rw_ready = sem("rwkv_mixed")
        kv_roped = sem("kv_roped")
        wqr_shift = sem("wqr_shifted")
        q_high = sem("query_high_parts")
        dup_ready = sem("kv_duplicated")
        kh_ready = sem("key_high_parts")
        qc_ready = sem("query_tile_ready")
        sc_full = sem("scores_filled")
        sc_out = sem("scores_emptied")
        p_exp = sem("probs_exponentiated")
        p_rec = sem("prob_sums_inverted")
        p_norm = sem("probs_normalised")
        t_full = sem("turned_filled")
        t_act = sem("turned_emptied_by_act")
        t_dve = sem("turned_emptied_by_dve")
        av_full = sem("context_filled")
        av_out = sem("context_emptied")
        mask_ready = sem("expert_choice_ready")
        e_shift = sem("logits_shifted")
        e_exp = sem("logits_exponentiated")
        comb_ready = sem("combine_ready")
        sq_ready = sem("squares_ready")
        m_part = sem("rotated_parts")
        m_sum = sem("rotated_summed")
        qk_ready = sem("rotated_ready")
        sh_ready = sem("scores_shifted")
        se_ready = sem("scores_exponentiated")
        si_ready = sem("sums_inverted")
        sn_ready = sem("softmax_ready")
        vm_ready = sem("masked_values_ready")

        A_UNITS = [(b, g, st) for b in range(B) for g in range(HKV) for st in range(2)]
        Y_UNITS = [(b, ct, hg, st) for ct in range(KC) for b in range(B) for hg in range(2) for st in range(2)]
        ctx.enter_context(nc.allow_non_contiguous_dma(reason="small strided loads"))
        block = ctx.enter_context(nc.Block())

        def ended(eng, n):
            eng.drain().then_inc(phase_ended, 1)
            eng.wait_ge(phase_ended, 4 * (n + 1))

        @block.tensor
        def _(pe):
            def begin(key, by):
                ps = banks.claim(key, by)
                if banks.earlier(key) is not None:
                    pe.wait_ge(*banks.emptied(banks.earlier(key)))
                return ps

            def mm(o, a, b, start=True, stop=True, **kw):
                return nc.tensor.matmul(o, a, b, start=start, stop=stop, **kw)

            def turn(key, by, parts):
                ps = begin(key, by)
                c = 0
                for a in parts:
                    r, w = a.shape
                    last = nc.tensor.transpose(ps[0:w, c:c + r], a, ident[0:r, 0:r])
                    c += r
                last.then_inc(filled, 1)

            def turn_x(k):
                for g in range(2):
                    pe.wait_ge(hn_ready, NT * k + 4 * (g + 1))
                    for kc in range(KC):
                        turn(("ht", k, g, kc), "act" if kc else "dve",
                             [HN[:, 4 * g + i, kc * P:(kc + 1) * P] for i in range(4)])

            def wait_ht(k, halves=2):
                for g in range(halves):
                    for kc in range(KC):
                        pe.wait_ge(*banks.emptied(("ht", k, g, kc)))

            def chan_product(key, by, w, half):
                ps = begin(key, by)
                for kc in range(KC):
                    last = mm(ps, w(kc), HT[:, kc, half * HALF:(half + 1) * HALF], kc == 0, kc == KC - 1)
                last.then_inc(filled, 1)

            def out_product(key, pairs):
                ps = begin(key, "dve")
                for i, (a, b) in enumerate(pairs):
                    last = mm(ps[:, 0:C], a, b, i == 0, i == len(pairs) - 1)
                last.then_inc(filled, 1)

            pe.wait_ge(consts_loaded, 16)
            pe.wait_ge(rwkv_loaded, 16 * 6)
            for w in range(4):
                turn(("rwt", w), "act", [r_nat[:, w, ot, kc * P:(kc + 1) * P] for kc in range(KC) for ot in range(KC)])
            turn_x(0)
            wait_ht(0)
            pe.wait_ge(*banks.emptied(("rwt", 3)))
            for half in range(2):
                for ct in range(KC):
                    for w in range(3):
                        chan_product(("kvr", w, ct, half), ("dve", "dve", "act")[w],
                                     lambda kc: r_wt[:, w, kc, ct * P:(ct + 1) * P], half)
            pe.wait_ge(rw_ready, KC)
            for t in range(NT):
                out_product(("ro", t), [(r_num[:, ct, t * P:(t + 1) * P], r_wt[:, 3, ct, :]) for ct in range(KC)])
            ended(pe, 0)
            if LAST == 1:
                return

            pe.wait_ge(xattn_loaded, 16 * 6)
            for h in range(H):
                ps = begin(("w1", h), "act" if h % 2 else "dve")
                for kc in range(KC):
                    last = mm(ps[:, kc * QW:(kc + 1) * QW], x_wq[:, h, kc * P:(kc + 1) * P], x_kcq[:, h, :])
                last.then_inc(filled, 1)
            for g in range(6):
                turn(("wqr", g), "act", [x_wqr[:, 4 * g + i, :] for i in range(4)])
            for g in range(2):
                turn(("wkr", g), "act", [x_wkr[:, 4 * g + i, :] for i in range(4)])
            for g in range(8):
                turn(("xwo", g), "dve", [x_wo[:, ot, h * P:(h + 1) * P] for h in (2 * g, 2 * g + 1) for ot in range(KC)])
            turn_x(1)
            pe.wait_ge(*banks.emptied(("xwo", 7)))
            for g in range(4):
                ps = begin(("u", g), "act")
                for i in range(2):
                    for s in range(2):
                        h = 4 * g + 2 * i + s
                        last = mm(ps[s * D:(s + 1) * D, i * C:(i + 1) * C], x_kckv[:, h, :], x_woT[:, h, :])
                last.then_inc(filled, 1)
            pe.wait_ge(*banks.emptied(("wkr", 1)))
            pe.wait_ge(wqr_shift, 2)
            for p in range(PAIRS):
                ps = begin(("w2", p), "dve")
                for c, w in enumerate((WqrT, WqrS)):
                    A = WkrT[:, 2 * p * D:(2 * p + 1) * D]
                    A2 = WkrT[:, (2 * p + 1) * D:(2 * p + 2) * D]
                    o, g = 256 * c, 3 * p * P
                    mm(ps[:, o:o + 64], w[:, g:g + P], A)
                    mm(ps[0:64, o + 64:o + 128], w[:, g + P:g + P + 64], A)
                    mm(ps[64:128, o + 128:o + 192], w[:, g + P + 64:g + 2 * P], A2)
                    last = mm(ps[:, o + 192:o + 256], w[:, g + 2 * P:g + 3 * P], A2)
                last.then_inc(filled, 1)
            ended(pe, 1)

            def z_jobs(n):
                p, half = n // 2, n % 2
                for j in range(3):
                    chan_product(("z", p, half, j), "dve", lambda kc: W1[:, kc, (3 * p + j) * P:(3 * p + j + 1) * P], half)

            def q_job(n):
                p, half, s = n // 2, n % 2, n % 2
                pe.wait_ge(*banks.emptied(("z", p, half, 2)))
                ps = begin(("q", p, half), "dve")
                for c, r in enumerate((zc, zs)):
                    mm(ps[0:64, :], W2[:, p, c, 0:64], r[:, s, 0, :], c == 0, False, skip_group_check=True)
                    mm(ps[64:128, :], W2[:, p, c, 192:256], r[:, s, 2, :], c == 0, False, skip_group_check=True)
                for c, r in enumerate((zc, zs)):
                    last = mm(ps, W2[:, p, c, 64:192], r[:, s, 1, :], False, c == 1, skip_group_check=True)
                last.then_inc(filled, 1)

            wait_ht(1)
            z_jobs(0)
            for n in range(2 * PAIRS):
                if n + 1 < 2 * PAIRS:
                    z_jobs(n + 1)
                q_job(n)
            ended(pe, 2)

            for b in range(B):
                for g in range(4):
                    pe.wait_ge(dup_ready, 2 * (b + 1))
                    turn(("kt", b, g), "dve", [DUP[0:P if lt < LT - 1 else LREST, lt, :]
                                               for lt in range(4 * g, min(4 * g + 4, LT))])
                pe.wait_ge(*banks.emptied(("kt", b, 3)))

                def scores(v, st, hd):
                    pe.wait_ge(qc_ready, 16 * b + v + 1)
                    n = 2 * (16 * b + v) + hd
                    for half, chunks in enumerate((((0, 512), (512, 1024)), ((1024, 1536), (1536, L + 1)))):
                        if b > 0 or half == 0 and hd == 1 or not isinstance(v, int) or v > 0 or hd == 1:
                            pe.wait_ge(sc_out, 2 * n - 1 + half)
                        for a, z in chunks:
                            mm(PS[:, a:z], QC[st][:, hd, :], KH[:, a:z], True, False)
                            last = mm(PS[:, a:z], QC[st][:, hd, :], KL[:, a:z], False, True)
                        last.then_inc(sc_full, 1)

                def turns(v, st, groups, first):
                    for g in groups:
                        n = 7 * (16 * b + v) + g
                        if g == 0:
                            pe.wait_ge(p_norm, 2 * (16 * b + v + 1))
                        if g >= 3:
                            m = g - 3
                            e, k = (t_act, 4) if m % 2 == 0 else (t_dve, 3)
                            pe.wait_ge(e, k * (16 * b + v) + m // 2 + 1)
                        elif not (first and b == 0):
                            m = (6, 4, 5)[g]
                            e, k = (t_act, 4) if m % 2 == 0 else (t_dve, 3)
                            pe.wait_ge(e, k * (16 * b + v - 1) + m // 2 + 1)
                        ps = PS[:, (4 + g % 3) * 512:(5 + g % 3) * 512]
                        c = 0
                        for lt in range(2 * g, min(2 * g + 2, LT)):
                            w = P if lt < LT - 1 else LREST
                            for hd in range(2):
                                last = nc.tensor.transpose(ps[0:w, c:c + P], SC[st][hd][:, lt * P:lt * P + w], ident[:, :])
                                c += P
                        last.then_inc(t_full, 1)

                def context(v, st, first):
                    pe.wait_ge(t_act, 4 * (16 * b + v + 1))
                    pe.wait_ge(t_dve, 3 * (16 * b + v + 1))
                    if not (first and b == 0):
                        pe.wait_ge(av_out, 16 * b + v)
                    for lt in range(LT):
                        w = P if lt < LT - 1 else LREST
                        for hd in range(2):
                            last = mm(PS[hd * D:(hd + 1) * D, 3584 + st * P:3584 + (st + 1) * P],
                                      KVR[0:w, b, lt, :], PT[0:w, lt, hd, :], lt == 0, lt == LT - 1)
                    last.then_inc(av_full, 1)

                def tile(v, st, first=False):
                    scores(v, st, 0)
                    if not first:
                        turns(v - 1, 1 - st, range(0, 4), v_first[0])
                    scores(v, st, 1)
                    if not first:
                        turns(v - 1, 1 - st, range(4, 7), v_first[0])
                        context(v - 1, 1 - st, v_first[0])

                v_first = [False]
                tile(0, 0, True)
                v_first[0] = True
                tile(1, 1)
                v_first[0] = False
                with pe.Fori(1, PAIRS) as j:
                    tile(2 * j, 0)
                    tile(2 * j + 1, 1)
                turns(15, 1, range(7), False)
                context(15, 1, False)
                ended(pe, 3 + b)
            for t in range(NT):
                out_product(("xo", t), [(CTX[:, p, t * P:(t + 1) * P], U[:, p, :]) for p in range(PAIRS)])
            ended(pe, 7)
            if LAST == 2:
                return

            pe.wait_ge(moe0_loaded, 16 * 5)
            turn(("gT", 0), "act", [g_nat[:, 0:P]])
            turn(("gT", 1), "act", [g_nat[:, P:C]])
            turn_x(2)
            wait_ht(2)
            pe.wait_ge(*banks.emptied(("gT", 1)))
            ps = begin("logits0", "dve")
            for t in range(NT):
                for kc in range(KC):
                    last = mm(ps[:, t * E0:(t + 1) * E0], HT[:, kc, t * P:(t + 1) * P], g_T[:, kc, :], kc == 0, kc == KC - 1)
            last.then_inc(filled, 1)
            pe.wait_ge(mask_ready, NT - 1)
            ps = begin("rank0", "dve")
            mm(ps[:, 0:NT * E0], f_tri[:, :], f_oh[:, :, 0:E0], True, False)
            mm(ps[:, 0:NT * E0], ones[:, :], f_pre[:, :, 0:E0], False, True).then_inc(filled, 1)

            def down0(n):
                e, half, s = n // 2, n % 2, n % 2
                pe.wait_ge(*banks.emptied(("u0", n, 1)))
                for i in range(2):
                    ps = begin(("d0", n, i), "dve")
                    for tt in range(2):
                        for it in range(KC):
                            o = (2 * i + tt) * P
                            last = mm(ps[:, tt * C:(tt + 1) * C], f_h[:, s, it, o:o + P], f_w2[:, e, it, :], it == 0, it == 1)
                    last.then_inc(filled, 1)

            for n in range(2 * E0 + 1):
                if n < 2 * E0:
                    for it in range(KC):
                        chan_product(("u0", n, it), "act", lambda kc: f_w1[:, n // 2, kc, it * P:(it + 1) * P], n % 2)
                if n >= 1:
                    down0(n - 1)
            ended(pe, 8)
            if LAST == 3:
                return

            pe.wait_ge(gqa_loaded, 32)
            for kc in range(KC):
                for g in range(6):
                    turn(("awT", kc, g), "act", [a_nat[:, 4 * g + i, kc * P:(kc + 1) * P] for i in range(4)])
            for g in range(8):
                turn(("awo", g), "act", [a_wo[:, ot, h * P:(h + 1) * P] for h in (2 * g, 2 * g + 1) for ot in range(KC)])
            turn_x(3)
            wait_ht(3)
            ended(pe, 9)

            def qkv(t):
                for g in range(6):
                    ps = begin(("qkv", t, g), "dve" if g < 5 else "act")
                    for kc in range(KC):
                        last = mm(ps, HT[:, kc, t * P:(t + 1) * P], a_wT[:, kc, g * HALF:(g + 1) * HALF], kc == 0, kc == 1)
                    last.then_inc(filled, 1)
                    n = 5 * t + g
                    if g < 5 and n >= 1:
                        qk_turn(n - 1)

            def qk_turn(n):
                pe.wait_ge(qk_ready, n + 1)
                turn(("qkT", n), "act", [a_m1[:, n % 2, i * P:(i + 1) * P] for i in range(4)])

            for t in range(NT):
                qkv(t)
            qk_turn(5 * NT - 1)
            ended(pe, 10)

            def softmax_units(tag, units, base_n, score, use):
                for n in range(len(units) + 1):
                    if n < len(units):
                        score(n, units[n])
                    if n >= 1:
                        m, st = n - 1, units[n - 1][-1]
                        pe.wait_ge(sn_ready, base_n + m + 1)
                        for kb in range(st + 1):
                            turn((tag, "pt", m, kb), "act", [s_sc[:, m % 2, i, kb * P:(kb + 1) * P] for i in range(4)])
                        for kb in range(st + 1):
                            pe.wait_ge(*banks.emptied((tag, "pt", m, kb)))
                        use(m, units[m])

            def a_score(n, unit):
                b, g, st = unit
                tok = slice((2 * b + st) * P, (2 * b + st + 1) * P)
                nk = P * (st + 1)
                for i in range(st + 1):
                    ps = begin(("a", "s", n, i), "dve")
                    for j in range(4 // (st + 1)):
                        h = 4 * g + i * 2 + j
                        last = mm(ps[:, j * nk:(j + 1) * nk], QKT[:, h, tok], QKT[:, H + g, 2 * b * P:2 * b * P + nk])
                    last.then_inc(filled, 1)

            def a_use(n, unit):
                b, g, st = unit
                ps = begin(("a", "o", n), "dve")
                for kb in range(st + 1):
                    last = mm(ps, a_v[:, 2 * b + kb, g * P:(g + 1) * P], s_pt[:, n % 2, kb, :], kb == 0, kb == st)
                last.then_inc(filled, 1)

            softmax_units("a", A_UNITS, 0, a_score, a_use)
            pe.wait_ge(*banks.emptied(("a", "o", len(A_UNITS) - 1)))
            for t in range(NT):
                out_product(("ao", t), [(QKT[:, h, t * P:(t + 1) * P], a_woT[:, h, :]) for h in range(H)])
            ended(pe, 11)
            if LAST == 4:
                return

            pe.wait_ge(lat_loaded, 16 * (4 + B))
            for w, nat in enumerate((y_wq, y_wo)):
                turn(("ywT", w), "act", [nat[:, ot, kc * P:(kc + 1) * P] for kc in range(KC) for ot in range(KC)])
            turn("ykvT", "act", [y_wkv[:, i, :] for i in range(4)])
            for g in range(2):
                turn(("ylat", g), "act", [y_lat[:, 4 * g + i, :] for i in range(4)])
            turn_x(4)
            pe.wait_ge(*banks.emptied(("ylat", 1)))
            for ct in range(KC):
                for g in range(2):
                    ps = begin(("yk", ct, g), "dve")
                    mm(ps, y_kvT[:, ct * P:(ct + 1) * P], y_latT[:, 2 * g:2 * g + 2, :]).then_inc(filled, 1)
            for b in range(B):
                ps = begin(("yv", b), "act")
                for kb in range(2):
                    last = mm(ps[:, kb * C:(kb + 1) * C], y_latT[:, b, kb * P:(kb + 1) * P], y_kvT[:, 2 * P:4 * P])
                last.then_inc(filled, 1)
            wait_ht(4)
            for ct in range(KC):
                for half in range(2):
                    chan_product(("yq", ct, half), "act", lambda kc: y_wT[:, 0, kc, ct * P:(ct + 1) * P], half)
            for ct in range(KC):
                for half in range(2):
                    pe.wait_ge(*banks.emptied(("yq", ct, half)))
                for g in range(2):
                    pe.wait_ge(*banks.emptied(("yk", ct, g)))

            def y_score(n, unit):
                b, ct, hg, st = unit
                tok = slice((2 * b + st) * P, (2 * b + st + 1) * P)
                for i in range(st + 1):
                    ps = begin(("y", "s", n, i), "dve")
                    h0 = 4 * hg + 2 * i
                    keys = y_km[:, b, ct, h0:h0 + 4 - 2 * st, 0:P * (st + 1)]
                    mm(ps, y_q[:, ct, tok], keys).then_inc(filled, 1)

            def y_use(n, unit):
                b, ct, hg, st = unit
                ps = begin(("y", "o", n), "dve")
                pe.wait_ge(vm_ready, 8 * ct + 2 * (b + 1))
                for i in range(4):
                    for kb in range(st + 1):
                        h = 4 * hg + i
                        last = mm(ps[:, 0:P], y_vm[:, b, kb, h * P:(h + 1) * P], s_pt[:, n % 2, kb, i * P:(i + 1) * P],
                                  i == 0 and kb == 0, i == 3 and kb == st)
                last.then_inc(filled, 1)

            softmax_units("y", Y_UNITS, len(A_UNITS), y_score, y_use)
            pe.wait_ge(*banks.emptied(("y", "o", len(Y_UNITS) - 1)))
            for t in range(NT):
                out_product(("yo", t), [(y_ax[:, ct, t * P:(t + 1) * P], y_wT[:, 1, ct, :]) for ct in range(KC)])
            ended(pe, 12)
            if LAST == 5:
                return

            pe.wait_ge(moe1_loaded, 16 * 11)
            turn("mrT", "act", [m_rw[:, 0:P], m_rw[:, P:C]])
            turn_x(5)
            wait_ht(5)
            pe.wait_ge(*banks.emptied("mrT"))
            ps = begin("logits1", "dve")
            for t in range(NT):
                for kc in range(KC):
                    last = mm(ps[:, t * E1:(t + 1) * E1], HT[:, kc, t * P:(t + 1) * P], m_rT[:, kc, :], kc == 0, kc == KC - 1)
            last.then_inc(filled, 1)

            def down1(n):
                e, s = n // 2, n % 2
                pe.wait_ge(*banks.emptied(("g1", n)))
                for i in range(2):
                    ps = begin(("d1", n, i), "dve")
                    for tt in range(2):
                        o = (2 * i + tt) * P
                        last = mm(ps[:, tt * C:(tt + 1) * C], m_h[:, s, o:o + P], m_wd[:, e, :])
                    last.then_inc(filled, 1)

            for n in range(2 * E1X + 1):
                if n < 2 * E1X:
                    chan_product(("u1", n), "act", lambda kc: m_wu[:, n // 2, kc, :], n % 2)
                    chan_product(("g1", n), "dve", lambda kc: m_wg[:, n // 2, kc, :], n % 2)
                if n >= 1:
                    down1(n - 1)
            ended(pe, 13)

        @block.scalar
        def _(act):
            steps = [0]

            def link(ins):
                steps[0] += 1
                ins.then_inc(act_step, 1)
                act.wait_ge(act_step, steps[0])

            def copy_out(key, dst, src=None):
                ps = banks.take(key, "act")
                act.wait_ge(*banks.filled(key))
                nc.scalar.activation(dst, src(ps) if src else ps, ACT.Copy).then_inc(emptied["act"], 1)

            def deviations(k):
                act.wait_ge(var_ready, k + 1)
                nc.scalar.activation(rstd[:, :], rstd[:, :], ACT.Sqrt).then_inc(std_ready, 1)

            def ht_out(k):
                for g in range(2):
                    copy_out(("ht", k, g, 1), HT[:, 1, g * HALF:(g + 1) * HALF])

            deviations(0)
            act.wait_ge(rwkv_loaded, 16 * 6)
            link(nc.scalar.activation(r_dec[:, :], r_td[:, :], ACT.Exp))
            nc.scalar.activation(r_dec[:, :], r_dec[:, :], ACT.Exp, scale=-1.0).then_inc(decay_exp, 1)
            link(nc.scalar.activation(r_tf[:, :], r_tf[:, :], ACT.Exp))
            for w in range(4):
                copy_out(("rwt", w), r_wt[:, w, :, :])
            ht_out(0)
            for half in range(2):
                for ct in range(KC):
                    n = half * KC + ct
                    cols = slice(half * HALF, (half + 1) * HALF)
                    act.wait_ge(*banks.emptied(("kvr", 0, ct, half)))
                    nc.scalar.activation(r_w[:, ct, cols], r_w[:, ct, cols], ACT.Exp).then_inc(w_exp, 1)
                    ps = banks.take(("kvr", 2, ct, half), "act")
                    act.wait_ge(*banks.filled(("kvr", 2, ct, half)))
                    nc.scalar.activation(r_sig[:, ct, cols], ps, ACT.Sigmoid).then_inc(emptied["act"], 1)
            ended(act, 0)
            if LAST == 1:
                return

            deviations(1)
            for h in range(1, H, 2):
                copy_out(("w1", h), W1[:, :, h * QW:(h + 1) * QW],
                         lambda ps: ps[:, 0:KC * QW].rearrange("p (k q) -> p k q", k=KC))
            for g in range(6):
                copy_out(("wqr", g), WqrT[:, g * HALF:(g + 1) * HALF], lambda ps: ps[0:D, :])
            for g in range(2):
                copy_out(("wkr", g), WkrT[:, g * HALF:(g + 1) * HALF], lambda ps: ps[0:D, :])
            ht_out(1)
            for g in range(4):
                copy_out(("u", g), U[:, 2 * g:2 * g + 2, :])
            ended(act, 1)
            for n in range(2 * PAIRS):
                p, half = n // 2, n % 2
                act.wait_ge(*banks.filled(("q", p, half)))
                for s in range(2):
                    rows = slice(s * D, (s + 1) * D)
                    src = banks.bank(("q", p, half))[rows, :].rearrange("p (b t) -> p b t", b=2)
                    nc.scalar.activation(QALL[rows, 2 * half:2 * half + 2, p, s, :], src, ACT.Copy).then_inc(q_high, 1)
            ended(act, 2)
            for b in range(B):
                for g in range(4):
                    act.wait_ge(*banks.filled(("kt", b, g)))
                    w = min(HALF, L - g * HALF)
                    nc.scalar.activation(KH[:, g * HALF:g * HALF + w], banks.bank(("kt", b, g))[:, 0:w],
                                         ACT.Copy).then_inc(kh_ready, 1)

                def exps(v, st, hd):
                    act.wait_ge(sc_out, 2 * (2 * (16 * b + v) + hd + 1))
                    nc.scalar.activation(SC[st][hd][:, :], SC[st][hd][:, :], ACT.Exp, bias=mx[:, st, hd, 1:2], scale=-1.0,
                                         accum_out=sm[:, st, hd:hd + 1]).then_inc(p_exp, 1)

                def turned(v, g, first=False):
                    act.wait_ge(t_full, 7 * (16 * b + v) + g + 1)
                    if g == 0 and not (first and b == 0):
                        act.wait_ge(av_full, 16 * b + v)
                    lt = 2 * g
                    if g < 6:
                        nc.scalar.activation(PT[:, lt:lt + 2, :, :], PS[:, (4 + g % 3) * 512:(5 + g % 3) * 512],
                                             ACT.Copy).then_inc(t_act, 1)
                    else:
                        nc.scalar.activation(PT[0:LREST, lt, :, :], PS[0:LREST, 4 * 512:4 * 512 + 2 * P],
                                             ACT.Copy).then_inc(t_act, 1)

                def context(j, v, st):
                    act.wait_ge(av_full, 16 * b + v + 1)
                    nc.scalar.activation(CTX[:, j, (2 * b + st) * P:(2 * b + st + 1) * P],
                                         PS[:, 3584 + st * P:3584 + (st + 1) * P], ACT.Copy).then_inc(av_out, 1)

                def tile(j, v, st, prev_j=None, first=False):
                    if prev_j is not None:
                        turned(v - 1, 0, first)
                        turned(v - 1, 2)
                    exps(v, st, 0)
                    if prev_j is not None:
                        turned(v - 1, 4)
                        turned(v - 1, 6)
                    exps(v, st, 1)
                    if prev_j is not None:
                        context(prev_j, v - 1, 1 - st)

                tile(0, 0, 0)
                tile(0, 1, 1, 0, True)
                with act.Fori(1, PAIRS) as j:
                    tile(j, 2 * j, 0, bass.ds(j - 1, 1))
                    tile(j, 2 * j + 1, 1, bass.ds(j, 1))
                for g in (0, 2, 4, 6):
                    turned(15, g)
                context(PAIRS - 1, 15, 1)
                ended(act, 3 + b)
            ended(act, 7)
            if LAST == 2:
                return

            deviations(2)
            copy_out(("gT", 0), g_T[:, 0, :], lambda ps: ps[:, 0:E0])
            copy_out(("gT", 1), g_T[:, 1, :], lambda ps: ps[:, 0:E0])
            ht_out(2)
            act.wait_ge(e_shift, 1)
            nc.scalar.activation(f_e[:, :, 0:E0], f_b[:, :, 0:E0], ACT.Exp).then_inc(e_exp, 1)
            for n in range(2 * E0):
                for it in range(KC):
                    key = ("u0", n, it)
                    ps = banks.take(key, "act")
                    act.wait_ge(*banks.filled(key))
                    if n >= 2:
                        act.wait_ge(*banks.filled(("d0", n - 2, 1)))
                    nc.scalar.activation(f_h[:, n % 2, it, :], ps, ACT.Gelu).then_inc(emptied["act"], 1)
            ended(act, 8)
            if LAST == 3:
                return

            deviations(3)
            for kc in range(KC):
                for g in range(6):
                    copy_out(("awT", kc, g), a_wT[:, kc, g * HALF:(g + 1) * HALF])
            for g in range(8):
                copy_out(("awo", g), a_woT[:, 2 * g:2 * g + 2, :])
            ht_out(3)
            ended(act, 9)

            def qk_out(n):
                t, g = n // 5, n % 5
                copy_out(("qkT", n), QKT[:, 4 * g:4 * g + 4, t * P:(t + 1) * P])

            for n in range(5 * NT + 2):
                if n < 5 * NT:
                    key = ("qkv", n // 5, n % 5)
                    act.wait_ge(*banks.filled(key))
                    if n >= 2:
                        act.wait_ge(hvar_ready, n - 1)
                    nc.scalar.activation(a_sq[:, n % 2, :], banks.bank(key), ACT.Square).then_inc(sq_ready, 1)
                if 1 <= n <= 5 * NT:
                    act.wait_ge(hvar_ready, n)
                    nc.scalar.activation(a_ss[:, (n - 1) % 2, :], a_ss[:, (n - 1) % 2, :], ACT.Sqrt).then_inc(hstd_ready, 1)
                if n >= 2:
                    qk_out(n - 2)
                    if (n - 2) % 5 == 3:
                        copy_out(("qkv", (n - 2) // 5, 5), a_v[:, (n - 2) // 5, :])
            ended(act, 10)

            def softmax_units(tag, units, base_n):
                for n in range(len(units) + 1):
                    if n < len(units):
                        st = units[n][-1]
                        nk = P * (st + 1)
                        act.wait_ge(sh_ready, base_n + n + 1)
                        sc = s_sc[:, n % 2, :, 0:nk]
                        nc.scalar.activation(sc, sc, ACT.Exp).then_inc(se_ready, 1)
                    if n >= 1:
                        m = n - 1
                        for kb in range(units[m][-1] + 1):
                            if m >= 2:
                                act.wait_ge(*banks.filled((tag, "o", m - 2)))
                            copy_out((tag, "pt", m, kb), s_pt[:, m % 2, kb, :])

            softmax_units("a", A_UNITS, 0)
            ended(act, 11)
            if LAST == 4:
                return

            deviations(4)
            for w in range(2):
                copy_out(("ywT", w), y_wT[:, w, :, :])
            copy_out("ykvT", y_kvT[:, :], lambda ps: ps[0:D, :])
            for g in range(2):
                copy_out(("ylat", g), y_latT[:, 2 * g:2 * g + 2, :], lambda ps: ps[0:D, :])
            ht_out(4)
            for b in range(B):
                copy_out(("yv", b), y_v[:, b, :, :])
            for ct in range(KC):
                for half in range(2):
                    copy_out(("yq", ct, half), y_q[:, ct, half * HALF:(half + 1) * HALF])
            softmax_units("y", Y_UNITS, len(A_UNITS))
            ended(act, 12)
            if LAST == 5:
                return

            deviations(5)
            copy_out("mrT", m_rT[:, :, :], lambda ps: ps[:, 0:KC * E1])
            ht_out(5)
            act.wait_ge(e_shift, 2)
            nc.scalar.activation(f_e[:, :, :], f_e[:, :, :], ACT.Exp).then_inc(e_exp, 1)
            for n in range(2 * E1X):
                key = ("u1", n)
                ps = banks.take(key, "act")
                act.wait_ge(*banks.filled(key))
                if n >= 2:
                    act.wait_ge(*banks.emptied(("g1", n - 2)))
                nc.scalar.activation(m_su[:, n % 2, :], ps, ACT.Silu).then_inc(emptied["act"], 1)
            ended(act, 13)

        @block.vector
        def _(dve):
            steps = [0]

            def link(ins):
                steps[0] += 1
                ins.then_inc(dve_step, 1)
                dve.wait_ge(dve_step, steps[0])

            V = nc.vector

            def copy_out(key, dst, src=None):
                ps = banks.take(key, "dve")
                dve.wait_ge(*banks.filled(key))
                V.tensor_copy(dst, src(ps) if src else ps).then_inc(emptied["dve"], 1)

            def normalise(k):
                for t in range(NT):
                    V.bn_stats(stats[:, t, :], X[:, t, :]).then_inc(dve_step, 1)
                steps[0] += NT
                for t in range(NT):
                    dve.wait_ge(dve_step, steps[0] - NT + t + 1)
                    V.bn_aggr(mv[:, t, :], stats[:, t, :]).then_inc(dve_step, 1)
                steps[0] += NT
                dve.wait_ge(dve_step, steps[0])
                V.tensor_scalar(rstd[:, :], mv[:, :, 1], LN_EPS, None, ALU.add).then_inc(var_ready, 1)
                dve.wait_ge(std_ready, k + 1)
                link(V.reciprocal(rstd[:, :], rstd[:, :]))
                for t in range(NT):
                    V.tensor_scalar(HN[:, t, :], X[:, t, :], mv[:, t, 0:1], rstd[:, t:t + 1],
                                    ALU.subtract, ALU.mult).then_inc(hn_ready, 1)

            def ht_out(k):
                for g in range(2):
                    copy_out(("ht", k, g, 0), HT[:, 0, g * HALF:(g + 1) * HALF])

            def residual(key, t):
                ps = banks.take(key, "dve")
                dve.wait_ge(*banks.filled(key))
                V.tensor_tensor(X[:, t, :], X[:, t, :], ps[:, 0:C], ALU.add).then_inc(emptied["dve"], 1)

            dve.wait_ge(x_loaded, 16 * NT)
            normalise(0)
            ht_out(0)
            dve.wait_ge(ones_set, 1)
            dve.wait_ge(decay_exp, 1)
            for ct in range(KC):
                link(V.tensor_scalar(r_decay[:, ct, :], r_ones[:, :], r_dec[:, ct:ct + 1], None, ALU.mult))
                link(V.memset(r_decay[:, ct, :].rearrange("p (b t) -> p b t", b=B)[:, :, 0:1], 0.0))
            for half in range(2):
                for ct in range(KC):
                    n = half * KC + ct
                    cols = slice(half * HALF, (half + 1) * HALF)
                    ps = banks.take(("kvr", 0, ct, half), "dve")
                    dve.wait_ge(*banks.filled(("kvr", 0, ct, half)))
                    V.tensor_scalar(r_w[:, ct, cols], ps, -10.0, 10.0, ALU.max, ALU.min).then_inc(emptied["dve"], 1)
                    dve.wait_ge(w_exp, n + 1)
                    first = r_w[:, ct, cols].rearrange("p (b t) -> p b t", b=2)[:, :, 0]
                    link(V.tensor_scalar(first, first, r_tf[:, ct:ct + 1], None, ALU.mult))
                    ps = banks.take(("kvr", 1, ct, half), "dve")
                    dve.wait_ge(*banks.filled(("kvr", 1, ct, half)))
                    V.tensor_tensor(r_wv[:, ct, cols], r_w[:, ct, cols], ps, ALU.mult).then_inc(emptied["dve"], 1)
            dve.wait_ge(*banks.emptied(("kvr", 1, KC - 1, 1)))
            for ct in range(KC):
                link(V.tensor_tensor_scan(r_num[:, ct, :], r_decay[:, ct, :], r_wv[:, ct, :], 0.0, ALU.mult, ALU.add))
                link(V.tensor_tensor_scan(r_den[:, ct, :], r_decay[:, ct, :], r_w[:, ct, :], 0.0, ALU.mult, ALU.add))
                link(V.tensor_scalar(r_den[:, ct, :], r_den[:, ct, :], 1e-6, None, ALU.add))
                link(V.reciprocal(r_den[:, ct, :], r_den[:, ct, :]))
                link(V.tensor_tensor(r_num[:, ct, :], r_num[:, ct, :], r_den[:, ct, :], ALU.mult))
                for half in range(2):
                    dve.wait_ge(*banks.emptied(("kvr", 2, ct, half)))
                V.tensor_tensor(r_num[:, ct, :], r_num[:, ct, :], r_sig[:, ct, :], ALU.mult).then_inc(rw_ready, 1)
            for t in range(NT):
                residual(("ro", t), t)
            ended(dve, 0)
            if LAST == 1:
                return

            normalise(1)
            for h in range(0, H, 2):
                copy_out(("w1", h), W1[:, :, h * QW:(h + 1) * QW],
                         lambda ps: ps[:, 0:KC * QW].rearrange("p (k q) -> p k q", k=KC))
            for g in range(8):
                copy_out(("xwo", g), x_woT[:, 2 * g:2 * g + 2, :])
            ht_out(1)
            dve.wait_ge(*banks.emptied(("w1", H - 2)))
            dve.wait_ge(*banks.emptied(("w1", H - 1)))
            link(V.memset(W2[:, :, :, :], 0.0))
            for p in range(PAIRS):
                ps = banks.take(("w2", p), "dve")
                dve.wait_ge(*banks.filled(("w2", p)))
                src = ps.rearrange("p (c w) -> p c w", c=2)
                V.tensor_copy(W2[:, p, :, 0:64], src[:, :, 0:64])
                V.tensor_copy(W2[0:64, p, :, 64:128], src[0:64, :, 64:128])
                V.tensor_copy(W2[64:128, p, :, 128:192], src[64:128, :, 128:192])
                V.tensor_copy(W2[:, p, :, 192:256], src[:, :, 192:256]).then_inc(emptied["dve"], 1)
            ended(dve, 1)
            dve.wait_ge(rope_loaded, 32)

            def rotate(n):
                p, half, s = n // 2, n % 2, n % 2
                for j in range(3):
                    key = ("z", p, half, j)
                    ps = banks.take(key, "dve")
                    dve.wait_ge(*banks.filled(key))
                    if n >= 2:
                        dve.wait_ge(*banks.filled(("q", (n - 2) // 2, n % 2)))
                    V.tensor_tensor(zc[:, s, j, :], ps, cosq[:, j, :], ALU.mult)
                    V.tensor_tensor(zs[:, s, j, :], ps, sinq[:, j, :], ALU.mult).then_inc(emptied["dve"], 1)

            def lows(n):
                p, half, s = n // 2, n % 2, n % 2
                ps = banks.take(("q", p, half), "dve")
                dve.wait_ge(q_high, 2 * (n + 1))
                if n >= 2:
                    dve.wait_ge(q_moved[s], 32 * (n // 2))
                for i in range(2):
                    rows = slice(i * D, (i + 1) * D)
                    hi = QALL[rows, 2 * half:2 * half + 2, p, i, :].bitcast(F32)
                    ins = V.tensor_tensor(qlo[rows, s, :].rearrange("p (b t) -> p b t", b=2),
                                          ps[rows, :].rearrange("p (b t) -> p b t", b=2), hi, ALU.subtract)
                ins.then_inc(emptied["dve"], 1)

            rotate(0)
            for n in range(2 * PAIRS):
                if n + 1 < 2 * PAIRS:
                    rotate(n + 1)
                lows(n)
            ended(dve, 2)
            for b in range(B):
                for g in range(4):
                    ps = banks.take(("kt", b, g), "dve")
                    dve.wait_ge(kh_ready, 4 * b + g + 1)
                    w = min(HALF, L - g * HALF)
                    cols = slice(g * HALF, g * HALF + w)
                    V.tensor_tensor(KL[:, cols], ps[:, 0:w], KH[:, cols].bitcast(F32), ALU.subtract).then_inc(emptied["dve"], 1)

                def scores_out(v, st, hd, first=False):
                    n = 2 * (16 * b + v) + hd
                    for half, (a, z) in enumerate(((0, 1024), (1024, L))):
                        dve.wait_ge(sc_full, 2 * n + half + 1)
                        if half == 0 and not first:
                            dve.wait_ge(t_full, 7 * (16 * b + v - 1))
                        if half == 1:
                            dve.wait_ge(sc_out, 2 * n + 1)
                        V.tensor_scalar(SC[st][hd][:, a:z], PS[:, a:z], -1.0, mx[:, st, hd, 0:1] if half else None,
                                        ALU.mult, ALU.min, accum_out=mx[:, st, hd, half:half + 1]).then_inc(sc_out, 1)

                def invert(v, st, hd):
                    dve.wait_ge(p_exp, 2 * (16 * b + v) + hd + 1)
                    V.reciprocal(ri[:, st, hd:hd + 1], sm[:, st, hd:hd + 1]).then_inc(p_rec, 1)

                def turned(v, g, first=False):
                    dve.wait_ge(t_full, 7 * (16 * b + v) + g + 1)
                    if g == 1 and not (first and b == 0):
                        dve.wait_ge(av_full, 16 * b + v)
                    V.tensor_copy(PT[:, 2 * g:2 * g + 2, :, :],
                                  PS[:, (4 + g % 3) * 512:(5 + g % 3) * 512]).then_inc(t_dve, 1)

                def tile(v, st, prev=True, first=False):
                    scores_out(v, st, 0, first or not prev)
                    if prev:
                        turned(v - 1, 1, first)
                        turned(v - 1, 3)
                    invert(v, st, 0)
                    scores_out(v, st, 1, first or not prev)
                    if prev:
                        turned(v - 1, 5)
                    invert(v, st, 1)

                tile(0, 0, False)
                tile(1, 1, True, True)
                with dve.Fori(1, PAIRS) as j:
                    tile(2 * j, 0)
                    tile(2 * j + 1, 1)
                for g in (1, 3, 5):
                    turned(15, g)
                ended(dve, 3 + b)
            for t in range(NT):
                residual(("xo", t), t)
            ended(dve, 7)
            if LAST == 2:
                return

            def bcast(a, n):
                return a.unsqueeze(2).to_broadcast([P, a.shape[1], n])

            def first_choice(src, E, dst, m):
                link(V.tensor_reduce(f_mx[:, m, :], src, AX, ALU.max))
                link(V.tensor_tensor(f_v[:, :, 0:E], src, bcast(f_mx[:, m, :], E), ALU.is_equal))
                link(V.tensor_tensor(f_v[:, :, 0:E], f_v[:, :, 0:E], f_rev[:, :, 0:E], ALU.mult))
                link(V.tensor_reduce(f_mx[:, 3, :], f_v[:, :, 0:E], AX, ALU.max))
                link(V.tensor_tensor(dst, f_v[:, :, 0:E], bcast(f_mx[:, 3, :], E), ALU.is_equal))

            normalise(2)
            ht_out(2)
            lg = f_l[:, :, 0:E0]
            dve.wait_ge(moe0_loaded, 16 * 5)
            copy_out("logits0", lg, lambda ps: ps[:, 0:NT * E0].rearrange("p (t e) -> p t e", t=NT))
            dve.wait_ge(*banks.emptied("logits0"))
            first_choice(lg, E0, f_oh[:, :, 0:E0], 0)
            V.tensor_tensor(f_b[:, :, 0:E0], lg, bcast(f_mx[:, 0, :], E0), ALU.subtract).then_inc(e_shift, 1)
            link(V.memset(f_pre[:, 0, :], 0.0))
            for t in range(1, NT):
                dve.wait_ge(mask_ready, t - 1) if t > 1 else None
                V.tensor_tensor(f_pre[:, t, 0:E0], f_pre[:, t - 1, 0:E0], f_oh[:, t - 1, 0:E0], ALU.add).then_inc(mask_ready, 1)
            dve.wait_ge(e_exp, 1)
            link(V.tensor_reduce(f_mx[:, 1, :], f_e[:, :, 0:E0], AX, ALU.add))
            link(V.reciprocal(f_mx[:, 2, :], f_mx[:, 1, :]))
            ps = banks.take("rank0", "dve")
            dve.wait_ge(*banks.filled("rank0"))
            V.scalar_tensor_tensor(f_comb[:, :, 0:E0], ps[:, 0:NT * E0].rearrange("p (t e) -> p t e", t=NT), float(CAP0),
                                   f_oh[:, :, 0:E0], ALU.is_lt, ALU.mult).then_inc(emptied["dve"], 1)
            dve.wait_ge(*banks.emptied("rank0"))
            link(V.tensor_tensor(f_comb[:, :, 0:E0], f_comb[:, :, 0:E0], bcast(f_mx[:, 2, :], E0), ALU.mult))

            def weigh(key, n, e):
                ps = banks.take(key, "dve")
                dve.wait_ge(*banks.filled(key))
                if n >= 2:
                    dve.wait_ge(*banks.emptied((key[0], n - 2, key[2])))
                for tt in range(2):
                    t = 4 * (n % 2) + 2 * key[2] + tt
                    ins = V.scalar_tensor_tensor(X[:, t, :], ps[:, tt * C:(tt + 1) * C], f_comb[:, t, e:e + 1], X[:, t, :],
                                                 ALU.mult, ALU.add)
                ins.then_inc(emptied["dve"], 1)

            for n in range(2 * E0):
                for i in range(2):
                    weigh(("d0", n, i), n, n // 2)
            ended(dve, 8)
            if LAST == 3:
                return

            normalise(3)
            ht_out(3)
            for kc in range(KC):
                for g in range(6):
                    dve.wait_ge(*banks.emptied(("awT", kc, g)))
            qk = a_wT[:, :, 0:20 * P].rearrange("p k (h d) -> p k h d", d=P)
            link(V.tensor_reduce(a_mu[:, :, :], qk, AX, ALU.add))
            link(V.tensor_scalar(a_mu[:, :, :], a_mu[:, :, :], 1.0 / P, None, ALU.mult))
            for kc in range(KC):
                link(V.tensor_tensor(qk[:, kc], qk[:, kc], bcast(a_mu[:, kc, :], P), ALU.subtract))
            dve.wait_ge(gqa_bcast, 16 * 6)
            for i in range(2):
                gain, bias = a_gb[:, 2 * i, :], a_gb[:, 2 * i + 1, :]
                for s in range(2):
                    link(V.tensor_tensor(a_gc[:, i, s, :], a_cos[:, s, :], gain, ALU.mult))
                    link(V.tensor_tensor(a_gs[:, i, s, 0:64], a_sin[:, s, 0:64], gain[:, 64:128], ALU.mult))
                    link(V.tensor_tensor(a_gs[:, i, s, 64:128], a_sin[:, s, 64:128], gain[:, 0:64], ALU.mult))
                    link(V.tensor_tensor(a_bt[:, i, s, :], a_cos[:, s, :], bias, ALU.mult))
                    link(V.tensor_tensor(a_tmp[:, s, 0:64], a_sin[:, s, 0:64], bias[:, 64:128], ALU.mult))
                    link(V.tensor_tensor(a_tmp[:, s, 64:128], a_sin[:, s, 64:128], bias[:, 0:64], ALU.mult))
                    link(V.tensor_tensor(a_bt[:, i, s, :], a_bt[:, i, s, :], a_tmp[:, s, :], ALU.add))
            ended(dve, 9)

            def table(a):
                return a.unsqueeze(1).to_broadcast([P, 4, a.shape[1]])

            def heads(n, m):
                return m[:, n % 2, :].rearrange("p (h d) -> p h d", h=4)

            def parts(n):
                i, s = n % 5 // 4, n // 5 % 2
                key = ("qkv", n // 5, n % 5)
                ps = banks.take(key, "dve")
                dve.wait_ge(*banks.filled(key))
                dve.wait_ge(sq_ready, n + 1)
                src, m1, m2 = ps.rearrange("p (h d) -> p h d", h=4), heads(n, a_m1), heads(n, a_m2)
                if n >= 2:
                    dve.wait_ge(*banks.filled(("qkT", n - 2)))
                V.tensor_tensor(m1, src, table(a_gc[:, i, s, :]), ALU.mult)
                V.tensor_tensor(m2[:, :, 0:64], src[:, :, 64:128], table(a_gs[:, i, s, 0:64]), ALU.mult)
                V.tensor_tensor(m2[:, :, 64:128], src[:, :, 0:64], table(a_gs[:, i, s, 64:128]), ALU.mult).then_inc(m_part, 1)
                V.tensor_reduce(a_ss[:, n % 2, :], a_sq[:, n % 2, :].rearrange("p (h d) -> p h d", h=4), AX,
                                ALU.add).then_inc(emptied["dve"], 1)
                dve.wait_ge(*banks.emptied(key))
                V.tensor_scalar(a_ss[:, n % 2, :], a_ss[:, n % 2, :], 1.0 / P, LN_EPS, ALU.mult, ALU.add).then_inc(hvar_ready, 1)

            def whole(n):
                i, s = n % 5 // 4, n // 5 % 2
                m1 = heads(n, a_m1)
                dve.wait_ge(hstd_ready, n + 1)
                link(V.reciprocal(a_ss[:, n % 2, :], a_ss[:, n % 2, :]))
                dve.wait_ge(m_sum, n + 1)
                link(V.tensor_tensor(m1, m1, bcast(a_ss[:, n % 2, :], P), ALU.mult))
                V.tensor_tensor(m1, m1, table(a_bt[:, i, s, :]), ALU.add).then_inc(qk_ready, 1)

            for n in range(5 * NT + 1):
                if n < 5 * NT:
                    parts(n)
                if n >= 1:
                    whole(n - 1)
            ended(dve, 10)

            def softmax_units(tag, units, base_n, scale, after):
                for n in range(len(units) + 1):
                    if n < len(units):
                        st = units[n][-1]
                        nk = P * (st + 1)
                        sc = s_sc[:, n % 2, :, 0:nk]
                        for i in range(st + 1):
                            key = (tag, "s", n, i)
                            ps = banks.take(key, "dve")
                            dve.wait_ge(*banks.filled(key))
                            if n >= 2:
                                dve.wait_ge(*banks.filled((tag, "pt", n - 2, units[n - 2][-1])))
                            hs = 4 // (st + 1)
                            V.scalar_tensor_tensor(sc[:, i * hs:(i + 1) * hs, :], ps.rearrange("p (h k) -> p h k", h=hs),
                                                   scale, (s_mask1 if st else s_mask0)[:, :].rearrange("p (h k) -> p h k", h=hs),
                                                   ALU.mult, ALU.add).then_inc(emptied["dve"], 1)
                            dve.wait_ge(*banks.emptied(key))
                        link(V.tensor_reduce(s_mx[:, n % 2, :], sc, AX, ALU.max))
                        V.tensor_tensor(sc, sc, bcast(s_mx[:, n % 2, :], nk), ALU.subtract).then_inc(sh_ready, 1)
                        dve.wait_ge(se_ready, base_n + n + 1)
                        link(V.tensor_reduce(s_sm[:, n % 2, :], sc, AX, ALU.add))
                        V.reciprocal(s_ri[:, n % 2, :], s_sm[:, n % 2, :]).then_inc(si_ready, 1)
                    if n >= 1:
                        after(n - 1, units[n - 1])

            def a_after(n, unit):
                b, g, st = unit
                copy_out(("a", "o", n), QKT[:, 4 * g:4 * g + 4, (2 * b + st) * P:(2 * b + st + 1) * P])

            dve.wait_ge(masks_loaded, 32)
            softmax_units("a", A_UNITS, 0, float(P) ** -0.5, a_after)
            for t in range(NT):
                residual(("ao", t), t)
            ended(dve, 11)
            if LAST == 4:
                return

            normalise(4)
            ht_out(4)
            dve.wait_ge(lat_loaded, 16 * (4 + B))
            for ct in range(KC):
                for g in range(2):
                    key = ("yk", ct, g)
                    ps = banks.take(key, "dve")
                    dve.wait_ge(*banks.filled(key))
                    for h in range(8):
                        ins = V.tensor_scalar(y_km[:, 2 * g:2 * g + 2, ct, h, :], ps.rearrange("p (b t) -> p b t", b=2),
                                              y_hm[:, h:h + 1], None, ALU.mult)
                    ins.then_inc(emptied["dve"], 1)

            def y_after(n, unit):
                b, ct, hg, st = unit
                dst = y_ax[:, ct, (2 * b + st) * P:(2 * b + st + 1) * P]
                key = ("y", "o", n)
                ps = banks.take(key, "dve")
                dve.wait_ge(*banks.filled(key))
                if hg == 0:
                    V.tensor_copy(dst, ps[:, 0:P]).then_inc(emptied["dve"], 1)
                else:
                    V.tensor_tensor(dst, dst, ps[:, 0:P], ALU.add).then_inc(emptied["dve"], 1)

            softmax_units("y", Y_UNITS, len(A_UNITS), 0.25, y_after)
            for t in range(NT):
                residual(("yo", t), t)
            ended(dve, 12)
            if LAST == 5:
                return

            normalise(5)
            ht_out(5)
            dve.wait_ge(moe1_loaded, 16 * 11)
            copy_out("logits1", f_l[:, :, :], lambda ps: ps[:, 0:NT * E1].rearrange("p (t e) -> p t e", t=NT))
            dve.wait_ge(*banks.emptied("logits1"))
            link(V.tensor_reduce(f_mx[:, 0, :], f_l[:, :, :], AX, ALU.max))
            V.tensor_tensor(f_e[:, :, :], f_l[:, :, :], bcast(f_mx[:, 0, :], E1), ALU.subtract).then_inc(e_shift, 1)
            link(V.tensor_tensor(f_b[:, :, :], f_l[:, :, :], m_rb[:, :].unsqueeze(1).to_broadcast([P, NT, E1]), ALU.add))
            first_choice(f_b[:, :, :], E1, f_oh[:, :, :], 1)
            link(V.scalar_tensor_tensor(f_b[:, :, :], f_oh[:, :, :], NEG, f_b[:, :, :], ALU.mult, ALU.add))
            first_choice(f_b[:, :, :], E1, f_oh2[:, :, :], 1)
            link(V.tensor_tensor(f_oh[:, :, :], f_oh[:, :, :], f_oh2[:, :, :], ALU.add))
            dve.wait_ge(e_exp, 2)
            link(V.tensor_tensor(f_v[:, :, :], f_oh[:, :, :], f_e[:, :, :], ALU.mult))
            link(V.tensor_reduce(f_mx[:, 1, :], f_v[:, :, :], AX, ALU.add))
            link(V.reciprocal(f_mx[:, 2, :], f_mx[:, 1, :]))
            link(V.memset(f_comb[:, :, E1:E1X], 1.0))
            link(V.tensor_tensor(f_comb[:, :, 0:E1], f_v[:, :, :], bcast(f_mx[:, 2, :], E1), ALU.mult))
            for n in range(2 * E1X + 1):
                if n < 2 * E1X:
                    key = ("g1", n)
                    ps = banks.take(key, "dve")
                    dve.wait_ge(*banks.filled(key))
                    dve.wait_ge(*banks.emptied(("u1", n)))
                    if n >= 2:
                        dve.wait_ge(*banks.filled(("d1", n - 2, 1)))
                    V.tensor_tensor(m_h[:, n % 2, :], m_su[:, n % 2, :], ps, ALU.mult).then_inc(emptied["dve"], 1)
                if n >= 1:
                    for i in range(2):
                        weigh(("d1", n - 1, i), n - 1, (n - 1) // 2)
            ended(dve, 13)

        @block.gpsimd
        def _(pool):
            G = nc.gpsimd
            steps = [0]

            def link(ins):
                steps[0] += 1
                ins.then_inc(pool_step, 1)
                pool.wait_ge(pool_step, steps[0])

            link(G.memset(r_ones[:, :], 1.0))
            G.memset(ones[:, :], 1.0).then_inc(ones_set, 1)
            G.memset(KVR[:, :, LT - 1, :], 0.0).then_inc(kv_cleared, 1)
            pool.wait_ge(kv_loaded, 16 * (2 * B + 2))
            for b in range(B):
                r, half = KVR[:, b, :, :], D // 2
                G.tensor_tensor(kt1[:, :, :], r, cosk[:, :, :], ALU.mult)
                G.tensor_tensor(kt2[:, :, 0:half], r[:, :, half:D], sink[:, :, 0:half], ALU.mult)
                link(G.tensor_tensor(kt2[:, :, half:D], r[:, :, 0:half], sink[:, :, half:D], ALU.mult))
                link(G.tensor_tensor(r, kt1[:, :, :], kt2[:, :, :], ALU.add))
            ended(pool, 0)
            if LAST == 1:
                return

            pool.wait_ge(*banks.emptied(("wqr", 5)))
            src = WqrT[:, :].rearrange("r (h s i) -> r h s i", h=H, s=2)
            dst = WqrS[:, :].rearrange("r (h s i) -> r h s i", h=H, s=2)
            G.tensor_copy(dst[:, :, 0, :], src[:, :, 1, :]).then_inc(wqr_shift, 1)
            G.tensor_copy(dst[:, :, 1, :], src[:, :, 0, :]).then_inc(wqr_shift, 1)
            ended(pool, 1)
            ended(pool, 2)
            for k in (KH, KL):
                link(G.memset(k[:, L:L + 1].bitcast(F32), 0.0))
            for b in range(B):
                for s in range(2):
                    G.tensor_copy(DUP[:, :, s * D:(s + 1) * D], KVR[:, b, :, :]).then_inc(dup_ready, 1)

                def query(j, v, st, first=False):
                    if not first:
                        pool.wait_ge(sc_full, 4 * (16 * b + v - 1))
                    G.tensor_copy(QC[st][:, :, :], QALL[:, b, j, :, st * P:(st + 1) * P]).then_inc(qc_ready, 1)

                def norm(v, st):
                    for hd in range(2):
                        pool.wait_ge(p_rec, 2 * (16 * b + v) + hd + 1)
                        G.tensor_tensor(pool_tick[:, 2 * st + hd:2 * st + hd + 1], ones[:, 0:1], ones[:, 0:1], ALU.mult)
                        G.tensor_scalar(SC[st][hd][:, :], SC[st][hd][:, :], ri[:, st, hd:hd + 1], 1.0,
                                        ALU.mult, ALU.mult).then_inc(p_norm, 1)

                pool.wait_ge(q_moved[0], 32 * PAIRS)
                pool.wait_ge(q_moved[1], 32 * PAIRS)
                query(0, 0, 0, True)
                query(0, 1, 1, True)
                with pool.Fori(0, PAIRS - 1) as j:
                    norm(2 * j, 0)
                    query(bass.ds(j + 1, 1), 2 * j + 2, 0)
                    norm(2 * j + 1, 1)
                    query(bass.ds(j + 1, 1), 2 * j + 3, 1)
                norm(14, 0)
                norm(15, 1)
                ended(pool, 3 + b)
            ended(pool, 7)
            if LAST == 2:
                return
            ended(pool, 8)
            if LAST == 3:
                return
            ended(pool, 9)
            for n in range(5 * NT):
                pool.wait_ge(m_part, n + 1)
                G.tensor_tensor(a_m1[:, n % 2, :], a_m1[:, n % 2, :], a_m2[:, n % 2, :], ALU.add).then_inc(m_sum, 1)
            ended(pool, 10)

            def softmax_units(units, base_n):
                for n, unit in enumerate(units):
                    nk = P * (unit[-1] + 1)
                    sc = s_sc[:, n % 2, :, 0:nk]
                    pool.wait_ge(si_ready, base_n + n + 1)
                    G.tensor_tensor(sc, sc, s_ri[:, n % 2, :].unsqueeze(2).to_broadcast([P, 4, nk]),
                                    ALU.mult).then_inc(sn_ready, 1)

            softmax_units(A_UNITS, 0)
            ended(pool, 11)
            if LAST == 4:
                return

            link(G.memset(y_vm[:, :, :, :], 0.0))
            vm = y_vm[:, :, :, :].rearrange("p b k (h r) -> p b k h r", r=P + 16)
            for ct in range(KC):
                for b in range(B):
                    if ct == 0:
                        pool.wait_ge(*banks.emptied(("yv", b)))
                    else:
                        last = 4 * b + 3
                        pool.wait_ge(*banks.filled(("y", "o", last)))
                    for kb in range(2):
                        G.tensor_copy(vm[:, b, kb, :, 0:16],
                                      y_v[:, b, kb, ct * P:(ct + 1) * P].rearrange("p (h d) -> p h d", d=16)).then_inc(vm_ready, 1)
                    units_n = slice(16 * ct + 4 * b, 16 * ct + 4 * b + 4)
                    for n in range(units_n.start, units_n.stop):
                        nk = P * (Y_UNITS[n][-1] + 1)
                        sc = s_sc[:, n % 2, :, 0:nk]
                        pool.wait_ge(si_ready, len(A_UNITS) + n + 1)
                        G.tensor_tensor(sc, sc, s_ri[:, n % 2, :].unsqueeze(2).to_broadcast([P, 4, nk]),
                                        ALU.mult).then_inc(sn_ready, 1)
            ended(pool, 12)
            if LAST == 5:
                return
            ended(pool, 13)

        @block.sync
        def _(sp):
            xv = x.rearrange("b (t p) c -> (b t) p c", p=P)
            ov = out.rearrange("b (t p) c -> (b t) p c", p=P)
            sp.dma_start(ident[:, :], ident_c).then_inc(consts_loaded, 16)
            for t in range(NT):
                sp.dma_start(X[:, t, :], xv[t]).then_inc(x_loaded, 16)
            for w, a in enumerate((L0_attn_Wk, L0_attn_Wv, L0_attn_Wr, L0_attn_Wo)):
                sp.dma_start(r_nat[:, w, :, :], a.rearrange("(o p) i -> p o i", p=P)).then_inc(rwkv_loaded, 16)
            for dst, a in ((r_td, L0_attn_time_decay), (r_tf, L0_attn_time_first)):
                sp.dma_start(dst[:, :], a.rearrange("(k h) s -> (h s) k", k=KC)).then_inc(rwkv_loaded, 16)
            sp.dma_start(cosk[:, :, :], cosk_c).then_inc(kv_loaded, 16)
            sp.dma_start(sink[:, :, :], sink_c).then_inc(kv_loaded, 16)
            sp.wait_ge(kv_cleared, 1)
            for b in range(B):
                whole = (LT - 1) * P
                sp.dma_start(KVR[:, b, 0:LT - 1, :], ctx_512[b, 0:whole, :].rearrange("(t p) d -> p t d", p=P)).then_inc(kv_loaded, 16)
                sp.dma_start(KVR[0:LREST, b, LT - 1, :], ctx_512[b, whole:L, :]).then_inc(kv_loaded, 16)

            def finish(n):
                sp.wait_ge(phase_ended, 4 * (n + 1))
                for t in range(NT):
                    sp.dma_start(ov[t], X[:, t, :]).then_inc(stored, 16)
                sp.wait_ge(stored, 16 * NT)

            if LAST == 1:
                return finish(0)
            sp.wait_ge(phase_ended, 4)
            sp.dma_start(x_wq[:, :, :], L0_xattn_Wq.rearrange("(h k) c -> k h c", k=P)).then_inc(xattn_loaded, 16)
            sp.dma_start(x_kcq[:, :, :], L0_xattn_w_kc_q.rearrange("h k q -> k h q")).then_inc(xattn_loaded, 16)
            sp.dma_start(x_wqr[:, :, :], L0_xattn_W_qr.rearrange("h q r -> (h q) r").rearrange("(t p) r -> p t r", p=P)).then_inc(xattn_loaded, 16)
            sp.dma_start(x_wkr[:, :, :], L0_xattn_W_kr.rearrange("h d r -> (h d) r").rearrange("(t p) r -> p t r", p=P)).then_inc(xattn_loaded, 16)
            sp.dma_start(x_wo[:, :, :], L0_xattn_Wo.rearrange("(o p) k -> p o k", p=P)).then_inc(xattn_loaded, 16)
            sp.dma_start(x_kckv[:, :, :], L0_xattn_w_kc_kv.rearrange("h k d -> k h d")).then_inc(xattn_loaded, 16)
            sp.wait_ge(phase_ended, 8)
            sp.dma_start(cosq[:, :, :], cosq_c).then_inc(rope_loaded, 16)
            sp.dma_start(sinq[:, :, :], sinq_c).then_inc(rope_loaded, 16)
            for n in range(2 * PAIRS):
                p, half, s = n // 2, n % 2, n % 2
                sp.wait_ge(*banks.emptied(("q", p, half)))
                for i in range(2):
                    o = slice((1 - i) * D, (2 - i) * D)
                    sp.dma_start(QALL[o, 2 * half:2 * half + 2, p, i, :].bitcast(F32),
                                 qlo[i * D:(i + 1) * D, s, :].bitcast(F32).rearrange("p (b t) -> p b t", b=2)).then_inc(q_moved[s], 16)
            if LAST == 2:
                return finish(7)
            sp.wait_ge(phase_ended, 4 * 7)
            sp.dma_start(g_nat[:, :], L0_ffn_gate_weight).then_inc(moe0_loaded, 16)
            sp.dma_start(f_rev[:, :, :], rev_c).then_inc(moe0_loaded, 16)
            sp.dma_start(f_tri[:, :], tri_c).then_inc(moe0_loaded, 16)
            sp.dma_start(f_w1[:, :, :, :], L0_ffn_w1.rearrange("e (k p) i -> p e k i", p=P)).then_inc(moe0_loaded, 16)
            sp.dma_start(f_w2[:, :, :, :], L0_ffn_w2.rearrange("e (k p) i -> p e k i", p=P)).then_inc(moe0_loaded, 16)
            if LAST == 3:
                return finish(8)
            sp.dma_start(a_nat[:, :, :], L1_attn_w_qkv.rearrange("(o p) c -> p o c", p=P)).then_inc(gqa_loaded, 16)
            sp.dma_start(a_wo[:, :, :], L1_attn_w_o.rearrange("(o p) k -> p o k", p=P)).then_inc(gqa_loaded, 16)
            sp.wait_ge(phase_ended, 4 * 9)
            sp.dma_start(a_cos[:, :, :], cos1_c).then_inc(gqa_bcast, 16)
            sp.dma_start(a_sin[:, :, :], sin1_c).then_inc(gqa_bcast, 16)
            for i, a in enumerate((L1_attn_qn_g, L1_attn_qn_b, L1_attn_kn_g, L1_attn_kn_b)):
                sp.dma_start(a_gb[:, i, :], a.partition_broadcast(P)).then_inc(gqa_bcast, 16)
            sp.wait_ge(phase_ended, 4 * 11)
            sp.dma_start(s_mask0[:, :], mask0_c).then_inc(masks_loaded, 16)
            sp.dma_start(s_mask1[:, :], mask1_c).then_inc(masks_loaded, 16)
            if LAST == 4:
                return finish(11)
            sp.wait_ge(phase_ended, 4 * 12)
            sp.dma_start(y_wq[:, :, :], L1_xattn_Wq.rearrange("(o p) i -> p o i", p=P)).then_inc(lat_loaded, 16)
            sp.dma_start(y_wo[:, :, :], L1_xattn_Wout.rearrange("(o p) i -> p o i", p=P)).then_inc(lat_loaded, 16)
            sp.dma_start(y_wkv[:, :, :], L1_xattn_Wkv_expand.rearrange("(o p) i -> p o i", p=P)).then_inc(lat_loaded, 16)
            for b in range(B):
                sp.dma_start(y_lat[:, 2 * b:2 * b + 2, :], ctx_512[b, 0:T, :].rearrange("(t p) d -> p t d", p=P)).then_inc(lat_loaded, 16)
            sp.dma_start(y_hm[:, :], hmask_c).then_inc(lat_loaded, 16)
            if LAST == 5:
                return finish(12)
            sp.wait_ge(phase_ended, 4 * 13)
            sp.dma_start(m_wu[:, 0:E1, :, :], L1_ffn_Wu.rearrange("e (k p) i -> p e k i", p=P)).then_inc(moe1_loaded, 16)
            sp.dma_start(m_wg[:, 0:E1, :, :], L1_ffn_Wg.rearrange("e (k p) i -> p e k i", p=P)).then_inc(moe1_loaded, 16)
            sp.dma_start(m_wd[:, 0:E1, :], L1_ffn_Wd.rearrange("e i c -> i e c")).then_inc(moe1_loaded, 16)
            for it in range(2):
                sp.dma_start(m_wu[:, E1 + it, :, :], L1_ffn_Su[0, :, it * P:(it + 1) * P].rearrange("(k p) i -> p k i", p=P)).then_inc(moe1_loaded, 16)
                sp.dma_start(m_wg[:, E1 + it, :, :], L1_ffn_Sg[0, :, it * P:(it + 1) * P].rearrange("(k p) i -> p k i", p=P)).then_inc(moe1_loaded, 16)
            sp.dma_start(m_wd[:, E1:E1X, :], L1_ffn_Sd[0].rearrange("(s i) c -> i s c", i=P)).then_inc(moe1_loaded, 16)
            sp.dma_start(m_rw[:, :], L1_ffn_router_w).then_inc(moe1_loaded, 16)
            sp.dma_start(m_rb[:, :], L1_ffn_router_bias.partition_broadcast(P)).then_inc(moe1_loaded, 16)
            sp.dma_start(f_rev[:, :, :], rev_c).then_inc(moe1_loaded, 16)
            finish(13)


def shape_constants():
    f = np.float32

    def angles(n, dim, base):
        inv = f(1.0) / np.power(f(base), np.arange(0, dim, 2, dtype=f) / f(dim), dtype=f)
        return np.arange(n, dtype=f)[:, None] * inv[None, :]

    c = {"ident_c": np.eye(P, dtype=f)}
    a = np.repeat(angles(T, QW, 10000.0), 2, axis=-1)
    cos, sin = np.cos(a), np.sin(a)
    half = QW // 2
    other = np.concatenate([sin[:, half:], -sin[:, :half]], axis=-1)
    pair = lambda t: np.tile(np.concatenate([t, t], -1).T.reshape(3, P, T).transpose(1, 0, 2), (1, 1, 2))
    c["cosq_c"], c["sinq_c"] = pair(cos), pair(other)
    a = np.zeros((LT * P, D), f)
    a[:L] = np.repeat(angles(L, D, 10000.0), 2, axis=-1)
    sign = np.concatenate([-np.ones(D // 2, f), np.ones(D // 2, f)])
    rows = lambda t: t.reshape(LT, P, D).transpose(1, 0, 2)
    c["cosk_c"], c["sink_c"] = rows(np.cos(a)), rows(np.sin(a) * sign)
    rev = np.arange(E1, 0, -1, dtype=f)
    c["rev_c"] = np.broadcast_to(rev, (P, NT, E1))
    c["tri_c"] = np.triu(np.ones((P, P), f), 1)
    a = angles(T, P, 1000000.0)
    rows = lambda t: np.concatenate([t, t], -1).reshape(2, P, P).transpose(1, 0, 2)
    sign = np.concatenate([-np.ones(P // 2, f), np.ones(P // 2, f)])
    c["cos1_c"], c["sin1_c"] = rows(np.cos(a)), rows(np.sin(a)) * sign
    tri = np.where(np.arange(P)[None, :] > np.arange(P)[:, None], f(NEG), f(0.0))
    c["mask0_c"] = np.tile(tri, (1, 4))
    c["mask1_c"] = np.tile(np.concatenate([np.zeros((P, P), f), tri], 1), (1, 2))
    c["hmask_c"] = (np.arange(P)[:, None] // 16 == np.arange(8)[None, :]).astype(f)
    return {k: np.ascontiguousarray(v, dtype=f) for k, v in c.items()}


_INS = ['x', 'ctx_512', 'L0_attn_Wk', 'L0_attn_Wv', 'L0_attn_Wr', 'L0_attn_Wo', 'L0_attn_time_decay', 'L0_attn_time_first',
        'L0_xattn_Wq', 'L0_xattn_w_kc_q', 'L0_xattn_w_kc_kv', 'L0_xattn_W_qr', 'L0_xattn_W_kr', 'L0_xattn_Wo',
        'L0_ffn_gate_weight', 'L0_ffn_w1', 'L0_ffn_w2', 'L1_attn_w_qkv', 'L1_attn_w_o', 'L1_attn_qn_g', 'L1_attn_qn_b',
        'L1_attn_kn_g', 'L1_attn_kn_b', 'L1_xattn_Wq', 'L1_xattn_Wkv_expand', 'L1_xattn_Wout', 'L1_ffn_router_w',
        'L1_ffn_router_bias', 'L1_ffn_Wu', 'L1_ffn_Wg', 'L1_ffn_Wd', 'L1_ffn_Su', 'L1_ffn_Sg', 'L1_ffn_Sd']
_CONSTS = ['ident_c', 'cosq_c', 'sinq_c', 'cosk_c', 'sink_c', 'rev_c', 'tri_c', 'cos1_c', 'sin1_c', 'mask0_c', 'mask1_c', 'hmask_c']
_OUTS = [((4, 256, 256), 'float32')]


def kernel(**inputs):
    import numpy as _np
    import concourse.bacc as _bacc
    from concourse import mybir as _mybir
    from concourse.bass_utils import run_bass_kernel_spmd as _run

    nc = _bacc.Bacc("TRN2", target_bir_lowering=False, num_devices=1)
    arrays, args = {}, []
    consts = shape_constants()
    for name in _INS + _CONSTS:
        a = _np.ascontiguousarray(inputs[name] if name in inputs else consts[name])
        arrays[f"in_{name}_dram"] = a
        args.append(nc.dram_tensor(f"in_{name}_dram", a.shape, _mybir.dt.from_np(a.dtype), kind="ExternalInput").ap())
    for i, (shape, dtype) in enumerate(_OUTS):
        dt = _mybir.dt.from_np(_np.dtype(dtype))
        args.append(nc.dram_tensor(f"out_{i}_dram", shape, dt, kind="ExternalOutput").ap())
    decoder(nc, *args)
    r = _run(nc, [arrays], core_ids=[0])
    got = tuple(r.results[0][f"out_{i}_dram"] for i in range(len(_OUTS)))
    return got[0]
```

```python
from contextlib import ExitStack

import numpy as np

import concourse.bass as bass
from concourse import mybir

P = 128
F32 = mybir.dt.float32
F32R = mybir.dt.float32r
BF16 = mybir.dt.bfloat16
ALU = mybir.AluOpType
ACT = mybir.ActivationFunctionType
AX = mybir.AxisListType.X
LN_EPS = 1e-5
LAST = 6

B, T, C = 4, 256, 256
NT = B * T // P
KC = C // P
HALF = 512
L = 1601
LT = (L + P - 1) // P
LREST = L - (LT - 1) * P
D = 64
H = 16
PAIRS = H // 2
QW = 192
E0, E1 = 8, 16
CAP0 = 160
E1X = E1 + 2
HKV = 4
NEG = -1e30


class PsumBanks:

    def __init__(self, psum, filled, emptied):
        self.psum, self.filled_sem, self.emptied_sem = psum, filled, emptied
        self.jobs, self.order, self.count = {}, [], {e: 0 for e in emptied}
        self.taken = {e: 0 for e in emptied}

    def claim(self, key, by):
        assert key not in self.jobs, key
        self.count[by] += 1
        self.jobs[key] = (len(self.order), by, self.count[by])
        self.order.append(key)
        return self.bank(key)

    def bank(self, key):
        n = self.jobs[key][0] % 8
        return self.psum[:, n * 512:(n + 1) * 512]

    def earlier(self, key):
        n = self.jobs[key][0]
        return self.order[n - 8] if n >= 8 else None

    def filled(self, key):
        return self.filled_sem, self.jobs[key][0] + 1

    def emptied(self, key):
        _, by, n = self.jobs[key]
        return self.emptied_sem[by], n

    def take(self, key, by):
        self.taken[by] += 1
        assert self.jobs[key][1:] == (by, self.taken[by]), (key, self.jobs[key], self.taken)
        return self.bank(key)


def decoder(nc, x, ctx_512, L0_attn_Wk, L0_attn_Wv, L0_attn_Wr, L0_attn_Wo, L0_attn_time_decay, L0_attn_time_first,
            L0_xattn_Wq, L0_xattn_w_kc_q, L0_xattn_w_kc_kv, L0_xattn_W_qr, L0_xattn_W_kr, L0_xattn_Wo,
            L0_ffn_gate_weight, L0_ffn_w1, L0_ffn_w2, L1_attn_w_qkv, L1_attn_w_o, L1_attn_qn_g, L1_attn_qn_b,
            L1_attn_kn_g, L1_attn_kn_b, L1_xattn_Wq, L1_xattn_Wkv_expand, L1_xattn_Wout, L1_ffn_router_w,
            L1_ffn_router_bias, L1_ffn_Wu, L1_ffn_Wg, L1_ffn_Wd, L1_ffn_Su, L1_ffn_Sg, L1_ffn_Sd,
            ident_c, cosq_c, sinq_c, cosk_c, sink_c, rev_c, tri_c, cos1_c, sin1_c, mask_c, hmask_c, out):
    with ExitStack() as ctx:
        base = [nc.sbuf_base]

        def sb(name, shape, dt=F32):
            return ctx.enter_context(nc.sbuf_tensor(name, shape, dt))

        def sem(name):
            return ctx.enter_context(nc.semaphore(name))

        X = sb("X", [P, NT, C])
        ident = sb("ident", [P, P])
        stats = sb("stats", [P, NT, 6])
        mv = sb("mv", [P, NT, 2])
        rstd = sb("rstd", [P, NT])
        ones = sb("ones", [P, P])
        pool_tick = sb("pool_tick", [P, 8])
        arena = nc.sbuf_base
        room = nc.sbuf_usable_end - arena

        def at(name, offset, shape, dt=F32):
            size = int(np.prod(shape[1:])) * 4
            assert offset + size <= room, (name, offset + size, room)
            return nc.alloc_sbuf_tensor_at(name, shape, dt, offset=arena + offset)

        HN = at("HN", 168192, [P, NT, C])
        HT = at("HT", 176384, [P, KC, NT * P])
        PS = ctx.enter_context(nc.psum_tensor("PS", [P, 8 * 512], F32))

        r_nat = at("r_nat", 112672, [P, 4, KC, C])
        r_wt = at("r_wt", 120864, [P, 4, KC, C])
        r_w = at("r_w", 0, [P, KC, B * T])
        r_wv = at("r_wv", 8192, [P, KC, B * T])
        r_sig = at("r_sig", 16384, [P, KC, B * T])
        r_num = at("r_num", 24576, [P, KC, B * T])
        r_den = at("r_den", 32768, [P, KC, B * T])
        r_decay = at("r_decay", 40960, [P, KC, B * T])
        r_ones = at("r_ones", 49152, [P, B * T])
        r_td = at("r_td", 53248, [P, KC])
        r_tf = at("r_tf", 53280, [P, KC])
        r_dec = at("r_dec", 53312, [P, KC])

        KVR = at("KVR", 91168, [P, B, LT, D])
        U = at("U", 184576, [P, PAIRS, C])
        cosk = at("cosk", 192768, [P, LT, D])
        sink = at("sink", 196096, [P, LT, D])
        DUP = at("DUP", 192768, [P, LT, 2 * D])
        kt1 = at("kt1", 138304, [P, LT, D])
        kt2 = at("kt2", 141632, [P, LT, D])
        x_wq = at("x_wq", 112672, [P, H, C])
        x_kcq = at("x_kcq", 129056, [P, H, QW])
        x_wqr = at("x_wqr", 141344, [P, 24, D])
        x_wkr = at("x_wkr", 147488, [P, 8, D])
        x_wo = at("x_wo", 149536, [P, KC, H * P])
        x_kckv = at("x_kckv", 192768, [P, H, D])
        WqrT = at("WqrT", 0, [D, H * QW])
        WqrS = at("WqrS", 12288, [D, H * QW])
        WkrT = at("WkrT", 24576, [D, H * D])
        x_woT = at("x_woT", 28672, [P, H, C])
        W1 = at("W1", 65536, [P, KC, H * QW])
        W2 = at("W2", 112672, [P, PAIRS, 2, 256])
        cosq = at("cosq", 129056, [P, 3, HALF])
        sinq = at("sinq", 135200, [P, 3, HALF])
        zc = at("zc", 141344, [P, 2, 3, HALF])
        zs = at("zs", 153632, [P, 2, 3, HALF])
        qlo = at("qlo", 165920, [P, 2, HALF], F32R)
        QALL = at("QALL", 0, [P, B, PAIRS, 2, T], F32R)
        KH = at("KH", 65536, [P, L + 1], F32R)
        KL = at("KL", 71968, [P, L + 1], F32R)
        SC = [[at(f"S{s}{h}", 112672 + 6432 * (2 * s + h), [P, L]) for h in range(2)] for s in range(2)]
        PT = at("PT", 138432, [P, 2, LT, P])
        CTX = at("CTX", 151744, [P, PAIRS, B * T])
        QC = [at(f"QC{s}", 78400 + 1024 * s, [P, 2, P], F32R) for s in range(2)]
        mx = at("mx", 80448, [P, 2, 2, 2])
        sm = at("sm", 80512, [P, 2, 2])
        ri = at("ri", 80544, [P, 2, 2])

        g_nat = at("g_nat", 34816, [E0, C])
        g_T = at("g_T", 35840, [P, KC, E0])
        f_w1 = at("f_w1", 0, [P, E0, KC, C])
        f_w2 = at("f_w2", 16384, [P, E0, KC, C])
        f_rev = at("f_rev", 36352, [P, NT, E1])
        f_tri = at("f_tri", 37376, [P, P])
        f_l = at("f_l", 38400, [P, NT, E1])
        f_e = at("f_e", 39424, [P, NT, E1])
        f_b = at("f_b", 40448, [P, NT, E1])
        f_v = at("f_v", 41472, [P, NT, E1])
        f_oh = at("f_oh", 42496, [P, NT, E1])
        f_oh2 = at("f_oh2", 43520, [P, NT, E1])
        f_pre = at("f_pre", 44544, [P, NT, E1])
        f_mx = at("f_mx", 45568, [P, 4, NT])
        f_comb = at("f_comb", 45824, [P, NT, E1X])
        f_h = at("f_h", 47104, [P, 2, 2, HALF])

        a_nat = at("a_nat", 61440, [P, 24, C])
        a_wo = at("a_wo", 86016, [P, KC, H * P])
        QKT = at("QKT", 0, [P, 20, B * T])
        a_wT = at("a_wT", 102400, [P, KC, 24 * P])
        a_woT = at("a_woT", 126976, [P, H, C])
        a_v = at("a_v", 143360, [P, NT, HKV * P])
        a_sq = at("a_sq", 86016, [P, 2, HALF])
        a_m1 = at("a_m1", 90112, [P, 4, HALF])
        a_m2 = at("a_m2", 190720, [P, 2, HALF])
        a_mu = at("a_mu", 194816, [P, KC, 20])
        a_ss = at("a_ss", 194976, [P, 4, 4])
        a_gc = at("a_gc", 195072, [P, 2, 2, P])
        a_gs = at("a_gs", 197120, [P, 2, 2, P])
        a_bt = at("a_bt", 199168, [P, 2, 2, P])
        a_cos = at("a_cos", 184576, [P, 2, P])
        a_sin = at("a_sin", 185600, [P, 2, P])
        a_gb = at("a_gb", 186624, [P, 4, P])
        a_tmp = at("a_tmp", 188672, [P, 2, P])
        s_sc = at("s_sc", 102400, [P, 3, 4, 2 * P])
        s_pt = at("s_pt", 114688, [P, 2, 2, HALF])
        s_mask = at("s_mask", 122880, [P, P])
        s_maskb = at("s_maskb", 123392, [P, P], BF16)
        s_identb = at("s_identb", 123904, [P, P], BF16)
        s_mx = at("s_mx", 124416, [P, 3, 4])
        s_nb = at("s_nb", 124480, [P, 3, 4])
        s_sm = at("s_sm", 124544, [P, 3, 4])
        s_ri = at("s_ri", 124608, [P, 4, 4])

        y_lat = at("y_lat", 124704, [P, B * 2, D])
        y_wq = at("y_wq", 143360, [P, KC, C])
        y_wo = at("y_wo", 145408, [P, KC, C])
        y_wkv = at("y_wkv", 147456, [P, 4, D])
        y_wT = at("y_wT", 148480, [P, 2, KC, C])
        y_kvT = at("y_kvT", 152576, [D, 4 * P])
        y_latT = at("y_latT", 154624, [D, B, T])
        y_hm = at("y_hm", 158720, [P, 8])
        y_q = at("y_q", 184576, [P, KC, B * T])
        y_ax = at("y_ax", 192768, [P, KC, B * T])
        y_km = at("y_km", 0, [P, B, KC, 8, T], F32)
        y_v = at("y_v", 128768, [P, B, 2, C])

        m_wu = at("m_wu", 0, [P, E1X, KC, P])
        m_wg = at("m_wg", 65536, [P, E1X, KC, P])
        m_wd = at("m_wd", 84480, [P, E1X, C])
        m_rw = at("m_rw", 102944, [E1, C])
        m_rT = at("m_rT", 104000, [P, KC, E1])
        m_rb = at("m_rb", 104128, [P, E1])
        m_su = at("m_su", 104416, [P, 2, HALF])
        m_h = at("m_h", 108512, [P, 2, HALF])

        filled = sem("bank_filled")
        emptied = {"act": sem("bank_emptied_by_act"), "dve": sem("bank_emptied_by_dve")}
        banks = PsumBanks(PS, filled, emptied)
        x_loaded = sem("x_loaded")
        consts_loaded = sem("consts_loaded")
        rwkv_loaded = sem("rwkv_weights_loaded")
        xattn_loaded = sem("xattn_weights_loaded")
        kv_cleared = sem("kv_tail_cleared")
        kv_loaded = sem("kv_loaded")
        rope_loaded = sem("query_rope_loaded")
        q_moved = [sem("query_low_parts_moved_even"), sem("query_low_parts_moved_odd")]
        moe0_loaded = sem("moe0_weights_loaded")
        gqa_loaded = sem("gqa_weights_loaded")
        gqa_bcast = sem("gqa_tables_loaded")
        masks_loaded = sem("masks_loaded")
        lat_loaded = sem("latent_weights_loaded")
        moe1_loaded = sem("moe1_weights_loaded")
        stored = sem("output_stored")
        phase_ended = sem("phase_ended")
        var_ready = sem("variances_ready")
        std_ready = sem("deviations_ready")
        hvar_ready = sem("head_variances_ready")
        hstd_ready = sem("head_deviations_ready")
        hn_ready = sem("normalised_tiles")
        dve_step = sem("dve_step")
        act_step = sem("act_step")
        pool_step = sem("pool_step")
        ones_set = sem("ones_set")
        w_exp = sem("rwkv_exp_ready")
        decay_exp = sem("decay_exp_ready")
        rw_ready = sem("rwkv_mixed")
        kv_roped = sem("kv_roped")
        wqr_shift = sem("wqr_shifted")
        q_high = sem("query_high_parts")
        dup_ready = sem("kv_duplicated")
        kt_full = sem("keys_turned")
        kh_ready = sem("key_high_parts")
        kl_ready = sem("key_low_parts")
        qc_ready = sem("query_tile_ready")
        sc_full = sem("scores_filled")
        sc_out = sem("scores_emptied")
        p_exp = sem("probs_exponentiated")
        p_rec = sem("prob_sums_inverted")
        p_norm = sem("probs_normalised")
        t_full = sem("turned_filled")
        t_act = sem("turned_emptied_by_act")
        t_dve = sem("turned_emptied_by_dve")
        av_full = sem("context_filled")
        av_out = sem("context_emptied")
        mask_ready = sem("expert_choice_ready")
        e_shift = sem("logits_shifted")
        e_exp = sem("logits_exponentiated")
        comb_ready = sem("combine_ready")
        sq_ready = sem("squares_ready")
        m_part = sem("rotated_parts")
        m_sum = sem("rotated_summed")
        qk_ready = sem("rotated_ready")
        sh_ready = sem("scores_shifted")
        si_ready = sem("sums_inverted")
        sn_ready = sem("softmax_ready")
        mask_set = sem("causal_mask_ready")
        tables_ready = sem("head_rotation_tables_ready")
        m_scaled = sem("rotated_scaled")

        TURNED_BY_ACT, TURNED_BY_DVE = (0, 1, 2, 4, 5), (3, 6, 7)

        def turn_bank(r):
            return PS[:, (4 + r % 3) * 512:(5 + r % 3) * 512]

        def turned_out(tile_n, r):
            by, taken = (t_act, TURNED_BY_ACT) if r in TURNED_BY_ACT else (t_dve, TURNED_BY_DVE)
            return by, len(taken) * tile_n + taken.index(r) + 1

        def turned_part(r):
            return (P, 4 * (r % 4), 4) if r % 4 < 3 else (LREST, 12, 1)

        A_UNITS = [(b, g, st) for b in range(B) for g in range(HKV) for st in range(2)]
        Y_UNITS = [(b, ct, hg, st) for ct in range(KC) for b in range(B) for hg in range(2) for st in range(2)]
        ctx.enter_context(nc.allow_non_contiguous_dma(reason="small strided loads"))
        block = ctx.enter_context(nc.Block())

        def ended(eng, n):
            eng.drain().then_inc(phase_ended, 1)
            eng.wait_ge(phase_ended, 4 * (n + 1))

        @block.tensor
        def _(pe):
            def begin(key, by):
                ps = banks.claim(key, by)
                if banks.earlier(key) is not None:
                    pe.wait_ge(*banks.emptied(banks.earlier(key)))
                return ps

            def mm(o, a, b, start=True, stop=True, **kw):
                return nc.tensor.matmul(o, a, b, start=start, stop=stop, **kw)

            def turn(key, by, parts):
                ps = begin(key, by)
                c = 0
                for a in parts:
                    r, w = a.shape
                    last = nc.tensor.transpose(ps[0:w, c:c + r], a, ident[0:r, 0:r])
                    c += r
                last.then_inc(filled, 1)

            def turn_x(k):
                for g in range(2):
                    pe.wait_ge(hn_ready, NT * k + 4 * (g + 1))
                    for kc in range(KC):
                        turn(("ht", k, g, kc), "act" if kc else "dve",
                             [HN[:, 4 * g + i, kc * P:(kc + 1) * P] for i in range(4)])

            def wait_ht(k, halves=2):
                for g in range(halves):
                    for kc in range(KC):
                        pe.wait_ge(*banks.emptied(("ht", k, g, kc)))

            def chan_product(key, by, w, half):
                ps = begin(key, by)
                for kc in range(KC):
                    last = mm(ps, w(kc), HT[:, kc, half * HALF:(half + 1) * HALF], kc == 0, kc == KC - 1)
                last.then_inc(filled, 1)

            def out_product(key, pairs):
                ps = begin(key, "dve")
                for i, (a, b) in enumerate(pairs):
                    last = mm(ps[:, 0:C], a, b, i == 0, i == len(pairs) - 1)
                last.then_inc(filled, 1)

            pe.wait_ge(consts_loaded, 16)
            pe.wait_ge(rwkv_loaded, 16 * 6)
            for w in range(4):
                turn(("rwt", w), "act", [r_nat[:, w, ot, kc * P:(kc + 1) * P] for kc in range(KC) for ot in range(KC)])
            turn_x(0)
            wait_ht(0)
            pe.wait_ge(*banks.emptied(("rwt", 3)))
            for half in range(2):
                for ct in range(KC):
                    for w in range(3):
                        chan_product(("kvr", w, ct, half), ("dve", "dve", "act")[w],
                                     lambda kc: r_wt[:, w, kc, ct * P:(ct + 1) * P], half)
            pe.wait_ge(rw_ready, KC)
            for t in range(NT):
                out_product(("ro", t), [(r_num[:, ct, t * P:(t + 1) * P], r_wt[:, 3, ct, :]) for ct in range(KC)])
            ended(pe, 0)
            if LAST == 1:
                return

            pe.wait_ge(xattn_loaded, 16 * 6)
            for h in range(H):
                ps = begin(("w1", h), "act" if h % 2 else "dve")
                for kc in range(KC):
                    last = mm(ps[:, kc * QW:(kc + 1) * QW], x_wq[:, h, kc * P:(kc + 1) * P], x_kcq[:, h, :])
                last.then_inc(filled, 1)
            for g in range(6):
                turn(("wqr", g), "act", [x_wqr[:, 4 * g + i, :] for i in range(4)])
            for g in range(2):
                turn(("wkr", g), "act", [x_wkr[:, 4 * g + i, :] for i in range(4)])
            for g in range(8):
                turn(("xwo", g), "dve", [x_wo[:, ot, h * P:(h + 1) * P] for h in (2 * g, 2 * g + 1) for ot in range(KC)])
            turn_x(1)
            pe.wait_ge(*banks.emptied(("xwo", 7)))
            for g in range(4):
                ps = begin(("u", g), "act")
                for i in range(2):
                    for s in range(2):
                        h = 4 * g + 2 * i + s
                        last = mm(ps[s * D:(s + 1) * D, i * C:(i + 1) * C], x_kckv[:, h, :], x_woT[:, h, :])
                last.then_inc(filled, 1)
            pe.wait_ge(*banks.emptied(("wkr", 1)))
            pe.wait_ge(wqr_shift, 2)
            for p in range(PAIRS):
                ps = begin(("w2", p), "dve")
                for c, w in enumerate((WqrT, WqrS)):
                    A = WkrT[:, 2 * p * D:(2 * p + 1) * D]
                    A2 = WkrT[:, (2 * p + 1) * D:(2 * p + 2) * D]
                    o, g = 256 * c, 3 * p * P
                    mm(ps[:, o:o + 64], w[:, g:g + P], A)
                    mm(ps[0:64, o + 64:o + 128], w[:, g + P:g + P + 64], A)
                    mm(ps[64:128, o + 128:o + 192], w[:, g + P + 64:g + 2 * P], A2)
                    last = mm(ps[:, o + 192:o + 256], w[:, g + 2 * P:g + 3 * P], A2)
                last.then_inc(filled, 1)
            ended(pe, 1)

            def z_jobs(n):
                p, half = n // 2, n % 2
                for j in range(3):
                    chan_product(("z", p, half, j), "dve", lambda kc: W1[:, kc, (3 * p + j) * P:(3 * p + j + 1) * P], half)

            def q_job(n):
                p, half, s = n // 2, n % 2, n % 2
                pe.wait_ge(*banks.emptied(("z", p, half, 2)))
                ps = begin(("q", p, half), "dve")
                for c, r in enumerate((zc, zs)):
                    mm(ps[0:64, :], W2[:, p, c, 0:64], r[:, s, 0, :], c == 0, False, skip_group_check=True)
                    mm(ps[64:128, :], W2[:, p, c, 192:256], r[:, s, 2, :], c == 0, False, skip_group_check=True)
                for c, r in enumerate((zc, zs)):
                    last = mm(ps, W2[:, p, c, 64:192], r[:, s, 1, :], False, c == 1, skip_group_check=True)
                last.then_inc(filled, 1)

            wait_ht(1)
            z_jobs(0)
            for n in range(2 * PAIRS):
                if n + 1 < 2 * PAIRS:
                    z_jobs(n + 1)
                q_job(n)
            ended(pe, 2)

            def keys(b):
                pe.wait_ge(dup_ready, 2 * (b + 1))
                if b > 0:
                    pe.wait_ge(sc_out, 64 * b)
                for g in range(4):
                    for i, lt in enumerate(range(4 * g, min(4 * g + 4, LT))):
                        w = P if lt < LT - 1 else LREST
                        last = nc.tensor.transpose(PS[:, g * HALF + i * P:g * HALF + i * P + w], DUP[0:w, lt, :], ident[0:w, 0:w])
                    last.then_inc(kt_full, 1)

            def scores(b, v, st, hd):
                pe.wait_ge(qc_ready, 16 * b + v + 1)
                n = 2 * (16 * b + v) + hd
                for half, chunks in enumerate((((0, 512), (512, 1024)), ((1024, 1536), (1536, L + 1)))):
                    if not isinstance(n, int) or n > 0:
                        pe.wait_ge(sc_out, 2 * n - 1 + half)
                    for a, z in chunks:
                        mm(PS[:, a:z], QC[st][:, hd, :], KH[:, a:z], True, False)
                        last = mm(PS[:, a:z], QC[st][:, hd, :], KL[:, a:z], False, True)
                    last.then_inc(sc_full, 1)

            def turns(b, v, st, hd):
                pe.wait_ge(p_norm, 2 * (16 * b + v) + hd + 1)
                for i in range(4):
                    r = 4 * hd + i
                    if r >= 3:
                        pe.wait_ge(*turned_out(16 * b + v, r - 3))
                    elif not isinstance(v, int) or 16 * b + v > 0:
                        pe.wait_ge(*turned_out(16 * b + v - 1, (6, 7, 5)[r]))
                    ps = turn_bank(r)
                    for c, lt in enumerate(range(4 * i, min(4 * i + 4, LT))):
                        w = P if lt < LT - 1 else LREST
                        last = nc.tensor.transpose(ps[0:w, c * P:(c + 1) * P], SC[st][hd][:, lt * P:lt * P + w], ident[:, :])
                    last.then_inc(t_full, 1)

            def context(b, v, st):
                pe.wait_ge(t_act, len(TURNED_BY_ACT) * (16 * b + v + 1))
                pe.wait_ge(t_dve, len(TURNED_BY_DVE) * (16 * b + v + 1))
                if not isinstance(v, int) or 16 * b + v > 0:
                    pe.wait_ge(av_out, 16 * b + v)
                for lt in range(LT):
                    w = P if lt < LT - 1 else LREST
                    for hd in range(2):
                        last = mm(PS[hd * D:(hd + 1) * D, 3584 + st * P:3584 + (st + 1) * P],
                                  KVR[0:w, b, lt, :], PT[0:w, hd, lt, :], lt == 0, lt == LT - 1)
                last.then_inc(av_full, 1)

            def tile(b, v, st):
                scores(b, v, st, 0)
                turns(b, v - 1, 1 - st, 0)
                scores(b, v, st, 1)
                turns(b, v - 1, 1 - st, 1)
                context(b, v - 1, 1 - st)

            keys(0)
            for b in range(B):
                pe.wait_ge(kl_ready, 4 * (b + 1))
                scores(b, 0, 0, 0)
                scores(b, 0, 0, 1)
                tile(b, 1, 1)
                with pe.Fori(1, PAIRS) as j:
                    tile(b, 2 * j, 0)
                    tile(b, 2 * j + 1, 1)
                if b + 1 < B:
                    keys(b + 1)
                turns(b, 15, 1, 0)
                turns(b, 15, 1, 1)
                context(b, 15, 1)
            ended(pe, 3)
            for t in range(NT):
                out_product(("xo", t), [(CTX[:, p, t * P:(t + 1) * P], U[:, p, :]) for p in range(PAIRS)])
            ended(pe, 4)
            if LAST == 2:
                return

            pe.wait_ge(moe0_loaded, 16 * 5)
            turn(("gT", 0), "act", [g_nat[:, 0:P]])
            turn(("gT", 1), "act", [g_nat[:, P:C]])
            turn_x(2)
            wait_ht(2)
            pe.wait_ge(*banks.emptied(("gT", 1)))
            ps = begin("logits0", "dve")
            for t in range(NT):
                for kc in range(KC):
                    last = mm(ps[:, t * E0:(t + 1) * E0], HT[:, kc, t * P:(t + 1) * P], g_T[:, kc, :], kc == 0, kc == KC - 1)
            last.then_inc(filled, 1)
            pe.wait_ge(mask_ready, NT - 1)
            ps = begin("rank0", "dve")
            mm(ps[:, 0:NT * E0], f_tri[:, :], f_oh[:, :, 0:E0], True, False)
            mm(ps[:, 0:NT * E0], ones[:, :], f_pre[:, :, 0:E0], False, True).then_inc(filled, 1)

            def down0(n):
                e, half, s = n // 2, n % 2, n % 2
                pe.wait_ge(*banks.emptied(("u0", n, 1)))
                for i in range(2):
                    ps = begin(("d0", n, i), "dve")
                    for tt in range(2):
                        for it in range(KC):
                            o = (2 * i + tt) * P
                            last = mm(ps[:, tt * C:(tt + 1) * C], f_h[:, s, it, o:o + P], f_w2[:, e, it, :], it == 0, it == 1)
                    last.then_inc(filled, 1)

            for n in range(2 * E0 + 1):
                if n < 2 * E0:
                    for it in range(KC):
                        chan_product(("u0", n, it), "act", lambda kc: f_w1[:, n // 2, kc, it * P:(it + 1) * P], n % 2)
                if n >= 1:
                    down0(n - 1)
            ended(pe, 5)
            if LAST == 3:
                return

            pe.wait_ge(gqa_loaded, 32)
            for kc in range(KC):
                for g in range(6):
                    turn(("awT", kc, g), "act", [a_nat[:, 4 * g + i, kc * P:(kc + 1) * P] for i in range(4)])
            for g in range(8):
                turn(("awo", g), "act", [a_wo[:, ot, h * P:(h + 1) * P] for h in (2 * g, 2 * g + 1) for ot in range(KC)])
            turn_x(3)
            wait_ht(3)
            ended(pe, 6)

            def qkv(n):
                t, g = n // 6, n % 6
                ps = begin(("qkv", t, g), "dve" if g < 5 else "act")
                for kc in range(KC):
                    last = mm(ps, HT[:, kc, t * P:(t + 1) * P], a_wT[:, kc, g * HALF:(g + 1) * HALF], kc == 0, kc == 1)
                last.then_inc(filled, 1)

            def qk_turn(n):
                pe.wait_ge(qk_ready, n + 1)
                turn(("qkT", n), "act", [a_m1[:, n % 4, i * P:(i + 1) * P] for i in range(4)])

            for n in range(6 * NT):
                qkv(n)
                t, g = n // 6, n % 6
                if g < 5 and 5 * t + g >= 3:
                    qk_turn(5 * t + g - 3)
            for n in range(5 * NT - 3, 5 * NT):
                qk_turn(n)
            ended(pe, 7)

            def softmax_units(tag, units, turnable, score, use):
                for k in range(len(units) + 3):
                    if k < len(units):
                        score(k, units[k])
                    if 2 <= k < len(units) + 2:
                        m = k - 2
                        pe.wait_ge(*turnable(m))
                        for kb in range(units[m][-1] + 1):
                            turn((tag, "pt", m, kb), "dve" if kb else "act",
                                 [s_sc[:, m % 3, i, kb * P:(kb + 1) * P] for i in range(4)])
                    if k >= 3:
                        m = k - 3
                        for kb in range(units[m][-1] + 1):
                            pe.wait_ge(*banks.emptied((tag, "pt", m, kb)))
                        use(m, units[m])

            def mask(ps, st, heads):
                nk = P * (st + 1)
                for j in range(heads):
                    last = mm(ps[:, (j + 1) * nk - P:(j + 1) * nk], s_identb[:, :], s_maskb[:, :], False, True,
                              skip_group_check=True)
                return last

            def a_score(n, unit):
                b, g, st = unit
                tok = slice((2 * b + st) * P, (2 * b + st + 1) * P)
                nk = P * (st + 1)
                for i in range(st + 1):
                    ps = begin(("a", "s", n, i), "act")
                    for j in range(4 // (st + 1)):
                        h = 4 * g + i * 2 + j
                        mm(ps[:, j * nk:(j + 1) * nk], QKT[:, h, tok], QKT[:, H + g, 2 * b * P:2 * b * P + nk], True, False,
                           skip_group_check=True)
                        last = mask(ps[:, j * nk:(j + 1) * nk], st, 1)
                    last.then_inc(filled, 1)

            def a_use(n, unit):
                b, g, st = unit
                ps = begin(("a", "o", n), "dve")
                for kb in range(st + 1):
                    last = mm(ps, a_v[:, 2 * b + kb, g * P:(g + 1) * P], s_pt[:, n % 2, kb, :], kb == 0, kb == st)
                last.then_inc(filled, 1)

            pe.wait_ge(mask_set, 1)
            softmax_units("a", A_UNITS, lambda m: (sn_ready, m + 1), a_score, a_use)
            for t in range(NT):
                if t % 2 == 0:
                    pe.wait_ge(*banks.emptied(("a", "o", 4 * (t + 2) - 1)))
                out_product(("ao", t), [(QKT[:, h, t * P:(t + 1) * P], a_woT[:, h, :]) for h in range(H)])
            ended(pe, 8)
            if LAST == 4:
                return

            pe.wait_ge(lat_loaded, 16 * (4 + B))
            for w, nat in enumerate((y_wq, y_wo)):
                turn(("ywT", w), "act", [nat[:, ot, kc * P:(kc + 1) * P] for kc in range(KC) for ot in range(KC)])
            turn("ykvT", "act", [y_wkv[:, i, :] for i in range(4)])
            for g in range(2):
                turn(("ylat", g), "act", [y_lat[:, 4 * g + i, :] for i in range(4)])
            turn_x(4)
            pe.wait_ge(*banks.emptied(("ylat", 1)))
            for ct in range(KC):
                for g in range(2):
                    ps = begin(("yk", ct, g), "act" if g else "dve")
                    mm(ps, y_kvT[:, ct * P:(ct + 1) * P], y_latT[:, 2 * g:2 * g + 2, :]).then_inc(filled, 1)
            for b in range(B):
                ps = begin(("yv", b), "act")
                for kb in range(2):
                    last = mm(ps[:, kb * C:(kb + 1) * C], y_latT[:, b, kb * P:(kb + 1) * P], y_kvT[:, 2 * P:4 * P])
                last.then_inc(filled, 1)
            wait_ht(4)
            for ct in range(KC):
                for half in range(2):
                    chan_product(("yq", ct, half), "act", lambda kc: y_wT[:, 0, kc, ct * P:(ct + 1) * P], half)
            for ct in range(KC):
                for half in range(2):
                    pe.wait_ge(*banks.emptied(("yq", ct, half)))
                for g in range(2):
                    pe.wait_ge(*banks.emptied(("yk", ct, g)))

            def y_score(n, unit):
                b, ct, hg, st = unit
                tok = slice((2 * b + st) * P, (2 * b + st + 1) * P)
                for i in range(st + 1):
                    ps = begin(("y", "s", n, i), "act")
                    h0 = 4 * hg + 2 * i
                    keys = y_km[:, b, ct, h0:h0 + 4 - 2 * st, 0:P * (st + 1)]
                    mm(ps, y_q[:, ct, tok], keys, True, False, skip_group_check=True)
                    mask(ps, st, 4 // (st + 1)).then_inc(filled, 1)

            def y_use(n, unit):
                b, ct, hg, st = unit
                ps = begin(("y", "o", n), "dve")
                for i in range(4):
                    c = ct * P + (4 * hg + i) * 16
                    for kb in range(st + 1):
                        last = mm(ps[:, 16 * i:16 * (i + 1)], s_pt[:, n % 2, kb, i * P:(i + 1) * P], y_v[:, b, kb, c:c + 16],
                                  kb == 0, kb == st)
                last.then_inc(filled, 1)

            softmax_units("y", Y_UNITS, lambda m: banks.emptied(("y", "s", m, Y_UNITS[m][-1])), y_score, y_use)
            pe.wait_ge(*banks.emptied(("y", "o", len(Y_UNITS) - 1)))
            for g in range(2):
                for ct in range(KC):
                    turn(("yax", g, ct), "act" if ct else "dve", [HN[:, 4 * g + i, ct * P:(ct + 1) * P] for i in range(4)])
            for t in range(NT):
                if t % 4 == 0:
                    for ct in range(KC):
                        pe.wait_ge(*banks.emptied(("yax", t // 4, ct)))
                out_product(("yo", t), [(y_ax[:, ct, t * P:(t + 1) * P], y_wT[:, 1, ct, :]) for ct in range(KC)])
            ended(pe, 9)
            if LAST == 5:
                return

            pe.wait_ge(moe1_loaded, 16 * 11)
            turn("mrT", "act", [m_rw[:, 0:P], m_rw[:, P:C]])
            turn_x(5)
            wait_ht(5)
            pe.wait_ge(*banks.emptied("mrT"))
            ps = begin("logits1", "dve")
            for t in range(NT):
                for kc in range(KC):
                    last = mm(ps[:, t * E1:(t + 1) * E1], HT[:, kc, t * P:(t + 1) * P], m_rT[:, kc, :], kc == 0, kc == KC - 1)
            last.then_inc(filled, 1)

            def down1(n):
                e, s = n // 2, n % 2
                pe.wait_ge(*banks.emptied(("g1", n)))
                for i in range(2):
                    ps = begin(("d1", n, i), "dve")
                    for tt in range(2):
                        o = (2 * i + tt) * P
                        last = mm(ps[:, tt * C:(tt + 1) * C], m_h[:, s, o:o + P], m_wd[:, e, :])
                    last.then_inc(filled, 1)

            for n in range(2 * E1X + 1):
                if n < 2 * E1X:
                    chan_product(("u1", n), "act", lambda kc: m_wu[:, n // 2, kc, :], n % 2)
                    chan_product(("g1", n), "dve", lambda kc: m_wg[:, n // 2, kc, :], n % 2)
                if n >= 1:
                    down1(n - 1)
            ended(pe, 10)

        @block.scalar
        def _(act):
            steps = [0]

            def link(ins):
                steps[0] += 1
                ins.then_inc(act_step, 1)
                act.wait_ge(act_step, steps[0])

            def copy_out(key, dst, src=None):
                ps = banks.take(key, "act")
                act.wait_ge(*banks.filled(key))
                nc.scalar.activation(dst, src(ps) if src else ps, ACT.Copy).then_inc(emptied["act"], 1)

            def deviations(k):
                act.wait_ge(var_ready, k + 1)
                nc.scalar.activation(rstd[:, :], rstd[:, :], ACT.Sqrt).then_inc(std_ready, 1)

            def ht_out(k):
                for g in range(2):
                    copy_out(("ht", k, g, 1), HT[:, 1, g * HALF:(g + 1) * HALF])

            deviations(0)
            act.wait_ge(rwkv_loaded, 16 * 6)
            link(nc.scalar.activation(r_dec[:, :], r_td[:, :], ACT.Exp))
            nc.scalar.activation(r_dec[:, :], r_dec[:, :], ACT.Exp, scale=-1.0).then_inc(decay_exp, 1)
            link(nc.scalar.activation(r_tf[:, :], r_tf[:, :], ACT.Exp))
            for w in range(4):
                copy_out(("rwt", w), r_wt[:, w, :, :])
            ht_out(0)
            for half in range(2):
                for ct in range(KC):
                    n = half * KC + ct
                    cols = slice(half * HALF, (half + 1) * HALF)
                    act.wait_ge(*banks.emptied(("kvr", 0, ct, half)))
                    nc.scalar.activation(r_w[:, ct, cols], r_w[:, ct, cols], ACT.Exp).then_inc(w_exp, 1)
                    ps = banks.take(("kvr", 2, ct, half), "act")
                    act.wait_ge(*banks.filled(("kvr", 2, ct, half)))
                    nc.scalar.activation(r_sig[:, ct, cols], ps, ACT.Sigmoid).then_inc(emptied["act"], 1)
            ended(act, 0)
            if LAST == 1:
                return

            deviations(1)
            for h in range(1, H, 2):
                copy_out(("w1", h), W1[:, :, h * QW:(h + 1) * QW],
                         lambda ps: ps[:, 0:KC * QW].rearrange("p (k q) -> p k q", k=KC))
            for g in range(6):
                copy_out(("wqr", g), WqrT[:, g * HALF:(g + 1) * HALF], lambda ps: ps[0:D, :])
            for g in range(2):
                copy_out(("wkr", g), WkrT[:, g * HALF:(g + 1) * HALF], lambda ps: ps[0:D, :])
            ht_out(1)
            for g in range(4):
                copy_out(("u", g), U[:, 2 * g:2 * g + 2, :])
            ended(act, 1)
            for n in range(2 * PAIRS):
                p, half = n // 2, n % 2
                act.wait_ge(*banks.filled(("q", p, half)))
                for s in range(2):
                    rows = slice(s * D, (s + 1) * D)
                    src = banks.bank(("q", p, half))[rows, :].rearrange("p (b t) -> p b t", b=2)
                    nc.scalar.activation(QALL[rows, 2 * half:2 * half + 2, p, s, :], src, ACT.Copy).then_inc(q_high, 1)
            ended(act, 2)
            def keys(b):
                for g in range(4):
                    act.wait_ge(kt_full, 4 * b + g + 1)
                    w = min(HALF, L - g * HALF)
                    nc.scalar.activation(KH[:, g * HALF:g * HALF + w], PS[:, g * HALF:g * HALF + w], ACT.Copy).then_inc(kh_ready, 1)

            def exps(b, v, st, hd):
                act.wait_ge(sc_out, 2 * (2 * (16 * b + v) + hd + 1))
                nc.scalar.activation(SC[st][hd][:, :], SC[st][hd][:, :], ACT.Exp, bias=mx[:, st, hd, 1:2], scale=-1.0,
                                     accum_out=sm[:, st, hd:hd + 1]).then_inc(p_exp, 1)

            def turned(b, v, groups):
                for r in groups:
                    act.wait_ge(t_full, 8 * (16 * b + v) + r + 1)
                    if r == 0 and (not isinstance(v, int) or 16 * b + v > 0):
                        act.wait_ge(av_full, 16 * b + v)
                    rows, lt, n = turned_part(r)
                    nc.scalar.activation(PT[0:rows, r // 4, lt:lt + n, :], turn_bank(r)[0:rows, 0:n * P], ACT.Copy).then_inc(t_act, 1)

            def context(b, j, v, st):
                act.wait_ge(av_full, 16 * b + v + 1)
                nc.scalar.activation(CTX[:, j, (2 * b + st) * P:(2 * b + st + 1) * P],
                                     PS[:, 3584 + st * P:3584 + (st + 1) * P], ACT.Copy).then_inc(av_out, 1)

            def tile(b, v, st, prev_j):
                turned(b, v - 1, TURNED_BY_ACT[:3])
                exps(b, v, st, 0)
                turned(b, v - 1, TURNED_BY_ACT[3:])
                exps(b, v, st, 1)
                context(b, prev_j, v - 1, 1 - st)

            keys(0)
            for b in range(B):
                exps(b, 0, 0, 0)
                exps(b, 0, 0, 1)
                tile(b, 1, 1, 0)
                with act.Fori(1, PAIRS) as j:
                    tile(b, 2 * j, 0, bass.ds(j - 1, 1))
                    tile(b, 2 * j + 1, 1, bass.ds(j, 1))
                if b + 1 < B:
                    keys(b + 1)
                turned(b, 15, TURNED_BY_ACT)
                context(b, PAIRS - 1, 15, 1)
            ended(act, 3)
            ended(act, 4)
            if LAST == 2:
                return

            deviations(2)
            copy_out(("gT", 0), g_T[:, 0, :], lambda ps: ps[:, 0:E0])
            copy_out(("gT", 1), g_T[:, 1, :], lambda ps: ps[:, 0:E0])
            ht_out(2)
            act.wait_ge(e_shift, 1)
            nc.scalar.activation(f_e[:, :, 0:E0], f_b[:, :, 0:E0], ACT.Exp).then_inc(e_exp, 1)
            for n in range(2 * E0):
                for it in range(KC):
                    key = ("u0", n, it)
                    ps = banks.take(key, "act")
                    act.wait_ge(*banks.filled(key))
                    if n >= 2:
                        act.wait_ge(*banks.filled(("d0", n - 2, 1)))
                    nc.scalar.activation(f_h[:, n % 2, it, :], ps, ACT.Gelu).then_inc(emptied["act"], 1)
            ended(act, 5)
            if LAST == 3:
                return

            deviations(3)
            for kc in range(KC):
                for g in range(6):
                    copy_out(("awT", kc, g), a_wT[:, kc, g * HALF:(g + 1) * HALF])
            for g in range(8):
                copy_out(("awo", g), a_woT[:, 2 * g:2 * g + 2, :])
            ht_out(3)
            ended(act, 6)

            def qk_out(n):
                t, g = n // 5, n % 5
                copy_out(("qkT", n), QKT[:, 4 * g:4 * g + 4, t * P:(t + 1) * P])

            for n in range(5 * NT + 3):
                if n < 5 * NT:
                    key = ("qkv", n // 5, n % 5)
                    act.wait_ge(*banks.filled(key))
                    if n >= 2:
                        act.wait_ge(hvar_ready, n - 1)
                    nc.scalar.activation(a_sq[:, n % 2, :], banks.bank(key), ACT.Square).then_inc(sq_ready, 1)
                if 1 <= n <= 5 * NT:
                    act.wait_ge(hvar_ready, n)
                    nc.scalar.activation(a_ss[:, (n - 1) % 4, :], a_ss[:, (n - 1) % 4, :], ACT.Sqrt).then_inc(hstd_ready, 1)
                if n % 5 == 0 and n >= 5 and n <= 5 * NT:
                    copy_out(("qkv", n // 5 - 1, 5), a_v[:, n // 5 - 1, :])
                if n >= 3:
                    qk_out(n - 3)
            ended(act, 7)

            def softmax_units(tag, units, base_n, scale):
                for k in range(len(units) + 2):
                    if k < len(units):
                        st = units[k][-1]
                        nk = P * (st + 1)
                        act.wait_ge(sh_ready, base_n + k + 1)
                        if k >= 3:
                            act.wait_ge(*banks.filled((tag, "pt", k - 3, units[k - 3][-1])))
                        per = 4 // (st + 1)
                        for i in range(st + 1):
                            ps = banks.take((tag, "s", k, i), "act")
                            for j in range(per):
                                h = i * per + j
                                ins = nc.scalar.activation(s_sc[:, k % 3, h, 0:nk], ps[:, j * nk:(j + 1) * nk], ACT.Exp,
                                                           bias=s_nb[:, k % 3, h:h + 1], scale=scale,
                                                           accum_out=s_sm[:, k % 3, h:h + 1])
                                if j == per - 1:
                                    ins.then_inc(emptied["act"], 1)
                    if k >= 2:
                        m = k - 2
                        if m >= 2:
                            act.wait_ge(*banks.filled((tag, "o", m - 2)))
                        copy_out((tag, "pt", m, 0), s_pt[:, m % 2, 0, :])

            softmax_units("a", A_UNITS, 0, float(P) ** -0.5)
            ended(act, 8)
            if LAST == 4:
                return

            def keys_out(ct, g):
                ps = banks.take(("yk", ct, g), "act")
                act.wait_ge(*banks.filled(("yk", ct, g)))
                for h in range(8):
                    ins = nc.scalar.activation(y_km[:, 2 * g:2 * g + 2, ct, h, :], ps.rearrange("p (b t) -> p b t", b=2),
                                               ACT.Copy, scale=y_hm[:, h:h + 1])
                ins.then_inc(emptied["act"], 1)

            deviations(4)
            for w in range(2):
                copy_out(("ywT", w), y_wT[:, w, :, :])
            copy_out("ykvT", y_kvT[:, :], lambda ps: ps[0:D, :])
            for g in range(2):
                copy_out(("ylat", g), y_latT[:, 2 * g:2 * g + 2, :], lambda ps: ps[0:D, :])
            ht_out(4)
            for ct in range(KC):
                keys_out(ct, 1)
            for b in range(B):
                copy_out(("yv", b), y_v[:, b, :, :])
            for ct in range(KC):
                for half in range(2):
                    copy_out(("yq", ct, half), y_q[:, ct, half * HALF:(half + 1) * HALF])
            softmax_units("y", Y_UNITS, len(A_UNITS), 0.25)
            for g in range(2):
                copy_out(("yax", g, 1), y_ax[:, 1, g * HALF:(g + 1) * HALF])
            ended(act, 9)
            if LAST == 5:
                return

            deviations(5)
            copy_out("mrT", m_rT[:, :, :], lambda ps: ps[:, 0:KC * E1])
            ht_out(5)
            act.wait_ge(e_shift, 2)
            nc.scalar.activation(f_e[:, :, :], f_e[:, :, :], ACT.Exp).then_inc(e_exp, 1)
            for n in range(2 * E1X):
                key = ("u1", n)
                ps = banks.take(key, "act")
                act.wait_ge(*banks.filled(key))
                if n >= 2:
                    act.wait_ge(*banks.emptied(("g1", n - 2)))
                nc.scalar.activation(m_su[:, n % 2, :], ps, ACT.Silu).then_inc(emptied["act"], 1)
            ended(act, 10)

        @block.vector
        def _(dve):
            steps = [0]

            def link(ins):
                steps[0] += 1
                ins.then_inc(dve_step, 1)
                dve.wait_ge(dve_step, steps[0])

            V = nc.vector

            def copy_out(key, dst, src=None):
                ps = banks.take(key, "dve")
                dve.wait_ge(*banks.filled(key))
                V.tensor_copy(dst, src(ps) if src else ps).then_inc(emptied["dve"], 1)

            def normalise(k):
                for t in range(NT):
                    V.bn_stats(stats[:, t, :], X[:, t, :]).then_inc(dve_step, 1)
                steps[0] += NT
                for t in range(NT):
                    dve.wait_ge(dve_step, steps[0] - NT + t + 1)
                    V.bn_aggr(mv[:, t, :], stats[:, t, :]).then_inc(dve_step, 1)
                steps[0] += NT
                dve.wait_ge(dve_step, steps[0])
                V.tensor_scalar(rstd[:, :], mv[:, :, 1], LN_EPS, None, ALU.add).then_inc(var_ready, 1)
                dve.wait_ge(std_ready, k + 1)
                link(V.reciprocal(rstd[:, :], rstd[:, :]))
                for t in range(NT):
                    V.tensor_scalar(HN[:, t, :], X[:, t, :], mv[:, t, 0:1], rstd[:, t:t + 1],
                                    ALU.subtract, ALU.mult).then_inc(hn_ready, 1)

            def ht_out(k):
                for g in range(2):
                    copy_out(("ht", k, g, 0), HT[:, 0, g * HALF:(g + 1) * HALF])

            def residual(key, t):
                ps = banks.take(key, "dve")
                dve.wait_ge(*banks.filled(key))
                V.tensor_tensor(X[:, t, :], X[:, t, :], ps[:, 0:C], ALU.add).then_inc(emptied["dve"], 1)

            dve.wait_ge(x_loaded, 16 * NT)
            normalise(0)
            ht_out(0)
            dve.wait_ge(ones_set, 1)
            dve.wait_ge(decay_exp, 1)
            for ct in range(KC):
                link(V.tensor_scalar(r_decay[:, ct, :], r_ones[:, :], r_dec[:, ct:ct + 1], None, ALU.mult))
                link(V.memset(r_decay[:, ct, :].rearrange("p (b t) -> p b t", b=B)[:, :, 0:1], 0.0))
            for half in range(2):
                for ct in range(KC):
                    n = half * KC + ct
                    cols = slice(half * HALF, (half + 1) * HALF)
                    ps = banks.take(("kvr", 0, ct, half), "dve")
                    dve.wait_ge(*banks.filled(("kvr", 0, ct, half)))
                    V.tensor_scalar(r_w[:, ct, cols], ps, -10.0, 10.0, ALU.max, ALU.min).then_inc(emptied["dve"], 1)
                    dve.wait_ge(w_exp, n + 1)
                    first = r_w[:, ct, cols].rearrange("p (b t) -> p b t", b=2)[:, :, 0]
                    link(V.tensor_scalar(first, first, r_tf[:, ct:ct + 1], None, ALU.mult))
                    ps = banks.take(("kvr", 1, ct, half), "dve")
                    dve.wait_ge(*banks.filled(("kvr", 1, ct, half)))
                    V.tensor_tensor(r_wv[:, ct, cols], r_w[:, ct, cols], ps, ALU.mult).then_inc(emptied["dve"], 1)
            dve.wait_ge(*banks.emptied(("kvr", 1, KC - 1, 1)))
            for ct in range(KC):
                link(V.tensor_tensor_scan(r_num[:, ct, :], r_decay[:, ct, :], r_wv[:, ct, :], 0.0, ALU.mult, ALU.add))
                link(V.tensor_tensor_scan(r_den[:, ct, :], r_decay[:, ct, :], r_w[:, ct, :], 0.0, ALU.mult, ALU.add))
                link(V.tensor_scalar(r_den[:, ct, :], r_den[:, ct, :], 1e-6, None, ALU.add))
                link(V.reciprocal(r_den[:, ct, :], r_den[:, ct, :]))
                link(V.tensor_tensor(r_num[:, ct, :], r_num[:, ct, :], r_den[:, ct, :], ALU.mult))
                for half in range(2):
                    dve.wait_ge(*banks.emptied(("kvr", 2, ct, half)))
                V.tensor_tensor(r_num[:, ct, :], r_num[:, ct, :], r_sig[:, ct, :], ALU.mult).then_inc(rw_ready, 1)
            for t in range(NT):
                residual(("ro", t), t)
            ended(dve, 0)
            if LAST == 1:
                return

            normalise(1)
            for h in range(0, H, 2):
                copy_out(("w1", h), W1[:, :, h * QW:(h + 1) * QW],
                         lambda ps: ps[:, 0:KC * QW].rearrange("p (k q) -> p k q", k=KC))
            for g in range(8):
                copy_out(("xwo", g), x_woT[:, 2 * g:2 * g + 2, :])
            ht_out(1)
            dve.wait_ge(*banks.emptied(("w1", H - 2)))
            dve.wait_ge(*banks.emptied(("w1", H - 1)))
            link(V.memset(W2[:, :, :, :], 0.0))
            for p in range(PAIRS):
                ps = banks.take(("w2", p), "dve")
                dve.wait_ge(*banks.filled(("w2", p)))
                src = ps.rearrange("p (c w) -> p c w", c=2)
                V.tensor_copy(W2[:, p, :, 0:64], src[:, :, 0:64])
                V.tensor_copy(W2[0:64, p, :, 64:128], src[0:64, :, 64:128])
                V.tensor_copy(W2[64:128, p, :, 128:192], src[64:128, :, 128:192])
                V.tensor_copy(W2[:, p, :, 192:256], src[:, :, 192:256]).then_inc(emptied["dve"], 1)
            ended(dve, 1)
            dve.wait_ge(rope_loaded, 32)

            def rotate(n):
                p, half, s = n // 2, n % 2, n % 2
                for j in range(3):
                    key = ("z", p, half, j)
                    ps = banks.take(key, "dve")
                    dve.wait_ge(*banks.filled(key))
                    if n >= 2:
                        dve.wait_ge(*banks.filled(("q", (n - 2) // 2, n % 2)))
                    V.tensor_tensor(zc[:, s, j, :], ps, cosq[:, j, :], ALU.mult)
                    V.tensor_tensor(zs[:, s, j, :], ps, sinq[:, j, :], ALU.mult).then_inc(emptied["dve"], 1)

            def lows(n):
                p, half, s = n // 2, n % 2, n % 2
                ps = banks.take(("q", p, half), "dve")
                dve.wait_ge(q_high, 2 * (n + 1))
                if n >= 2:
                    dve.wait_ge(q_moved[s], 32 * (n // 2))
                for i in range(2):
                    rows = slice(i * D, (i + 1) * D)
                    hi = QALL[rows, 2 * half:2 * half + 2, p, i, :].bitcast(F32)
                    ins = V.tensor_tensor(qlo[rows, s, :].rearrange("p (b t) -> p b t", b=2),
                                          ps[rows, :].rearrange("p (b t) -> p b t", b=2), hi, ALU.subtract)
                ins.then_inc(emptied["dve"], 1)

            rotate(0)
            for n in range(2 * PAIRS):
                if n + 1 < 2 * PAIRS:
                    rotate(n + 1)
                lows(n)
            ended(dve, 2)
            def keys(b):
                for g in range(4):
                    dve.wait_ge(kh_ready, 4 * b + g + 1)
                    w = min(HALF, L - g * HALF)
                    cols = slice(g * HALF, g * HALF + w)
                    V.tensor_tensor(KL[:, cols], PS[:, cols], KH[:, cols].bitcast(F32), ALU.subtract).then_inc(kl_ready, 1)

            def scores_out(b, v, st, hd):
                n = 2 * (16 * b + v) + hd
                for half, (a, z) in enumerate(((0, 1024), (1024, L))):
                    dve.wait_ge(sc_full, 2 * n + half + 1)
                    if half == 0 and (not isinstance(v, int) or 16 * b + v >= 2):
                        dve.wait_ge(t_full, 8 * (16 * b + v - 2) + 4 * hd + 4)
                    if half == 1:
                        dve.wait_ge(sc_out, 2 * n + 1)
                    V.tensor_scalar(SC[st][hd][:, a:z], PS[:, a:z], -1.0, mx[:, st, hd, 0:1] if half else None,
                                    ALU.mult, ALU.min, accum_out=mx[:, st, hd, half:half + 1]).then_inc(sc_out, 1)

            def invert(b, v, st, hd):
                dve.wait_ge(p_exp, 2 * (16 * b + v) + hd + 1)
                V.reciprocal(ri[:, st, hd:hd + 1], sm[:, st, hd:hd + 1]).then_inc(p_rec, 1)

            def turned(b, v, groups):
                for r in groups:
                    dve.wait_ge(t_full, 8 * (16 * b + v) + r + 1)
                    if r == TURNED_BY_DVE[0] and (not isinstance(v, int) or 16 * b + v > 0):
                        dve.wait_ge(av_full, 16 * b + v)
                    rows, lt, n = turned_part(r)
                    V.tensor_copy(PT[0:rows, r // 4, lt:lt + n, :], turn_bank(r)[0:rows, 0:n * P]).then_inc(t_dve, 1)

            def tile(b, v, st):
                scores_out(b, v, st, 0)
                turned(b, v - 1, TURNED_BY_DVE[:1])
                scores_out(b, v, st, 1)
                invert(b, v, st, 0)
                turned(b, v - 1, TURNED_BY_DVE[1:])
                invert(b, v, st, 1)

            keys(0)
            for b in range(B):
                for hd in range(2):
                    scores_out(b, 0, 0, hd)
                    invert(b, 0, 0, hd)
                tile(b, 1, 1)
                with dve.Fori(1, PAIRS) as j:
                    tile(b, 2 * j, 0)
                    tile(b, 2 * j + 1, 1)
                if b + 1 < B:
                    keys(b + 1)
                turned(b, 15, TURNED_BY_DVE)
            ended(dve, 3)
            for t in range(NT):
                residual(("xo", t), t)
            ended(dve, 4)
            if LAST == 2:
                return

            def bcast(a, n):
                return a.unsqueeze(2).to_broadcast([P, a.shape[1], n])

            def first_choice(src, E, dst, m):
                link(V.tensor_reduce(f_mx[:, m, :], src, AX, ALU.max))
                link(V.tensor_tensor(f_v[:, :, 0:E], src, bcast(f_mx[:, m, :], E), ALU.is_equal))
                link(V.tensor_tensor(f_v[:, :, 0:E], f_v[:, :, 0:E], f_rev[:, :, 0:E], ALU.mult))
                link(V.tensor_reduce(f_mx[:, 3, :], f_v[:, :, 0:E], AX, ALU.max))
                link(V.tensor_tensor(dst, f_v[:, :, 0:E], bcast(f_mx[:, 3, :], E), ALU.is_equal))

            normalise(2)
            ht_out(2)
            lg = f_l[:, :, 0:E0]
            dve.wait_ge(moe0_loaded, 16 * 5)
            copy_out("logits0", lg, lambda ps: ps[:, 0:NT * E0].rearrange("p (t e) -> p t e", t=NT))
            dve.wait_ge(*banks.emptied("logits0"))
            first_choice(lg, E0, f_oh[:, :, 0:E0], 0)
            V.tensor_tensor(f_b[:, :, 0:E0], lg, bcast(f_mx[:, 0, :], E0), ALU.subtract).then_inc(e_shift, 1)
            link(V.memset(f_pre[:, 0, :], 0.0))
            for t in range(1, NT):
                dve.wait_ge(mask_ready, t - 1) if t > 1 else None
                V.tensor_tensor(f_pre[:, t, 0:E0], f_pre[:, t - 1, 0:E0], f_oh[:, t - 1, 0:E0], ALU.add).then_inc(mask_ready, 1)
            dve.wait_ge(e_exp, 1)
            link(V.tensor_reduce(f_mx[:, 1, :], f_e[:, :, 0:E0], AX, ALU.add))
            link(V.reciprocal(f_mx[:, 2, :], f_mx[:, 1, :]))
            ps = banks.take("rank0", "dve")
            dve.wait_ge(*banks.filled("rank0"))
            V.scalar_tensor_tensor(f_comb[:, :, 0:E0], ps[:, 0:NT * E0].rearrange("p (t e) -> p t e", t=NT), float(CAP0),
                                   f_oh[:, :, 0:E0], ALU.is_lt, ALU.mult).then_inc(emptied["dve"], 1)
            dve.wait_ge(*banks.emptied("rank0"))
            link(V.tensor_tensor(f_comb[:, :, 0:E0], f_comb[:, :, 0:E0], bcast(f_mx[:, 2, :], E0), ALU.mult))

            def weigh(key, n, e):
                ps = banks.take(key, "dve")
                dve.wait_ge(*banks.filled(key))
                if n >= 2:
                    dve.wait_ge(*banks.emptied((key[0], n - 2, key[2])))
                for tt in range(2):
                    t = 4 * (n % 2) + 2 * key[2] + tt
                    ins = V.scalar_tensor_tensor(X[:, t, :], ps[:, tt * C:(tt + 1) * C], f_comb[:, t, e:e + 1], X[:, t, :],
                                                 ALU.mult, ALU.add)
                ins.then_inc(emptied["dve"], 1)

            for n in range(2 * E0):
                for i in range(2):
                    weigh(("d0", n, i), n, n // 2)
            ended(dve, 5)
            if LAST == 3:
                return

            normalise(3)
            ht_out(3)
            for kc in range(KC):
                for g in range(6):
                    dve.wait_ge(*banks.emptied(("awT", kc, g)))
            qk = a_wT[:, :, 0:20 * P].rearrange("p k (h d) -> p k h d", d=P)
            link(V.tensor_reduce(a_mu[:, :, :], qk, AX, ALU.add))
            link(V.tensor_scalar(a_mu[:, :, :], a_mu[:, :, :], 1.0 / P, None, ALU.mult))
            for kc in range(KC):
                link(V.tensor_tensor(qk[:, kc], qk[:, kc], bcast(a_mu[:, kc, :], P), ALU.subtract))
            ended(dve, 6)

            def table(a):
                return a.unsqueeze(1).to_broadcast([P, 4, a.shape[1]])

            def m1_of(n):
                return a_m1[:, n % 4, :].rearrange("p (h d) -> p h d", h=4)

            def parts(n):
                i, s = n % 5 // 4, n // 5 % 2
                key = ("qkv", n // 5, n % 5)
                ps = banks.take(key, "dve")
                dve.wait_ge(*banks.filled(key))
                dve.wait_ge(sq_ready, n + 1)
                src, m1, m2 = ps.rearrange("p (h d) -> p h d", h=4), m1_of(n), a_m2[:, n % 2, :].rearrange("p (h d) -> p h d", h=4)
                if n >= 2:
                    dve.wait_ge(m_sum, n - 1)
                if n >= 4:
                    dve.wait_ge(*banks.filled(("qkT", n - 4)))
                V.tensor_tensor(m1, src, table(a_gc[:, i, s, :]), ALU.mult)
                V.tensor_tensor(m2[:, :, 0:64], src[:, :, 64:128], table(a_gs[:, i, s, 0:64]), ALU.mult)
                V.tensor_tensor(m2[:, :, 64:128], src[:, :, 0:64], table(a_gs[:, i, s, 64:128]), ALU.mult).then_inc(m_part, 1)
                V.tensor_reduce(a_ss[:, n % 4, :], a_sq[:, n % 2, :].rearrange("p (h d) -> p h d", h=4), AX,
                                ALU.add).then_inc(emptied["dve"], 1)
                dve.wait_ge(*banks.emptied(key))
                V.tensor_scalar(a_ss[:, n % 4, :], a_ss[:, n % 4, :], 1.0 / P, LN_EPS, ALU.mult, ALU.add).then_inc(hvar_ready, 1)

            def scaled(n):
                m1 = m1_of(n)
                dve.wait_ge(hstd_ready, n + 1)
                link(V.reciprocal(a_ss[:, n % 4, :], a_ss[:, n % 4, :]))
                dve.wait_ge(m_sum, n + 1)
                V.tensor_tensor(m1, m1, bcast(a_ss[:, n % 4, :], P), ALU.mult).then_inc(m_scaled, 1)

            dve.wait_ge(tables_ready, 1)
            for n in range(5 * NT + 1):
                if n < 5 * NT:
                    parts(n)
                if n >= 1:
                    scaled(n - 1)
            dve.wait_ge(masks_loaded, 16)
            V.tensor_copy(s_maskb[:, :], s_mask[:, :])
            V.tensor_copy(s_identb[:, :], ident[:, :]).then_inc(mask_set, 1)
            ended(dve, 7)

            def softmax_units(tag, units, base_n, scale, after):
                for k in range(len(units) + 3):
                    if k < len(units):
                        st = units[k][-1]
                        per = 4 // (st + 1)
                        for i in range(st + 1):
                            key = (tag, "s", k, i)
                            dve.wait_ge(*banks.filled(key))
                            ins = V.tensor_reduce(s_mx[:, k % 3, i * per:(i + 1) * per],
                                                  banks.bank(key).rearrange("p (h k) -> p h k", h=per), AX, ALU.max)
                        link(ins)
                        V.tensor_scalar(s_nb[:, k % 3, :], s_mx[:, k % 3, :], -scale, None, ALU.mult).then_inc(sh_ready, 1)
                    if 1 <= k < len(units) + 1:
                        m = k - 1
                        dve.wait_ge(*banks.emptied((tag, "s", m, units[m][-1])))
                        V.reciprocal(s_ri[:, m % 4, :], s_sm[:, m % 3, :]).then_inc(si_ready, 1)
                    if 2 <= k < len(units) + 2 and units[k - 2][-1]:
                        m = k - 2
                        if m >= 2:
                            dve.wait_ge(*banks.filled((tag, "o", m - 2)))
                        copy_out((tag, "pt", m, 1), s_pt[:, m % 2, 1, :])
                    if k >= 3:
                        after(k - 3, units[k - 3])

            def a_after(n, unit):
                b, g, st = unit
                copy_out(("a", "o", n), QKT[:, 4 * g:4 * g + 4, (2 * b + st) * P:(2 * b + st + 1) * P])

            softmax_units("a", A_UNITS, 0, float(P) ** -0.5, a_after)
            for t in range(NT):
                residual(("ao", t), t)
            ended(dve, 8)
            if LAST == 4:
                return

            normalise(4)
            ht_out(4)
            dve.wait_ge(lat_loaded, 16 * (4 + B))
            for ct in range(KC):
                key = ("yk", ct, 0)
                ps = banks.take(key, "dve")
                dve.wait_ge(*banks.filled(key))
                for h in range(8):
                    ins = V.tensor_scalar(y_km[:, 0:2, ct, h, :], ps.rearrange("p (b t) -> p b t", b=2),
                                          y_hm[:, h:h + 1], None, ALU.mult)
                ins.then_inc(emptied["dve"], 1)

            def y_after(n, unit):
                b, ct, hg, st = unit
                ps = banks.take(("y", "o", n), "dve")
                dve.wait_ge(*banks.filled(("y", "o", n)))
                dst = HN[:, 2 * b + st, ct * P + hg * D:ct * P + (hg + 1) * D]
                V.tensor_tensor(dst.rearrange("p (h d) -> p h d", h=4), ps[:, 0:D].rearrange("p (h d) -> p h d", h=4),
                                bcast(s_ri[:, n % 4, :], 16), ALU.mult).then_inc(emptied["dve"], 1)

            softmax_units("y", Y_UNITS, len(A_UNITS), 0.25, y_after)
            for g in range(2):
                copy_out(("yax", g, 0), y_ax[:, 0, g * HALF:(g + 1) * HALF])
            for t in range(NT):
                residual(("yo", t), t)
            ended(dve, 9)
            if LAST == 5:
                return

            normalise(5)
            ht_out(5)
            dve.wait_ge(moe1_loaded, 16 * 11)
            copy_out("logits1", f_l[:, :, :], lambda ps: ps[:, 0:NT * E1].rearrange("p (t e) -> p t e", t=NT))
            dve.wait_ge(*banks.emptied("logits1"))
            link(V.tensor_reduce(f_mx[:, 0, :], f_l[:, :, :], AX, ALU.max))
            V.tensor_tensor(f_e[:, :, :], f_l[:, :, :], bcast(f_mx[:, 0, :], E1), ALU.subtract).then_inc(e_shift, 1)
            link(V.tensor_tensor(f_b[:, :, :], f_l[:, :, :], m_rb[:, :].unsqueeze(1).to_broadcast([P, NT, E1]), ALU.add))
            first_choice(f_b[:, :, :], E1, f_oh[:, :, :], 1)
            link(V.scalar_tensor_tensor(f_b[:, :, :], f_oh[:, :, :], NEG, f_b[:, :, :], ALU.mult, ALU.add))
            first_choice(f_b[:, :, :], E1, f_oh2[:, :, :], 1)
            link(V.tensor_tensor(f_oh[:, :, :], f_oh[:, :, :], f_oh2[:, :, :], ALU.add))
            dve.wait_ge(e_exp, 2)
            link(V.tensor_tensor(f_v[:, :, :], f_oh[:, :, :], f_e[:, :, :], ALU.mult))
            link(V.tensor_reduce(f_mx[:, 1, :], f_v[:, :, :], AX, ALU.add))
            link(V.reciprocal(f_mx[:, 2, :], f_mx[:, 1, :]))
            link(V.memset(f_comb[:, :, E1:E1X], 1.0))
            link(V.tensor_tensor(f_comb[:, :, 0:E1], f_v[:, :, :], bcast(f_mx[:, 2, :], E1), ALU.mult))
            for n in range(2 * E1X + 1):
                if n < 2 * E1X:
                    key = ("g1", n)
                    ps = banks.take(key, "dve")
                    dve.wait_ge(*banks.filled(key))
                    dve.wait_ge(*banks.emptied(("u1", n)))
                    if n >= 2:
                        dve.wait_ge(*banks.filled(("d1", n - 2, 1)))
                    V.tensor_tensor(m_h[:, n % 2, :], m_su[:, n % 2, :], ps, ALU.mult).then_inc(emptied["dve"], 1)
                if n >= 1:
                    for i in range(2):
                        weigh(("d1", n - 1, i), n - 1, (n - 1) // 2)
            ended(dve, 10)

        @block.gpsimd
        def _(pool):
            G = nc.gpsimd
            steps = [0]

            def link(ins):
                steps[0] += 1
                ins.then_inc(pool_step, 1)
                pool.wait_ge(pool_step, steps[0])

            link(G.memset(r_ones[:, :], 1.0))
            G.memset(ones[:, :], 1.0).then_inc(ones_set, 1)
            G.memset(KVR[:, :, LT - 1, :], 0.0).then_inc(kv_cleared, 1)
            pool.wait_ge(kv_loaded, 16 * (2 * B + 2))
            for b in range(B):
                r, half = KVR[:, b, :, :], D // 2
                G.tensor_tensor(kt1[:, :, :], r, cosk[:, :, :], ALU.mult)
                G.tensor_tensor(kt2[:, :, 0:half], r[:, :, half:D], sink[:, :, 0:half], ALU.mult)
                link(G.tensor_tensor(kt2[:, :, half:D], r[:, :, 0:half], sink[:, :, half:D], ALU.mult))
                link(G.tensor_tensor(r, kt1[:, :, :], kt2[:, :, :], ALU.add))
            ended(pool, 0)
            if LAST == 1:
                return

            pool.wait_ge(*banks.emptied(("wqr", 5)))
            src = WqrT[:, :].rearrange("r (h s i) -> r h s i", h=H, s=2)
            dst = WqrS[:, :].rearrange("r (h s i) -> r h s i", h=H, s=2)
            G.tensor_copy(dst[:, :, 0, :], src[:, :, 1, :]).then_inc(wqr_shift, 1)
            G.tensor_copy(dst[:, :, 1, :], src[:, :, 0, :]).then_inc(wqr_shift, 1)
            ended(pool, 1)
            def doubled(b):
                for s in range(2):
                    G.tensor_copy(DUP[:, :, s * D:(s + 1) * D], KVR[:, b, :, :]).then_inc(dup_ready, 1)

            doubled(0)
            ended(pool, 2)
            for k in (KH, KL):
                link(G.memset(k[:, L:L + 1].bitcast(F32), 0.0))

            def query(b, j, v, st):
                if not isinstance(v, int) or 16 * b + v >= 2:
                    pool.wait_ge(sc_full, 4 * (16 * b + v - 1))
                G.tensor_copy(QC[st][:, :, :], QALL[:, b, j, :, st * P:(st + 1) * P]).then_inc(qc_ready, 1)

            def norm(b, v, st, hd):
                pool.wait_ge(p_rec, 2 * (16 * b + v) + hd + 1)
                G.tensor_tensor(pool_tick[:, 2 * st + hd:2 * st + hd + 1], ones[:, 0:1], ones[:, 0:1], ALU.mult)
                G.tensor_scalar(SC[st][hd][:, :], SC[st][hd][:, :], ri[:, st, hd:hd + 1], 1.0,
                                ALU.mult, ALU.mult).then_inc(p_norm, 1)

            def tile(b, j, v, st):
                norm(b, v, st, 0)
                query(b, j, v + 2, st)
                norm(b, v, st, 1)

            pool.wait_ge(q_moved[0], 32 * PAIRS)
            pool.wait_ge(q_moved[1], 32 * PAIRS)
            for b in range(B):
                query(b, 0, 0, 0)
                query(b, 0, 1, 1)
                if b + 1 < B:
                    pool.wait_ge(kt_full, 4 * (b + 1))
                    doubled(b + 1)
                with pool.Fori(0, PAIRS - 1) as j:
                    tile(b, bass.ds(j + 1, 1), 2 * j, 0)
                    tile(b, bass.ds(j + 1, 1), 2 * j + 1, 1)
                for st in range(2):
                    for hd in range(2):
                        norm(b, 14 + st, st, hd)
            ended(pool, 3)
            ended(pool, 4)
            if LAST == 2:
                return
            ended(pool, 5)
            if LAST == 3:
                return
            pool.wait_ge(gqa_bcast, 16 * 6)
            for i in range(2):
                gain, bias = a_gb[:, 2 * i, :], a_gb[:, 2 * i + 1, :]
                for s in range(2):
                    link(G.tensor_tensor(a_gc[:, i, s, :], a_cos[:, s, :], gain, ALU.mult))
                    link(G.tensor_tensor(a_gs[:, i, s, 0:64], a_sin[:, s, 0:64], gain[:, 64:128], ALU.mult))
                    link(G.tensor_tensor(a_gs[:, i, s, 64:128], a_sin[:, s, 64:128], gain[:, 0:64], ALU.mult))
                    link(G.tensor_tensor(a_bt[:, i, s, :], a_cos[:, s, :], bias, ALU.mult))
                    link(G.tensor_tensor(a_tmp[:, s, 0:64], a_sin[:, s, 0:64], bias[:, 64:128], ALU.mult))
                    link(G.tensor_tensor(a_tmp[:, s, 64:128], a_sin[:, s, 64:128], bias[:, 0:64], ALU.mult))
                    link(G.tensor_tensor(a_bt[:, i, s, :], a_bt[:, i, s, :], a_tmp[:, s, :], ALU.add))
            pool.drain().then_inc(tables_ready, 1)
            ended(pool, 6)

            def rotated(n):
                pool.wait_ge(m_part, n + 1)
                G.tensor_tensor(a_m1[:, n % 4, :], a_m1[:, n % 4, :], a_m2[:, n % 2, :], ALU.add).then_inc(m_sum, 1)

            def biased(n):
                i, s = n % 5 // 4, n // 5 % 2
                m1 = a_m1[:, n % 4, :].rearrange("p (h d) -> p h d", h=4)
                pool.wait_ge(m_scaled, n + 1)
                G.tensor_tensor(m1, m1, a_bt[:, i, s, :].unsqueeze(1).to_broadcast([P, 4, P]), ALU.add).then_inc(qk_ready, 1)

            for n in range(5 * NT + 1):
                if n < 5 * NT:
                    rotated(n)
                if n >= 1:
                    biased(n - 1)
            ended(pool, 7)
            for n, unit in enumerate(A_UNITS):
                nk = P * (unit[-1] + 1)
                pool.wait_ge(si_ready, n + 1)
                for h in range(4):
                    ins = G.tensor_scalar(s_sc[:, n % 3, h, 0:nk], s_sc[:, n % 3, h, 0:nk], s_ri[:, n % 4, h:h + 1], 1.0,
                                          ALU.mult, ALU.mult)
                ins.then_inc(sn_ready, 1)
            ended(pool, 8)
            if LAST == 4:
                return
            ended(pool, 9)
            if LAST == 5:
                return
            ended(pool, 10)

        @block.sync
        def _(sp):
            xv = x.rearrange("b (t p) c -> (b t) p c", p=P)
            ov = out.rearrange("b (t p) c -> (b t) p c", p=P)
            sp.dma_start(ident[:, :], ident_c).then_inc(consts_loaded, 16)
            for t in range(NT):
                sp.dma_start(X[:, t, :], xv[t]).then_inc(x_loaded, 16)
            for w, a in enumerate((L0_attn_Wk, L0_attn_Wv, L0_attn_Wr, L0_attn_Wo)):
                sp.dma_start(r_nat[:, w, :, :], a.rearrange("(o p) i -> p o i", p=P)).then_inc(rwkv_loaded, 16)
            for dst, a in ((r_td, L0_attn_time_decay), (r_tf, L0_attn_time_first)):
                sp.dma_start(dst[:, :], a.rearrange("(k h) s -> (h s) k", k=KC)).then_inc(rwkv_loaded, 16)
            sp.dma_start(cosk[:, :, :], cosk_c).then_inc(kv_loaded, 16)
            sp.dma_start(sink[:, :, :], sink_c).then_inc(kv_loaded, 16)
            sp.wait_ge(kv_cleared, 1)
            for b in range(B):
                whole = (LT - 1) * P
                sp.dma_start(KVR[:, b, 0:LT - 1, :], ctx_512[b, 0:whole, :].rearrange("(t p) d -> p t d", p=P)).then_inc(kv_loaded, 16)
                sp.dma_start(KVR[0:LREST, b, LT - 1, :], ctx_512[b, whole:L, :]).then_inc(kv_loaded, 16)

            def finish(n):
                sp.wait_ge(phase_ended, 4 * (n + 1))
                for t in range(NT):
                    sp.dma_start(ov[t], X[:, t, :]).then_inc(stored, 16)
                sp.wait_ge(stored, 16 * NT)

            if LAST == 1:
                return finish(0)
            sp.wait_ge(phase_ended, 4)
            sp.dma_start(x_wq[:, :, :], L0_xattn_Wq.rearrange("(h k) c -> k h c", k=P)).then_inc(xattn_loaded, 16)
            sp.dma_start(x_kcq[:, :, :], L0_xattn_w_kc_q.rearrange("h k q -> k h q")).then_inc(xattn_loaded, 16)
            sp.dma_start(x_wqr[:, :, :], L0_xattn_W_qr.rearrange("h q r -> (h q) r").rearrange("(t p) r -> p t r", p=P)).then_inc(xattn_loaded, 16)
            sp.dma_start(x_wkr[:, :, :], L0_xattn_W_kr.rearrange("h d r -> (h d) r").rearrange("(t p) r -> p t r", p=P)).then_inc(xattn_loaded, 16)
            sp.dma_start(x_wo[:, :, :], L0_xattn_Wo.rearrange("(o p) k -> p o k", p=P)).then_inc(xattn_loaded, 16)
            sp.dma_start(x_kckv[:, :, :], L0_xattn_w_kc_kv.rearrange("h k d -> k h d")).then_inc(xattn_loaded, 16)
            sp.wait_ge(phase_ended, 8)
            sp.dma_start(cosq[:, :, :], cosq_c).then_inc(rope_loaded, 16)
            sp.dma_start(sinq[:, :, :], sinq_c).then_inc(rope_loaded, 16)
            for n in range(2 * PAIRS):
                p, half, s = n // 2, n % 2, n % 2
                sp.wait_ge(*banks.emptied(("q", p, half)))
                for i in range(2):
                    o = slice((1 - i) * D, (2 - i) * D)
                    sp.dma_start(QALL[o, 2 * half:2 * half + 2, p, i, :].bitcast(F32),
                                 qlo[i * D:(i + 1) * D, s, :].bitcast(F32).rearrange("p (b t) -> p b t", b=2)).then_inc(q_moved[s], 16)
            if LAST == 2:
                return finish(4)
            sp.wait_ge(phase_ended, 4 * 4)
            sp.dma_start(g_nat[:, :], L0_ffn_gate_weight).then_inc(moe0_loaded, 16)
            sp.dma_start(f_rev[:, :, :], rev_c).then_inc(moe0_loaded, 16)
            sp.dma_start(f_tri[:, :], tri_c).then_inc(moe0_loaded, 16)
            sp.dma_start(f_w1[:, :, :, :], L0_ffn_w1.rearrange("e (k p) i -> p e k i", p=P)).then_inc(moe0_loaded, 16)
            sp.dma_start(f_w2[:, :, :, :], L0_ffn_w2.rearrange("e (k p) i -> p e k i", p=P)).then_inc(moe0_loaded, 16)
            if LAST == 3:
                return finish(5)
            sp.dma_start(a_nat[:, :, :], L1_attn_w_qkv.rearrange("(o p) c -> p o c", p=P)).then_inc(gqa_loaded, 16)
            sp.dma_start(a_wo[:, :, :], L1_attn_w_o.rearrange("(o p) k -> p o k", p=P)).then_inc(gqa_loaded, 16)
            sp.wait_ge(phase_ended, 4 * 6)
            sp.dma_start(a_cos[:, :, :], cos1_c).then_inc(gqa_bcast, 16)
            sp.dma_start(a_sin[:, :, :], sin1_c).then_inc(gqa_bcast, 16)
            for i, a in enumerate((L1_attn_qn_g, L1_attn_qn_b, L1_attn_kn_g, L1_attn_kn_b)):
                sp.dma_start(a_gb[:, i, :], a.partition_broadcast(P)).then_inc(gqa_bcast, 16)
            sp.wait_ge(*banks.filled(("qkT", 5 * NT - 1)))
            sp.dma_start(s_mask[:, :], mask_c).then_inc(masks_loaded, 16)
            if LAST == 4:
                return finish(8)
            sp.wait_ge(phase_ended, 4 * 9)
            sp.dma_start(y_wq[:, :, :], L1_xattn_Wq.rearrange("(o p) i -> p o i", p=P)).then_inc(lat_loaded, 16)
            sp.dma_start(y_wo[:, :, :], L1_xattn_Wout.rearrange("(o p) i -> p o i", p=P)).then_inc(lat_loaded, 16)
            sp.dma_start(y_wkv[:, :, :], L1_xattn_Wkv_expand.rearrange("(o p) i -> p o i", p=P)).then_inc(lat_loaded, 16)
            for b in range(B):
                sp.dma_start(y_lat[:, 2 * b:2 * b + 2, :], ctx_512[b, 0:T, :].rearrange("(t p) d -> p t d", p=P)).then_inc(lat_loaded, 16)
            sp.dma_start(y_hm[:, :], hmask_c).then_inc(lat_loaded, 16)
            if LAST == 5:
                return finish(9)
            sp.wait_ge(phase_ended, 4 * 10)
            sp.dma_start(m_wu[:, 0:E1, :, :], L1_ffn_Wu.rearrange("e (k p) i -> p e k i", p=P)).then_inc(moe1_loaded, 16)
            sp.dma_start(m_wg[:, 0:E1, :, :], L1_ffn_Wg.rearrange("e (k p) i -> p e k i", p=P)).then_inc(moe1_loaded, 16)
            sp.dma_start(m_wd[:, 0:E1, :], L1_ffn_Wd.rearrange("e i c -> i e c")).then_inc(moe1_loaded, 16)
            for it in range(2):
                sp.dma_start(m_wu[:, E1 + it, :, :], L1_ffn_Su[0, :, it * P:(it + 1) * P].rearrange("(k p) i -> p k i", p=P)).then_inc(moe1_loaded, 16)
                sp.dma_start(m_wg[:, E1 + it, :, :], L1_ffn_Sg[0, :, it * P:(it + 1) * P].rearrange("(k p) i -> p k i", p=P)).then_inc(moe1_loaded, 16)
            sp.dma_start(m_wd[:, E1:E1X, :], L1_ffn_Sd[0].rearrange("(s i) c -> i s c", i=P)).then_inc(moe1_loaded, 16)
            sp.dma_start(m_rw[:, :], L1_ffn_router_w).then_inc(moe1_loaded, 16)
            sp.dma_start(m_rb[:, :], L1_ffn_router_bias.partition_broadcast(P)).then_inc(moe1_loaded, 16)
            sp.dma_start(f_rev[:, :, :], rev_c).then_inc(moe1_loaded, 16)
            finish(10)


def shape_constants():
    f = np.float32

    def angles(n, dim, base):
        inv = f(1.0) / np.power(f(base), np.arange(0, dim, 2, dtype=f) / f(dim), dtype=f)
        return np.arange(n, dtype=f)[:, None] * inv[None, :]

    c = {"ident_c": np.eye(P, dtype=f)}
    a = np.repeat(angles(T, QW, 10000.0), 2, axis=-1)
    cos, sin = np.cos(a), np.sin(a)
    half = QW // 2
    other = np.concatenate([sin[:, half:], -sin[:, :half]], axis=-1)
    pair = lambda t: np.tile(np.concatenate([t, t], -1).T.reshape(3, P, T).transpose(1, 0, 2), (1, 1, 2))
    c["cosq_c"], c["sinq_c"] = pair(cos), pair(other)
    a = np.zeros((LT * P, D), f)
    a[:L] = np.repeat(angles(L, D, 10000.0), 2, axis=-1)
    sign = np.concatenate([-np.ones(D // 2, f), np.ones(D // 2, f)])
    rows = lambda t: t.reshape(LT, P, D).transpose(1, 0, 2)
    c["cosk_c"], c["sink_c"] = rows(np.cos(a)), rows(np.sin(a) * sign)
    rev = np.arange(E1, 0, -1, dtype=f)
    c["rev_c"] = np.broadcast_to(rev, (P, NT, E1))
    c["tri_c"] = np.triu(np.ones((P, P), f), 1)
    a = angles(T, P, 1000000.0)
    rows = lambda t: np.concatenate([t, t], -1).reshape(2, P, P).transpose(1, 0, 2)
    sign = np.concatenate([-np.ones(P // 2, f), np.ones(P // 2, f)])
    c["cos1_c"], c["sin1_c"] = rows(np.cos(a)), rows(np.sin(a)) * sign
    tri = np.where(np.arange(P)[None, :] > np.arange(P)[:, None], f(NEG), f(0.0))
    c["mask_c"] = tri
    c["hmask_c"] = (np.arange(P)[:, None] // 16 == np.arange(8)[None, :]).astype(f)
    return {k: np.ascontiguousarray(v, dtype=f) for k, v in c.items()}


_INS = ['x', 'ctx_512', 'L0_attn_Wk', 'L0_attn_Wv', 'L0_attn_Wr', 'L0_attn_Wo', 'L0_attn_time_decay', 'L0_attn_time_first',
        'L0_xattn_Wq', 'L0_xattn_w_kc_q', 'L0_xattn_w_kc_kv', 'L0_xattn_W_qr', 'L0_xattn_W_kr', 'L0_xattn_Wo',
        'L0_ffn_gate_weight', 'L0_ffn_w1', 'L0_ffn_w2', 'L1_attn_w_qkv', 'L1_attn_w_o', 'L1_attn_qn_g', 'L1_attn_qn_b',
        'L1_attn_kn_g', 'L1_attn_kn_b', 'L1_xattn_Wq', 'L1_xattn_Wkv_expand', 'L1_xattn_Wout', 'L1_ffn_router_w',
        'L1_ffn_router_bias', 'L1_ffn_Wu', 'L1_ffn_Wg', 'L1_ffn_Wd', 'L1_ffn_Su', 'L1_ffn_Sg', 'L1_ffn_Sd']
_CONSTS = ['ident_c', 'cosq_c', 'sinq_c', 'cosk_c', 'sink_c', 'rev_c', 'tri_c', 'cos1_c', 'sin1_c', 'mask_c', 'hmask_c']
_OUTS = [((4, 256, 256), 'float32')]


def kernel(**inputs):
    import numpy as _np
    import concourse.bacc as _bacc
    from concourse import mybir as _mybir
    from concourse.bass_utils import run_bass_kernel_spmd as _run

    nc = _bacc.Bacc("TRN2", target_bir_lowering=False, num_devices=1)
    arrays, args = {}, []
    consts = shape_constants()
    for name in _INS + _CONSTS:
        a = _np.ascontiguousarray(inputs[name] if name in inputs else consts[name])
        arrays[f"in_{name}_dram"] = a
        args.append(nc.dram_tensor(f"in_{name}_dram", a.shape, _mybir.dt.from_np(a.dtype), kind="ExternalInput").ap())
    for i, (shape, dtype) in enumerate(_OUTS):
        dt = _mybir.dt.from_np(_np.dtype(dtype))
        args.append(nc.dram_tensor(f"out_{i}_dram", shape, dt, kind="ExternalOutput").ap())
    decoder(nc, *args)
    r = _run(nc, [arrays], core_ids=[0])
    got = tuple(r.results[0][f"out_{i}_dram"] for i in range(len(_OUTS)))
    return got[0]
```

```python
from contextlib import ExitStack

import numpy as np

import concourse.bass as bass
from concourse import mybir

P = 128
F32 = mybir.dt.float32
F32R = mybir.dt.float32r
BF16 = mybir.dt.bfloat16
ALU = mybir.AluOpType
ACT = mybir.ActivationFunctionType
AX = mybir.AxisListType.X
LN_EPS = 1e-5

B, T, C = 4, 256, 256
NT = B * T // P
KC = C // P
HALF = 512
L = 1601
LT = (L + P - 1) // P
LREST = L - (LT - 1) * P
D = 64
H = 16
PAIRS = H // 2
QW = 192
E0, E1 = 8, 16
CAP0 = 160
E1X = E1 + 2
HKV = 4
NEG = -1e30


class PsumBanks:

    def __init__(self, psum, filled, emptied):
        self.psum, self.filled_sem, self.emptied_sem = psum, filled, emptied
        self.jobs, self.order, self.count = {}, [], {e: 0 for e in emptied}
        self.taken = {e: 0 for e in emptied}

    def claim(self, key, by):
        assert key not in self.jobs, key
        self.count[by] += 1
        self.jobs[key] = (len(self.order), by, self.count[by])
        self.order.append(key)
        return self.bank(key)

    def bank(self, key):
        n = self.jobs[key][0] % 8
        return self.psum[:, n * 512:(n + 1) * 512]

    def earlier(self, key):
        n = self.jobs[key][0]
        return self.order[n - 8] if n >= 8 else None

    def filled(self, key):
        return self.filled_sem, self.jobs[key][0] + 1

    def emptied(self, key):
        _, by, n = self.jobs[key]
        return self.emptied_sem[by], n

    def take(self, key, by):
        self.taken[by] += 1
        assert self.jobs[key][1:] == (by, self.taken[by]), (key, self.jobs[key], self.taken)
        return self.bank(key)


def decoder(nc, x, ctx_512, L0_attn_Wk, L0_attn_Wv, L0_attn_Wr, L0_attn_Wo, L0_attn_time_decay, L0_attn_time_first,
            L0_xattn_Wq, L0_xattn_w_kc_q, L0_xattn_w_kc_kv, L0_xattn_W_qr, L0_xattn_W_kr, L0_xattn_Wo,
            L0_ffn_gate_weight, L0_ffn_w1, L0_ffn_w2, L1_attn_w_qkv, L1_attn_w_o, L1_attn_qn_g, L1_attn_qn_b,
            L1_attn_kn_g, L1_attn_kn_b, L1_xattn_Wq, L1_xattn_Wkv_expand, L1_xattn_Wout, L1_ffn_router_w,
            L1_ffn_router_bias, L1_ffn_Wu, L1_ffn_Wg, L1_ffn_Wd, L1_ffn_Su, L1_ffn_Sg, L1_ffn_Sd,
            ident_c, cosq_c, sinq_c, cosk_c, sink_c, rev_c, tri_c, cos1_c, sin1_c, mask_c, hmask_c, out):
    with ExitStack() as ctx:
        base = [nc.sbuf_base]

        def sb(name, shape, dt=F32):
            return ctx.enter_context(nc.sbuf_tensor(name, shape, dt))

        def sem(name):
            return ctx.enter_context(nc.semaphore(name))

        X = sb("X", [P, NT, C])
        ident = sb("ident", [P, P])
        stats = sb("stats", [P, NT, 6])
        mv = sb("mv", [P, NT, 2])
        rstd = sb("rstd", [P, NT])
        ones = sb("ones", [P, P])
        pool_tick = sb("pool_tick", [P, 8])
        arena = nc.sbuf_base
        room = nc.sbuf_usable_end - arena

        def at(name, offset, shape, dt=F32):
            size = int(np.prod(shape[1:])) * 4
            assert offset + size <= room, (name, offset + size, room)
            return nc.alloc_sbuf_tensor_at(name, shape, dt, offset=arena + offset)

        HN_AT, HT_AT = at("HN", 168192, [P, NT, C]), at("HT", 176384, [P, KC, NT * P])
        HN_3, HT_3 = at("HN_3", 126976, [P, NT, C]), at("HT_3", 135168, [P, KC, NT * P])
        HN, HT = [HN_AT] * 6, [HT_AT] * 6
        HN[2], HT[2] = HN_3, HT_3
        PS = ctx.enter_context(nc.psum_tensor("PS", [P, 8 * 512], F32))

        r_nat = at("r_nat", 112672, [P, 4, KC, C])
        r_wt = at("r_wt", 120864, [P, 4, KC, C])
        r_w = at("r_w", 0, [P, KC, B * T])
        r_wv = at("r_wv", 8192, [P, KC, B * T])
        r_sig = at("r_sig", 16384, [P, KC, B * T])
        r_num = at("r_num", 24576, [P, KC, B * T])
        r_den = at("r_den", 32768, [P, KC, B * T])
        r_decay = at("r_decay", 40960, [P, KC, B * T])
        r_ones = at("r_ones", 49152, [P, B * T])
        r_td = at("r_td", 161536, [P, KC])
        r_tf = at("r_tf", 161568, [P, KC])
        r_dec = at("r_dec", 161600, [P, KC])

        KVR = at("KVR", 91168, [P, B, LT, D])
        U = at("U", 184576, [P, PAIRS, C])
        cosk = at("cosk", 192768, [P, LT, D])
        sink = at("sink", 196096, [P, LT, D])
        DUP = at("DUP", 192768, [P, LT, 2 * D])
        kt1 = at("kt1", 138304, [P, LT, D])
        kt2 = at("kt2", 141632, [P, LT, D])
        x_wq = at("x_wq", 145152, [P, H, C])
        x_kcq = at("x_kcq", 53248, [P, H, QW])
        x_wqr = at("x_wqr", 161664, [P, 24, D])
        x_wkr = at("x_wkr", 199424, [P, 8, D])
        x_wo = [at("x_wo0", 104480, [P, H * P]), at("x_wo1", 184576, [P, H * P])]
        x_kckv = at("x_kckv", 192768, [P, H, D])
        WqrT = at("WqrT", 0, [D, H * QW])
        WqrS = at("WqrS", 12288, [D, H * QW])
        WkrT = at("WkrT", 24576, [D, H * D])
        x_woT = at("x_woT", 28672, [P, H, C])
        W1 = at("W1", 65536, [P, KC, H * QW])
        W2 = at("W2", 112672, [P, PAIRS, 2, 256])
        cosq = at("cosq", 129056, [P, 3, HALF])
        sinq = at("sinq", 135200, [P, 3, HALF])
        zc = at("zc", 141344, [P, 2, 3, HALF])
        zs = at("zs", 153632, [P, 2, 3, HALF])
        qlo = [at("qlo0", 165920, [P, HALF], F32R), at("qlo1", 199424, [P, HALF], F32R)]
        QALL = at("QALL", 0, [P, PAIRS, B, 2, T], F32R)
        z_w = [[at(f"z_w{p}{i}", 8192 * (p or PAIRS - 1) + 3072 * i, [P, KC, 3 * P], F32R) for i in range(2)] for p in range(PAIRS)]
        z_HTh, z_HTl = at("z_HTh", 176384, [P, 2, KC, HALF], F32R), at("z_HTl", 168192, [P, 2, KC, HALF], F32R)
        KH = [at("KH0", 65536, [P, L + 1], F32R), at("KH1", 80576, [P, L + 1], F32R)]
        KL = [at("KL0", 71968, [P, L + 1], F32R), at("KL1", 104480, [P, L + 1], F32R)]
        SC = [[at(f"S{s}{h}", 112672 + 6432 * (2 * s + h), [P, L]) for h in range(2)] for s in range(2)]
        PT = at("PT", 138432, [P, 2, LT, P])
        CTX = at("CTX", 151744, [P, PAIRS, B * T])
        QC = [at(f"QC{s}", 78400 + 1024 * s, [P, 2, P], F32R) for s in range(2)]
        mx = at("mx", 80448, [P, 2, 2, 2])
        sm = at("sm", 80512, [P, 2, 2])
        ri = at("ri", 80544, [P, 2, 2])

        g_nat = at("g_nat", 34816, [E0, C])
        g_T = at("g_T", 35840, [P, KC, E0])
        f_w1 = at("f_w1", 0, [P, E0, KC, C])
        f_w2 = at("f_w2", 16384, [P, E0, KC, C])
        f_rev = at("f_rev", 36352, [P, NT, E1])
        f_tri = at("f_tri", 37376, [P, P])
        f_l = at("f_l", 38400, [P, NT, E1])
        f_e = at("f_e", 39424, [P, NT, E1])
        f_b = at("f_b", 40448, [P, NT, E1])
        f_v = at("f_v", 41472, [P, NT, E1])
        f_oh = at("f_oh", 42496, [P, NT, E1])
        f_oh2 = at("f_oh2", 43520, [P, NT, E1])
        f_pre = at("f_pre", 44544, [P, NT, E1])
        f_mx = at("f_mx", 45568, [P, 4, NT])
        f_comb = at("f_comb", 45824, [P, NT, E1X])
        f_h = at("f_h", 47104, [P, 3, KC, HALF])
        f_w1l, f_w2l = (at(f"f_w{i + 1}l", 16384 * i, [P, E0, KC, C], F32R) for i in range(2))
        f_hl = at("f_hl", 47104, [P, 3, KC, HALF], F32R)
        f_hh = at("f_hh", 126976, [P, 3, KC, HALF], F32R)
        f_HTh = at("f_HTh", 143360, [P, KC, B * T], F32R)
        f_HTl = at("f_HTl", 151552, [P, KC, B * T], F32R)
        f_wh = at("f_wh", 159744, [P, 3, 2, KC * C], F32R)

        a_nat = at("a_nat", 61440, [P, 24, C])
        a_wo = at("a_wo", 86016, [P, KC, H * P])
        QKT = at("QKT", 0, [P, 20, B * T])
        a_wT = at("a_wT", 102400, [P, KC, 24 * P])
        a_woT = at("a_woT", 126976, [P, H, C])
        a_v = at("a_v", 143360, [P, NT, HKV * P])
        a_sq = at("a_sq", 86016, [P, 2, HALF])
        a_m1 = at("a_m1", 90112, [P, 6, HALF])
        a_m2 = at("a_m2", 190720, [P, 2, HALF])
        a_mu = at("a_mu", 194816, [P, KC, 20])
        a_ss = at("a_ss", 194976, [P, 4, 4])
        a_gc = at("a_gc", 195072, [P, 2, 2, P])
        a_gs = at("a_gs", 197120, [P, 2, 2, P])
        a_bt = at("a_bt", 199168, [P, 2, 2, P])
        a_cos = at("a_cos", 184576, [P, 2, P])
        a_sin = at("a_sin", 185600, [P, 2, P])
        a_gb = at("a_gb", 186624, [P, 4, P])
        a_tmp = at("a_tmp", 188672, [P, 2, P])
        s_sc = at("s_sc", 102400, [P, 4, 4, 2 * P])
        s_pt = at("s_pt", 118784, [P, 2, 2, HALF])
        s_mask = at("s_mask", 165120, [P, P])
        s_maskb = at("s_maskb", 165632, [P, P], BF16)
        s_identb = at("s_identb", 166144, [P, P], BF16)
        s_mx = at("s_mx", 166656, [P, 3, 4])
        s_nb = at("s_nb", 166720, [P, 3, 4])
        s_sm = at("s_sm", 166784, [P, 3, 4])
        s_ri = at("s_ri", 166848, [P, 4, 4])

        y_lat = at("y_lat", 159744, [P, B * 2, D])
        y_wq = at("y_wq", 143360, [P, KC, C])
        y_wo = at("y_wo", 145408, [P, KC, C])
        y_wkv = at("y_wkv", 147456, [P, 4, D])
        y_wqT = at("y_wqT", 148480, [P, KC, C])
        y_kvT = at("y_kvT", 152576, [D, 4 * P])
        y_latT = at("y_latT", 154624, [D, B, T])
        y_hm = at("y_hm", 158720, [P, 8])
        y_kr = at("y_kr", 86016, [P, KC, B * T])
        y_km = at("y_km", 0, [P, B, KC, 8, T], F32)
        y_q = at("y_q", 126976, [P, KC, B * T])
        PAD = 32
        y_v = at("y_v", 184576, [P, B, 2, H, PAD])
        y_ax = [at("y_ax0", 176384, [P, 2, B * T]), at("y_ax1", 135168, [P, 2, B * T])]
        y_wop = at("y_wop", 168192, [P, KC, H, PAD])
        y_woT = at("y_woT", 143360, [P, 4, C])

        m_wu = at("m_wu", 0, [P, E1X, KC, P])
        m_wg = at("m_wg", 65536, [P, E1X, KC, P])
        m_wd = at("m_wd", 83968, [P, E1X, C])
        m_rw = at("m_rw", 163840, [E1, C])
        m_rT = at("m_rT", 164864, [P, KC, E1])
        m_rb = at("m_rb", 164992, [P, E1])
        m_su = at("m_su", 104416, [P, 2, HALF])
        m_h = at("m_h", 47104, [P, 3, HALF])
        m_hh = at("m_hh", 53248, [P, 3, HALF], F32R)
        m_hl = at("m_hl", 59392, [P, 3, HALF], F32R)
        m_wh = at("m_wh", 112672, [P, 3, 3, C], F32R)
        m_wl = at("m_wl", 121888, [P, 3, 3, C], F32R)
        m_HTh = at("m_HTh", 131104, [P, KC, B * T], F32R)
        m_HTl = at("m_HTl", 139296, [P, KC, B * T], F32R)

        filled = sem("bank_filled")
        emptied = {"act": sem("bank_emptied_by_act"), "dve": sem("bank_emptied_by_dve")}
        banks = PsumBanks(PS, filled, emptied)
        x_loaded = [sem("x_first_half_loaded"), sem("x_second_half_loaded")]
        consts_loaded = sem("consts_loaded")
        rwkv_loaded = sem("rwkv_weights_loaded")
        w1_loaded = sem("query_weights_loaded")
        xattn_loaded = sem("xattn_weights_loaded")
        kckv_loaded = sem("context_value_weights_loaded")
        kv_cleared = sem("kv_tail_cleared")
        kv_loaded = sem("kv_loaded")
        rope_loaded = sem("query_rope_loaded")
        q_moved = [sem("query_low_parts_moved_even"), sem("query_low_parts_moved_odd")]
        moe0_loaded = sem("moe0_weights_loaded")
        gqa_loaded = sem("gqa_weights_loaded")
        gqa_bcast = sem("gqa_tables_loaded")
        masks_loaded = sem("masks_loaded")
        lat_loaded = sem("latent_weights_loaded")
        km_ready = sem("masked_keys_ready")
        v_cleared = sem("padded_values_cleared")
        wo_padded = sem("latent_output_weights_padded")
        moe1_loaded = sem("moe1_weights_loaded")
        x_high1 = sem("normalised_high_parts_2")
        w1_split = sem("folded_query_weights_split")
        x_high0, x_low0 = sem("normalised_high_parts_3"), sem("normalised_low_parts_3")
        w_high0, w_low0 = sem("expert_weights_high_parts_3"), sem("expert_weights_low_parts_3")
        h_high0, h_low0 = sem("hidden_high_parts_3"), sem("hidden_low_parts_3")
        x_high = sem("normalised_high_parts")
        x_low = sem("normalised_low_parts")
        w_high = sem("expert_weights_high_parts")
        w_low = sem("expert_weights_low_parts")
        h_high = sem("hidden_high_parts")
        h_low = sem("hidden_low_parts")
        stored = sem("output_stored")
        phase_ended = sem("phase_ended")
        var_ready = sem("variances_ready")
        std_ready = sem("deviations_ready")
        hvar_ready = sem("head_variances_ready")
        hstd_ready = sem("head_deviations_ready")
        hn_ready = sem("normalised_tiles")
        dve_step = sem("dve_step")
        act_step = sem("act_step")
        pool_step = sem("pool_step")
        ones_set = sem("ones_set")
        w_exp = sem("rwkv_exp_ready")
        decay_exp = sem("decay_exp_ready")
        rw_ready = sem("rwkv_mixed")
        kv_roped = sem("kv_roped")
        w2_cleared = sem("folded_weights_cleared")
        wqr_shift = sem("wqr_shifted")
        q_high = sem("query_high_parts")
        dup_ready = sem("kv_duplicated")
        kt_full = sem("keys_turned")
        kh_ready = sem("key_high_parts")
        kl_ready = sem("key_low_parts")
        qc_ready = sem("query_tile_ready")
        sc_full = sem("scores_filled")
        sc_out = sem("scores_emptied")
        p_exp = sem("probs_exponentiated")
        p_rec = sem("prob_sums_inverted")
        p_norm = sem("probs_normalised")
        t_full = sem("turned_filled")
        t_act = sem("turned_emptied_by_act")
        t_dve = sem("turned_emptied_by_dve")
        av_full = sem("context_filled")
        av_out = sem("context_emptied")
        mask_ready = sem("expert_choice_ready")
        e_shift = sem("logits_shifted")
        e_exp = sem("logits_exponentiated")
        comb_ready = sem("combine_ready")
        sq_ready = sem("squares_ready")
        m_part = sem("rotated_parts")
        m_sum = sem("rotated_summed")
        qk_ready = sem("rotated_ready")
        sh_ready = sem("scores_shifted")
        si_ready = sem("sums_inverted")
        sn_ready = sem("softmax_ready")
        mask_set = sem("causal_mask_ready")
        tables_ready = sem("head_rotation_tables_ready")
        m_scaled = sem("rotated_scaled")
        hinv_ready = sem("head_deviations_inverted")

        TURNED_BY_ACT, TURNED_BY_DVE = (0, 1, 2, 4, 5, 6), (3, 7)

        def turn_bank(r):
            return PS[:, (4 + r % 3) * 512:(5 + r % 3) * 512]

        def turned_out(tile_n, r):
            by, taken = (t_act, TURNED_BY_ACT) if r in TURNED_BY_ACT else (t_dve, TURNED_BY_DVE)
            return by, len(taken) * tile_n + taken.index(r) + 1

        def before(b, v, k):
            if not isinstance(v, int) or v >= k:
                return b, v - k
            return (b - 1, v - k + 2 * PAIRS) if b > 0 else None

        def turned_part(r):
            return (P, 4 * (r % 4), 4) if r % 4 < 3 else (LREST, 12, 1)

        def wqr_half(s):
            swapped, plain = (w[:, :].rearrange("r (h s i) -> r h s i", h=H, s=2) for w in (WqrS, WqrT))
            return swapped[:, :, s, :], plain[:, :, 1 - s, :]

        def expert(w, e):
            return w[:, e, :] if len(w.shape) == 3 else w[:, e, :, :].rearrange("p k i -> p (k i)")

        A_UNITS = [(b, g, st) for b in range(B) for g in range(HKV) for st in range(2)]
        Y_UNITS = [(b, ct, hg, st) for ct in range(KC) for b in range(B) for hg in range(2) for st in range(2)]
        ctx.enter_context(nc.allow_non_contiguous_dma(reason="small strided loads"))
        block = ctx.enter_context(nc.Block())

        def ended(eng, n):
            eng.drain().then_inc(phase_ended, 1)
            eng.wait_ge(phase_ended, 4 * (n + 1))

        @block.tensor
        def _(pe):
            def begin(key, by):
                ps = banks.claim(key, by)
                if banks.earlier(key) is not None:
                    pe.wait_ge(*banks.emptied(banks.earlier(key)))
                return ps

            def mm(o, a, b, start=True, stop=True, **kw):
                return nc.tensor.matmul(o, a, b, start=start, stop=stop, **kw)

            def turn(key, by, parts):
                ps = begin(key, by)
                c = 0
                for a in parts:
                    r, w = a.shape
                    last = nc.tensor.transpose(ps[0:w, c:c + r], a, ident[0:r, 0:r])
                    c += r
                last.then_inc(filled, 1)

            def turn_x(k):
                for g in range(2):
                    pe.wait_ge(hn_ready, NT * k + 4 * (g + 1))
                    for kc in range(KC):
                        turn(("ht", k, g, kc), "act" if kc and k != 1 else "dve",
                             [HN[k][:, 4 * g + i, kc * P:(kc + 1) * P] for i in range(4)])

            def wait_ht(k, halves=2):
                for g in range(halves):
                    for kc in range(KC):
                        pe.wait_ge(*banks.emptied(("ht", k, g, kc)))

            def chan_product(k, key, by, w, half):
                ps = begin(key, by)
                for kc in range(KC):
                    last = mm(ps, w(kc), HT[k][:, kc, half * HALF:(half + 1) * HALF], kc == 0, kc == KC - 1)
                last.then_inc(filled, 1)

            def split_product(o, parts):
                for i, (ah, al, bh, bl) in enumerate(parts):
                    mm(o, ah, bh, i == 0, False)
                    mm(o, ah, bl, False, False)
                    last = mm(o, al, bh, False, i == len(parts) - 1)
                return last

            def out_product(key, pairs):
                ps = begin(key, "dve")
                for i, (a, b) in enumerate(pairs):
                    last = mm(ps[:, 0:C], a, b, i == 0, i == len(pairs) - 1)
                last.then_inc(filled, 1)

            pe.wait_ge(consts_loaded, 16)
            pe.wait_ge(rwkv_loaded, 16 * 6)
            for w in range(4):
                turn(("rwt", w), "act", [r_nat[:, w, ot, kc * P:(kc + 1) * P] for kc in range(KC) for ot in range(KC)])
            turn_x(0)
            wait_ht(0)
            pe.wait_ge(*banks.emptied(("rwt", 3)))
            for w, ct, half in [(w, ct, half) for ct in range(KC) for half in range(2) for w in range(2)] + [
                    (2, ct, half) for ct in range(KC) for half in range(2)]:
                chan_product(0, ("kvr", w, ct, half), ("dve", "dve", "act")[w],
                             lambda kc: r_wt[:, w, kc, ct * P:(ct + 1) * P], half)
            pe.wait_ge(w1_loaded, 32)
            for h in range(H):
                ps = begin(("w1", h), "act")
                for kc in range(KC):
                    last = mm(ps[:, kc * QW:(kc + 1) * QW], x_wq[:, h, kc * P:(kc + 1) * P], x_kcq[:, h, :])
                last.then_inc(filled, 1)
            pe.wait_ge(rw_ready, KC)
            for t in range(NT):
                out_product(("ro", t), [(r_num[:, ct, t * P:(t + 1) * P], r_wt[:, 3, ct, :]) for ct in range(KC)])
            turn_x(1)
            ended(pe, 0)

            pe.wait_ge(xattn_loaded, 16 * 4)
            for g in range(6):
                turn(("wqr", g), "act", [x_wqr[:, 4 * g + i, :] for i in range(4)])
            for g in range(2):
                turn(("wkr", g), "act", [x_wkr[:, 4 * g + i, :] for i in range(4)])
            for g in range(8):
                turn(("xwo", g), "dve", [x_wo[ot][:, h * P:(h + 1) * P] for h in (2 * g, 2 * g + 1) for ot in range(KC)])
            pe.wait_ge(kckv_loaded, 16)
            pe.wait_ge(*banks.emptied(("xwo", 7)))
            for g in range(4):
                ps = begin(("u", g), "act")
                for i in range(2):
                    for s in range(2):
                        h = 4 * g + 2 * i + s
                        last = mm(ps[s * D:(s + 1) * D, i * C:(i + 1) * C], x_kckv[:, h, :], x_woT[:, h, :])
                last.then_inc(filled, 1)
            pe.wait_ge(*banks.emptied(("wkr", 1)))
            pe.wait_ge(wqr_shift, 2)
            for p in range(PAIRS):
                ps = begin(("w2", p), "dve")
                for c, w in enumerate((WqrT, WqrS)):
                    A = WkrT[:, 2 * p * D:(2 * p + 1) * D]
                    A2 = WkrT[:, (2 * p + 1) * D:(2 * p + 2) * D]
                    o, g = 256 * c, 3 * p * P
                    mm(ps[:, o:o + 64], w[:, g:g + P], A)
                    mm(ps[0:64, o + 64:o + 128], w[:, g + P:g + P + 64], A)
                    mm(ps[64:128, o + 128:o + 192], w[:, g + P + 64:g + 2 * P], A2)
                    last = mm(ps[:, o + 192:o + 256], w[:, g + 2 * P:g + 3 * P], A2)
                last.then_inc(filled, 1)
            ended(pe, 1)

            def z_jobs(n):
                p, half = n // 2, n % 2
                pe.wait_ge(w1_split, p + 1)
                for j in range(3):
                    ps = begin(("z", p, half, j), "dve")
                    wh, wl = (w[:, :, j * P:(j + 1) * P] for w in z_w[p])
                    split_product(ps, [(wh[:, kc, :], wl[:, kc, :], z_HTh[:, half, kc, :], z_HTl[:, half, kc, :])
                                       for kc in range(KC)]).then_inc(filled, 1)

            def q_job(n):
                p, half, s = n // 2, n % 2, n % 2
                pe.wait_ge(*banks.emptied(("z", p, half, 2)))
                ps = begin(("q", p, half), "dve")
                for c, r in enumerate((zc, zs)):
                    mm(ps[0:64, :], W2[:, p, c, 0:64], r[:, s, 0, :], c == 0, False, skip_group_check=True)
                    mm(ps[64:128, :], W2[:, p, c, 192:256], r[:, s, 2, :], c == 0, False, skip_group_check=True)
                for c, r in enumerate((zc, zs)):
                    last = mm(ps, W2[:, p, c, 64:192], r[:, s, 1, :], False, c == 1, skip_group_check=True)
                last.then_inc(filled, 1)

            wait_ht(1)
            z_jobs(0)
            for n in range(2 * PAIRS):
                if n + 1 < 2 * PAIRS:
                    z_jobs(n + 1)
                q_job(n)
            ended(pe, 2)

            def keys(b):
                pe.wait_ge(dup_ready, 2 * (b + 1))
                for g in range(4):
                    if b > 0 and g < 3:
                        pe.wait_ge(*turned_out(16 * b - 3, (6, 7, 5)[g]))
                    if g == 3:
                        pe.wait_ge(kl_ready, 4 * b + 1)
                    for i, lt in enumerate(range(4 * g, min(4 * g + 4, LT))):
                        w = P if lt < LT - 1 else LREST
                        last = nc.tensor.transpose(turn_bank(g)[:, i * P:i * P + w], DUP[0:w, lt, :], ident[0:w, 0:w])
                    last.then_inc(kt_full, 1)

            def scores(b, v, st, hd):
                pe.wait_ge(qc_ready, 16 * b + v + 1)
                n = 2 * (16 * b + v) + hd
                for half, chunks in enumerate((((0, 512), (512, 1024)), ((1024, 1536), (1536, L + 1)))):
                    if not isinstance(n, int) or n > 0:
                        pe.wait_ge(sc_out, 2 * n - 1 + half)
                    for a, z in chunks:
                        mm(PS[:, a:z], QC[st][:, hd, :], KH[b % 2][:, a:z], True, False)
                        last = mm(PS[:, a:z], QC[st][:, hd, :], KL[b % 2][:, a:z], False, True)
                    last.then_inc(sc_full, 1)

            def turns(b, v, st, hd):
                pe.wait_ge(p_norm, 2 * (16 * b + v) + hd + 1)
                for i in range(4):
                    r = 4 * hd + i
                    if r >= 3:
                        pe.wait_ge(*turned_out(16 * b + v, r - 3))
                    elif isinstance(v, int) and v == 14 and b + 1 < B:
                        pe.wait_ge(kl_ready, 4 * (b + 1) + (4, 2, 3)[r])
                    elif not isinstance(v, int) or 16 * b + v > 0:
                        pe.wait_ge(*turned_out(16 * b + v - 1, (6, 7, 5)[r]))
                    ps = turn_bank(r)
                    for c, lt in enumerate(range(4 * i, min(4 * i + 4, LT))):
                        w = P if lt < LT - 1 else LREST
                        last = nc.tensor.transpose(ps[0:w, c * P:(c + 1) * P], SC[st][hd][:, lt * P:lt * P + w], ident[:, :])
                    last.then_inc(t_full, 1)

            def context(b, v, st):
                pe.wait_ge(t_act, len(TURNED_BY_ACT) * (16 * b + v + 1))
                pe.wait_ge(t_dve, len(TURNED_BY_DVE) * (16 * b + v + 1))
                if not isinstance(v, int) or 16 * b + v > 0:
                    pe.wait_ge(av_out, 16 * b + v)
                for lt in range(LT):
                    w = P if lt < LT - 1 else LREST
                    for hd in range(2):
                        last = mm(PS[hd * D:(hd + 1) * D, 3584 + st * P:3584 + (st + 1) * P],
                                  KVR[0:w, b, lt, :], PT[0:w, hd, lt, :], lt == 0, lt == LT - 1)
                last.then_inc(av_full, 1)

            def tile(b, v, st):
                last, used = before(b, v, 1), before(b, v, 2)
                scores(b, v, st, 0)
                if used:
                    context(*used, st)
                if last:
                    turns(*last, 1 - st, 0)
                scores(b, v, st, 1)
                if last:
                    turns(*last, 1 - st, 1)

            keys(0)
            for b in range(B):
                pe.wait_ge(kl_ready, 4 * (b + 1))
                tile(b, 0, 0)
                tile(b, 1, 1)
                with pe.Fori(1, PAIRS - 1) as j:
                    tile(b, 2 * j, 0)
                    tile(b, 2 * j + 1, 1)
                tile(b, 14, 0)
                if b + 1 < B:
                    keys(b + 1)
                tile(b, 15, 1)
            context(B - 1, 14, 0)
            for hd in range(2):
                turns(B - 1, 15, 1, hd)
            context(B - 1, 15, 1)
            ended(pe, 3)
            for t in range(NT):
                out_product(("xo", t), [(CTX[:, p, t * P:(t + 1) * P], U[:, p, :]) for p in range(PAIRS)])
            turn_x(2)
            ended(pe, 4)

            pe.wait_ge(moe0_loaded, 16 * 5)
            turn(("gT", 0), "act", [g_nat[:, 0:P]])
            turn(("gT", 1), "act", [g_nat[:, P:C]])
            pe.wait_ge(*banks.emptied(("gT", 1)))
            def logits0():
                ps = begin("logits0", "dve")
                for t in range(NT):
                    for kc in range(KC):
                        last = mm(ps[:, t * E0:(t + 1) * E0], HT[2][:, kc, t * P:(t + 1) * P], g_T[:, kc, :], kc == 0, kc == KC - 1)
                last.then_inc(filled, 1)

            def rank0():
                pe.wait_ge(mask_ready, NT - 1)
                ps = begin("rank0", "dve")
                mm(ps[:, 0:NT * E0], f_tri[:, :], f_oh[:, :, 0:E0], True, False)
                mm(ps[:, 0:NT * E0], ones[:, :], f_pre[:, :, 0:E0], False, True).then_inc(filled, 1)

            def up0(n, it):
                e, cols = n // 2, slice(n % 2 * HALF, (n % 2 + 1) * HALF)
                pe.wait_ge(w_low0, 2 * (e + 1))
                if n < 2:
                    pe.wait_ge(x_low0, 2 * (n + 1))
                ps = begin(("u0", n, it), "act")
                parts = []
                for kc in range(KC):
                    o = kc * C + it * P
                    parts.append((f_wh[:, e % 3, 0, o:o + P], f_w1l[:, e, kc, it * P:(it + 1) * P],
                                  f_HTh[:, kc, cols], f_HTl[:, kc, cols]))
                split_product(ps, parts).then_inc(filled, 1)

            def down0(n):
                e, s = n // 2, n % 3
                pe.wait_ge(h_low0, n + 1)
                for i in range(2):
                    ps = begin(("d0", n, i), "dve")
                    for tt in range(2):
                        o = (2 * i + tt) * P
                        last = split_product(ps[:, tt * C:(tt + 1) * C], [
                            (f_hh[:, s, it, o:o + P], f_hl[:, s, it, o:o + P],
                             f_wh[:, e % 3, 1, it * C:(it + 1) * C], f_w2l[:, e, it, :]) for it in range(KC)])
                    last.then_inc(filled, 1)

            logits0()
            for n in range(2 * E0 + 2):
                if n < 2 * E0:
                    for it in range(KC):
                        up0(n, it)
                if n == 1:
                    rank0()
                if n >= 2:
                    down0(n - 2)
                if n in (2, 4):
                    kc = n // 2 - 1
                    pe.wait_ge(gqa_loaded, 32)
                    for g in range(6):
                        turn(("awT", kc, g), "act", [a_nat[:, 4 * g + i, kc * P:(kc + 1) * P] for i in range(4)])
            for g in range(8):
                turn(("awo", g), "act", [a_wo[:, ot, h * P:(h + 1) * P] for h in (2 * g, 2 * g + 1) for ot in range(KC)])
            turn_x(3)
            ended(pe, 5)

            def qkv(n):
                t, g = n // 6, n % 6
                ps = begin(("qkv", t, g), "dve" if g < 5 else "act")
                for kc in range(KC):
                    last = mm(ps, HT[3][:, kc, t * P:(t + 1) * P], a_wT[:, kc, g * HALF:(g + 1) * HALF], kc == 0, kc == 1)
                last.then_inc(filled, 1)

            def qk_turn(n):
                pe.wait_ge(qk_ready, n + 1)
                turn(("qkT", n), "act", [a_m1[:, n % 6, i * P:(i + 1) * P] for i in range(4)])

            for n in range(6 * NT):
                qkv(n)
                t, g = n // 6, n % 6
                if g < 5 and 5 * t + g >= 4:
                    qk_turn(5 * t + g - 4)
            for n in range(5 * NT - 4, 5 * NT):
                qk_turn(n)
            ended(pe, 6)

            def softmax_units(tag, units, turnable, score, use):
                for k in range(len(units) + 4):
                    if k < len(units):
                        score(k, units[k])
                    if 3 <= k < len(units) + 3:
                        m = k - 3
                        pe.wait_ge(*turnable(m))
                        for kb in range(units[m][-1] + 1):
                            turn((tag, "pt", m, kb), "dve" if kb else "act",
                                 [s_sc[:, m % 4, i, kb * P:(kb + 1) * P] for i in range(4)])
                    if k >= 4:
                        m = k - 4
                        for kb in range(units[m][-1] + 1):
                            pe.wait_ge(*banks.emptied((tag, "pt", m, kb)))
                        use(m, units[m])

            def mask(ps, st, heads):
                nk = P * (st + 1)
                for j in range(heads):
                    last = mm(ps[:, (j + 1) * nk - P:(j + 1) * nk], s_identb[:, :], s_maskb[:, :], False, True,
                              skip_group_check=True)
                return last

            def a_score(n, unit):
                b, g, st = unit
                tok = slice((2 * b + st) * P, (2 * b + st + 1) * P)
                nk = P * (st + 1)
                for i in range(st + 1):
                    ps = begin(("a", "s", n, i), "act")
                    for j in range(4 // (st + 1)):
                        h = 4 * g + i * 2 + j
                        mm(ps[:, j * nk:(j + 1) * nk], QKT[:, h, tok], QKT[:, H + g, 2 * b * P:2 * b * P + nk], True, False,
                           skip_group_check=True)
                        last = mask(ps[:, j * nk:(j + 1) * nk], st, 1)
                    last.then_inc(filled, 1)

            def a_use(n, unit):
                b, g, st = unit
                ps = begin(("a", "o", n), "dve")
                for kb in range(st + 1):
                    last = mm(ps, a_v[:, 2 * b + kb, g * P:(g + 1) * P], s_pt[:, n % 2, kb, :], kb == 0, kb == st)
                last.then_inc(filled, 1)

            def latents():
                pe.wait_ge(lat_loaded, 16 * (4 + B))
                turn("ykvT", "act", [y_wkv[:, i, :] for i in range(4)])
                for g in range(2):
                    turn(("ylat", g), "act", [y_lat[:, 4 * g + i, :] for i in range(4)])
                turn("ywqT", "act", [y_wq[:, ot, kc * P:(kc + 1) * P] for kc in range(KC) for ot in range(KC)])
                for ct in range(KC):
                    for g in range(2):
                        pe.wait_ge(*banks.emptied(("ylat", g)))
                        ps = begin(("yk", ct, g), "act")
                        mm(ps, y_kvT[:, ct * P:(ct + 1) * P], y_latT[:, 2 * g:2 * g + 2, :]).then_inc(filled, 1)
                for b in range(B):
                    ps = begin(("yv", b), "act")
                    for kb in range(2):
                        last = mm(ps[:, kb * C:(kb + 1) * C], y_latT[:, b, kb * P:(kb + 1) * P], y_kvT[:, 2 * P:4 * P])
                    last.then_inc(filled, 1)

            pe.wait_ge(mask_set, 1)
            softmax_units("a", A_UNITS, lambda m: (sn_ready, m + 1), a_score, a_use)
            for t in range(NT):
                if t == 4:
                    latents()
                if t % 2 == 0:
                    pe.wait_ge(*banks.emptied(("a", "o", 4 * (t + 2) - 1)))
                out_product(("ao", t), [(QKT[:, h, t * P:(t + 1) * P], a_woT[:, h, :]) for h in range(H)])
            turn_x(4)
            ended(pe, 7)

            for ct in range(KC):
                for half in range(2):
                    chan_product(4, ("yq", ct, half), "act", lambda kc: y_wqT[:, kc, ct * P:(ct + 1) * P], half)

            def y_score(n, unit):
                b, ct, hg, st = unit
                tok = slice((2 * b + st) * P, (2 * b + st + 1) * P)
                pe.wait_ge(km_ready, 2 * (4 * ct + b) + hg + 1)
                pe.wait_ge(*banks.emptied(("yq", ct, b // 2)))
                for i in range(st + 1):
                    ps = begin(("y", "s", n, i), "act")
                    h0 = 4 * hg + 2 * i
                    keys = y_km[:, b, ct, h0:h0 + 4 - 2 * st, 0:P * (st + 1)]
                    mm(ps, y_q[:, ct, tok], keys, True, False, skip_group_check=True)
                    mask(ps, st, 4 // (st + 1)).then_inc(filled, 1)

            def y_use(n, unit):
                b, ct, hg, st = unit
                ps = begin(("y", "o", n), "dve")
                for kb in range(st + 1):
                    for i in range(4):
                        last = mm(ps[PAD * i:PAD * (i + 1), 0:P], y_v[:, b, kb, 8 * ct + 4 * hg + i, :],
                                  s_pt[:, n % 2, kb, i * P:(i + 1) * P], kb == 0, kb == st, skip_group_check=True)
                last.then_inc(filled, 1)

            softmax_units("y", Y_UNITS, lambda m: (sn_ready, len(A_UNITS) + m + 1), y_score, y_use)
            pe.wait_ge(wo_padded, KC)
            for w in range(2):
                turn(("ywo", w), "act", [y_wop[:, ot, 4 * c:4 * (c + 1), :].rearrange("p h r -> p (h r)")
                                         for c in (2 * w, 2 * w + 1) for ot in range(KC)])
            for w in range(2):
                pe.wait_ge(*banks.emptied(("ywo", w)))
            pe.wait_ge(*banks.emptied(("y", "o", len(Y_UNITS) - 1)))
            for t in range(NT):
                out_product(("yo", t), [(y_ax[ct][:, hg, t * P:(t + 1) * P], y_woT[:, 2 * ct + hg, :])
                                        for ct in range(KC) for hg in range(2)])
            turn_x(5)
            ended(pe, 8)

            pe.wait_ge(moe1_loaded, 16 * 11)
            turn("mrT", "act", [m_rw[:, 0:P], m_rw[:, P:C]])
            pe.wait_ge(*banks.emptied("mrT"))
            def logits1():
                ps = begin("logits1", "dve")
                for t in range(NT):
                    for kc in range(KC):
                        last = mm(ps[:, t * E1:(t + 1) * E1], HT[5][:, kc, t * P:(t + 1) * P], m_rT[:, kc, :], kc == 0, kc == KC - 1)
                last.then_inc(filled, 1)

            def up1(key, by, i, n):
                e, cols = n // 2, slice(n % 2 * HALF, (n % 2 + 1) * HALF)
                if n % 2 == 0:
                    pe.wait_ge(w_low, 3 * (e + 1))
                if n < 2:
                    pe.wait_ge(x_low, 2 * (n + 1))
                ps = begin(key, by)
                k = lambda w, kc: w[:, e % 3, i, kc * P:(kc + 1) * P]
                split_product(ps, [(k(m_wh, kc), k(m_wl, kc), m_HTh[:, kc, cols], m_HTl[:, kc, cols])
                                   for kc in range(KC)]).then_inc(filled, 1)

            def down1(n):
                e, s = n // 2, n % 3
                pe.wait_ge(h_low, n + 1)
                for i in range(2):
                    ps = begin(("d1", n, i), "dve")
                    for tt in range(2):
                        o = (2 * i + tt) * P
                        last = split_product(ps[:, tt * C:(tt + 1) * C], [
                            (m_hh[:, s, o:o + P], m_hl[:, s, o:o + P], m_wh[:, e % 3, 2, :], m_wl[:, e % 3, 2, :])])
                    last.then_inc(filled, 1)

            logits1()
            for n in range(2 * E1X + 2):
                if n < 2 * E1X:
                    up1(("u1", n), "act", 0, n)
                    up1(("g1", n), "dve", 1, n)
                if n >= 2:
                    down1(n - 2)
            ended(pe, 9)

        @block.scalar
        def _(act):
            steps = [0]

            def link(ins):
                steps[0] += 1
                ins.then_inc(act_step, 1)
                act.wait_ge(act_step, steps[0])

            def copy_out(key, dst, src=None):
                ps = banks.take(key, "act")
                act.wait_ge(*banks.filled(key))
                nc.scalar.activation(dst, src(ps) if src else ps, ACT.Copy).then_inc(emptied["act"], 1)

            def deviations(k, g):
                act.wait_ge(var_ready, 2 * k + g + 1)
                nc.scalar.activation(rstd[:, 4 * g:4 * g + 4], rstd[:, 4 * g:4 * g + 4], ACT.Sqrt).then_inc(std_ready, 1)

            def ht_out(k):
                for g in range(2):
                    copy_out(("ht", k, g, 1), HT[k][:, 1, g * HALF:(g + 1) * HALF])

            def turned_norm(k):
                for g in range(2):
                    deviations(k, g)
                ht_out(k)

            for g in range(2):
                deviations(0, g)
            for w in range(4):
                copy_out(("rwt", w), r_wt[:, w, :, :])
            act.wait_ge(rwkv_loaded, 16 * 6)
            link(nc.scalar.activation(r_dec[:, :], r_td[:, :], ACT.Exp))
            nc.scalar.activation(r_dec[:, :], r_dec[:, :], ACT.Exp, scale=-1.0).then_inc(decay_exp, 1)
            link(nc.scalar.activation(r_tf[:, :], r_tf[:, :], ACT.Exp))
            ht_out(0)
            for ct in range(KC):
                for half in range(2):
                    cols = slice(half * HALF, (half + 1) * HALF)
                    act.wait_ge(*banks.emptied(("kvr", 0, ct, half)))
                    nc.scalar.activation(r_w[:, ct, cols], r_w[:, ct, cols], ACT.Exp).then_inc(w_exp, 1)
            for ct in range(KC):
                for half in range(2):
                    cols = slice(half * HALF, (half + 1) * HALF)
                    ps = banks.take(("kvr", 2, ct, half), "act")
                    act.wait_ge(*banks.filled(("kvr", 2, ct, half)))
                    nc.scalar.activation(r_sig[:, ct, cols], ps, ACT.Sigmoid).then_inc(emptied["act"], 1)
            for h in range(H):
                copy_out(("w1", h), W1[:, :, h * QW:(h + 1) * QW],
                         lambda ps: ps[:, 0:KC * QW].rearrange("p (k q) -> p k q", k=KC))
            for g in range(2):
                deviations(1, g)
            for g in range(2):
                for kc in range(KC):
                    act.wait_ge(*banks.filled(("ht", 1, g, kc)))
                    nc.scalar.activation(z_HTh[:, g, kc, :], banks.bank(("ht", 1, g, kc)), ACT.Copy).then_inc(x_high1, 1)
            ended(act, 0)

            for g in range(6):
                copy_out(("wqr", g), WqrT[:, g * HALF:(g + 1) * HALF], lambda ps: ps[0:D, :])
            act.wait_ge(*banks.emptied(("wqr", 5)))
            nc.scalar.activation(*wqr_half(1), ACT.Copy).then_inc(wqr_shift, 1)
            for g in range(2):
                copy_out(("wkr", g), WkrT[:, g * HALF:(g + 1) * HALF], lambda ps: ps[0:D, :])
            for g in range(4):
                copy_out(("u", g), U[:, 2 * g:2 * g + 2, :])
            ended(act, 1)
            for n in range(2 * PAIRS):
                p, half = n // 2, n % 2
                act.wait_ge(*banks.filled(("q", p, half)))
                for s in range(2):
                    rows = slice(s * D, (s + 1) * D)
                    src = banks.bank(("q", p, half))[rows, :].rearrange("p (b t) -> p b t", b=2)
                    nc.scalar.activation(QALL[rows, p, 2 * half:2 * half + 2, s, :], src, ACT.Copy).then_inc(q_high, 1)
            ended(act, 2)
            def keys(b):
                for g in range(4):
                    act.wait_ge(kt_full, 4 * b + g + 1)
                    w = min(HALF, L - g * HALF)
                    nc.scalar.activation(KH[b % 2][:, g * HALF:g * HALF + w], turn_bank(g)[:, 0:w], ACT.Copy).then_inc(kh_ready, 1)

            def exps(b, v, st, hd):
                act.wait_ge(sc_out, 2 * (2 * (16 * b + v) + hd + 1))
                nc.scalar.activation(SC[st][hd][:, :], SC[st][hd][:, :], ACT.Exp, bias=mx[:, st, hd, 1:2], scale=-1.0,
                                     accum_out=sm[:, st, hd:hd + 1]).then_inc(p_exp, 1)

            def turned(b, v, groups):
                for r in groups:
                    act.wait_ge(t_full, 8 * (16 * b + v) + r + 1)
                    if r == 0 and (not isinstance(v, int) or 16 * b + v > 0):
                        act.wait_ge(av_full, 16 * b + v)
                    rows, lt, n = turned_part(r)
                    nc.scalar.activation(PT[0:rows, r // 4, lt:lt + n, :], turn_bank(r)[0:rows, 0:n * P], ACT.Copy).then_inc(t_act, 1)

            def context(b, j, v, st):
                act.wait_ge(av_full, 16 * b + v + 1)
                nc.scalar.activation(CTX[:, j, (2 * b + st) * P:(2 * b + st + 1) * P],
                                     PS[:, 3584 + st * P:3584 + (st + 1) * P], ACT.Copy).then_inc(av_out, 1)

            def tile(b, v, st, used_j):
                last, used = before(b, v, 1), before(b, v, 2)
                exps(b, v, st, 0)
                if used:
                    context(used[0], used_j, used[1], st)
                if last:
                    turned(*last, TURNED_BY_ACT)
                exps(b, v, st, 1)

            keys(0)
            for b in range(B):
                tile(b, 0, 0, PAIRS - 1)
                tile(b, 1, 1, PAIRS - 1)
                with act.Fori(1, PAIRS - 1) as j:
                    tile(b, 2 * j, 0, bass.ds(j - 1, 1))
                    tile(b, 2 * j + 1, 1, bass.ds(j - 1, 1))
                tile(b, 14, 0, PAIRS - 2)
                if b + 1 < B:
                    keys(b + 1)
                tile(b, 15, 1, PAIRS - 2)
            context(B - 1, PAIRS - 1, 14, 0)
            turned(B - 1, 15, TURNED_BY_ACT)
            context(B - 1, PAIRS - 1, 15, 1)
            ended(act, 3)
            turned_norm(2)
            ended(act, 4)

            copy_out(("gT", 0), g_T[:, 0, :], lambda ps: ps[:, 0:E0])
            copy_out(("gT", 1), g_T[:, 1, :], lambda ps: ps[:, 0:E0])
            for half in range(2):
                for kc in range(KC):
                    cols = slice(half * HALF, (half + 1) * HALF)
                    nc.scalar.activation(f_HTh[:, kc, cols], HT[2][:, kc, cols], ACT.Copy).then_inc(x_high0, 1)

            def weights_high(e):
                if e >= 3:
                    act.wait_ge(*banks.filled(("d0", 2 * e - 5, 1)))
                for i, w in enumerate((f_w1, f_w2)):
                    nc.scalar.activation(f_wh[:, e % 3, i, :], expert(w, e), ACT.Copy).then_inc(w_high0, 1)

            def gelus(n):
                for it in range(KC):
                    key = ("u0", n, it)
                    ps = banks.take(key, "act")
                    act.wait_ge(*banks.filled(key))
                    if n >= 3 and it == 0:
                        act.wait_ge(*banks.filled(("d0", n - 3, 1)))
                    nc.scalar.activation(f_h[:, n % 3, it, :], ps, ACT.Gelu).then_inc(emptied["act"], 1)
                act.wait_ge(*banks.emptied(("u0", n, KC - 1)))
                nc.scalar.activation(f_hh[:, n % 3, :, :], f_h[:, n % 3, :, :], ACT.Copy).then_inc(h_high0, 1)

            act.wait_ge(moe0_loaded, 16 * 5)
            weights_high(0)
            weights_high(1)
            for n in range(2 * E0):
                gelus(n)
                if n % 2 == 0 and 2 <= n // 2 + 1 < E0:
                    weights_high(n // 2 + 1)
                if n == 0:
                    act.wait_ge(e_shift, 1)
                    nc.scalar.activation(f_e[:, :, 0:E0], f_b[:, :, 0:E0], ACT.Exp).then_inc(e_exp, 1)
                if n in (2, 4):
                    kc = n // 2 - 1
                    for g in range(6):
                        copy_out(("awT", kc, g), a_wT[:, kc, g * HALF:(g + 1) * HALF])
            for g in range(8):
                if g % 4 == 0:
                    deviations(3, g // 4)
                copy_out(("awo", g), a_woT[:, 2 * g:2 * g + 2, :])
            ht_out(3)
            ended(act, 5)

            def qk_out(n):
                t, g = n // 5, n % 5
                copy_out(("qkT", n), QKT[:, 4 * g:4 * g + 4, t * P:(t + 1) * P])

            def scaled(n):
                act.wait_ge(hinv_ready, n + 1)
                act.wait_ge(m_sum, n + 1)
                for h in range(4):
                    m1 = a_m1[:, n % 6, h * P:(h + 1) * P]
                    ins = nc.scalar.activation(m1, m1, ACT.Copy, scale=a_ss[:, n % 4, h:h + 1])
                ins.then_inc(m_scaled, 1)

            for n in range(5 * NT + 4):
                if n < 5 * NT:
                    key = ("qkv", n // 5, n % 5)
                    act.wait_ge(*banks.filled(key))
                    if n >= 2:
                        act.wait_ge(hvar_ready, n - 1)
                    nc.scalar.activation(a_sq[:, n % 2, :], banks.bank(key), ACT.Square).then_inc(sq_ready, 1)
                if 1 <= n <= 5 * NT:
                    act.wait_ge(hvar_ready, n)
                    nc.scalar.activation(a_ss[:, (n - 1) % 4, :], a_ss[:, (n - 1) % 4, :], ACT.Sqrt).then_inc(hstd_ready, 1)
                if 2 <= n <= 5 * NT + 1:
                    scaled(n - 2)
                if n % 5 == 0 and n >= 5 and n <= 5 * NT:
                    copy_out(("qkv", n // 5 - 1, 5), a_v[:, n // 5 - 1, :])
                if n >= 4:
                    qk_out(n - 4)
            ended(act, 6)

            def softmax_units(tag, units, base_n, scale):
                for k in range(len(units) + 3):
                    if k < len(units):
                        st = units[k][-1]
                        nk = P * (st + 1)
                        act.wait_ge(sh_ready, base_n + k + 1)
                        if k >= 4:
                            act.wait_ge(*banks.filled((tag, "pt", k - 4, units[k - 4][-1])))
                        per = 4 // (st + 1)
                        for i in range(st + 1):
                            ps = banks.take((tag, "s", k, i), "act")
                            for j in range(per):
                                h = i * per + j
                                ins = nc.scalar.activation(s_sc[:, k % 4, h, 0:nk], ps[:, j * nk:(j + 1) * nk], ACT.Exp,
                                                           bias=s_nb[:, k % 3, h:h + 1], scale=scale,
                                                           accum_out=s_sm[:, k % 3, h:h + 1])
                                if j == per - 1:
                                    ins.then_inc(emptied["act"], 1)
                    if k >= 3:
                        m = k - 3
                        if m >= 2:
                            act.wait_ge(*banks.filled((tag, "o", m - 2)))
                        copy_out((tag, "pt", m, 0), s_pt[:, m % 2, 0, :])

            softmax_units("a", A_UNITS, 0, float(P) ** -0.5)
            copy_out("ykvT", y_kvT[:, :], lambda ps: ps[0:D, :])
            for g in range(2):
                copy_out(("ylat", g), y_latT[:, 2 * g:2 * g + 2, :], lambda ps: ps[0:D, :])
            copy_out("ywqT", y_wqT[:, :, :])
            for ct in range(KC):
                for g in range(2):
                    copy_out(("yk", ct, g), y_kr[:, ct, g * HALF:(g + 1) * HALF])
            act.wait_ge(v_cleared, 1)
            for b in range(B):
                copy_out(("yv", b), y_v[:, b, :, :, 0:16], lambda ps: ps.rearrange("p (k h d) -> p k h d", k=2, h=H))
            turned_norm(4)
            ended(act, 7)

            for ct in range(KC):
                for half in range(2):
                    copy_out(("yq", ct, half), y_q[:, ct, half * HALF:(half + 1) * HALF])
            softmax_units("y", Y_UNITS, len(A_UNITS), 0.25)
            for w in range(2):
                copy_out(("ywo", w), y_woT[:, 2 * w:2 * w + 2, :])
            turned_norm(5)
            ended(act, 8)

            copy_out("mrT", m_rT[:, :, :], lambda ps: ps[:, 0:KC * E1])
            for half in range(2):
                for kc in range(KC):
                    cols = slice(half * HALF, (half + 1) * HALF)
                    nc.scalar.activation(m_HTh[:, kc, cols], HT[5][:, kc, cols], ACT.Copy).then_inc(x_high, 1)

            def weights_high(e):
                if e >= 3:
                    act.wait_ge(*banks.filled(("d1", 2 * e - 5, 1)))
                for i, w in enumerate((m_wu, m_wg, m_wd)):
                    nc.scalar.activation(m_wh[:, e % 3, i, :], expert(w, e), ACT.Copy).then_inc(w_high, 1)

            def hidden_high(n):
                act.wait_ge(*banks.emptied(("g1", n)))
                if n >= 3:
                    act.wait_ge(*banks.filled(("d1", n - 3, 1)))
                nc.scalar.activation(m_hh[:, n % 3, :], m_h[:, n % 3, :], ACT.Copy).then_inc(h_high, 1)

            act.wait_ge(moe1_loaded, 16 * 11)
            weights_high(0)
            for n in range(2 * E1X + 1):
                if n < 2 * E1X:
                    key = ("u1", n)
                    ps = banks.take(key, "act")
                    act.wait_ge(*banks.filled(key))
                    if n >= 2:
                        act.wait_ge(*banks.emptied(("g1", n - 2)))
                    nc.scalar.activation(m_su[:, n % 2, :], ps, ACT.Silu).then_inc(emptied["act"], 1)
                if n % 2 == 0 and n // 2 + 1 < E1X:
                    weights_high(n // 2 + 1)
                if n == 0:
                    act.wait_ge(e_shift, 2)
                    nc.scalar.activation(f_e[:, :, :], f_e[:, :, :], ACT.Exp).then_inc(e_exp, 1)
                if n >= 1:
                    hidden_high(n - 1)
            ended(act, 9)

        @block.vector
        def _(dve):
            steps = [0]

            def link(ins):
                steps[0] += 1
                ins.then_inc(dve_step, 1)
                dve.wait_ge(dve_step, steps[0])

            V = nc.vector

            def copy_out(key, dst, src=None):
                ps = banks.take(key, "dve")
                dve.wait_ge(*banks.filled(key))
                V.tensor_copy(dst, src(ps) if src else ps).then_inc(emptied["dve"], 1)

            def normalise(k, g, before=None):
                tiles = range(4 * g, 4 * g + 4)
                for t in tiles:
                    if before is not None:
                        before(t)
                    V.bn_stats(stats[:, t, :], X[:, t, :]).then_inc(dve_step, 1)
                steps[0] += 4
                for t in tiles:
                    dve.wait_ge(dve_step, steps[0] - 3 + t - 4 * g)
                    V.bn_aggr(mv[:, t, :], stats[:, t, :]).then_inc(dve_step, 1)
                steps[0] += 4
                dve.wait_ge(dve_step, steps[0])
                r = rstd[:, 4 * g:4 * g + 4]
                V.tensor_scalar(r, mv[:, 4 * g:4 * g + 4, 1], LN_EPS, None, ALU.add).then_inc(var_ready, 1)
                dve.wait_ge(std_ready, 2 * k + g + 1)
                link(V.reciprocal(r, r))
                for t in tiles:
                    V.tensor_scalar(HN[k][:, t, :], X[:, t, :], mv[:, t, 0:1], rstd[:, t:t + 1],
                                    ALU.subtract, ALU.mult).then_inc(hn_ready, 1)

            def ht_out(k):
                for g in range(2):
                    copy_out(("ht", k, g, 0), HT[k][:, 0, g * HALF:(g + 1) * HALF])

            def added(tag):
                def add(t):
                    residual((tag, t), t)
                    dve.wait_ge(*banks.emptied((tag, t)))
                return add

            def turned_norm(k, before):
                for g in range(2):
                    normalise(k, g, before)
                ht_out(k)

            def residual(key, t):
                ps = banks.take(key, "dve")
                dve.wait_ge(*banks.filled(key))
                V.tensor_tensor(X[:, t, :], X[:, t, :], ps[:, 0:C], ALU.add).then_inc(emptied["dve"], 1)

            for g in range(2):
                dve.wait_ge(x_loaded[g], 16 * 4)
                normalise(0, g)
            ht_out(0)
            dve.wait_ge(ones_set, 1)
            dve.wait_ge(decay_exp, 1)
            for ct in range(KC):
                link(V.tensor_scalar(r_decay[:, ct, :], r_ones[:, :], r_dec[:, ct:ct + 1], None, ALU.mult))
                link(V.memset(r_decay[:, ct, :].rearrange("p (b t) -> p b t", b=B)[:, :, 0:1], 0.0))
            for ct in range(KC):
                for half in range(2):
                    cols = slice(half * HALF, (half + 1) * HALF)
                    ps = banks.take(("kvr", 0, ct, half), "dve")
                    dve.wait_ge(*banks.filled(("kvr", 0, ct, half)))
                    V.tensor_scalar(r_w[:, ct, cols], ps, -10.0, 10.0, ALU.max, ALU.min).then_inc(emptied["dve"], 1)
                    dve.wait_ge(w_exp, 2 * ct + half + 1)
                    first = r_w[:, ct, cols].rearrange("p (b t) -> p b t", b=2)[:, :, 0]
                    link(V.tensor_scalar(first, first, r_tf[:, ct:ct + 1], None, ALU.mult))
                    ps = banks.take(("kvr", 1, ct, half), "dve")
                    dve.wait_ge(*banks.filled(("kvr", 1, ct, half)))
                    V.tensor_tensor(r_wv[:, ct, cols], r_w[:, ct, cols], ps, ALU.mult).then_inc(emptied["dve"], 1)
                dve.wait_ge(*banks.emptied(("kvr", 1, ct, 1)))
                V.tensor_tensor_scan(r_num[:, ct, :], r_decay[:, ct, :], r_wv[:, ct, :], 0.0, ALU.mult, ALU.add)
                link(V.tensor_tensor_scan(r_den[:, ct, :], r_decay[:, ct, :], r_w[:, ct, :], 0.0, ALU.mult, ALU.add))
                link(V.tensor_scalar(r_den[:, ct, :], r_den[:, ct, :], 1e-6, None, ALU.add))
            for ct in range(KC):
                link(V.reciprocal(r_den[:, ct, :], r_den[:, ct, :]))
                link(V.tensor_tensor(r_num[:, ct, :], r_num[:, ct, :], r_den[:, ct, :], ALU.mult))
                for half in range(2):
                    dve.wait_ge(*banks.emptied(("kvr", 2, ct, half)))
                V.tensor_tensor(r_num[:, ct, :], r_num[:, ct, :], r_sig[:, ct, :], ALU.mult).then_inc(rw_ready, 1)
            for g in range(2):
                normalise(1, g, added("ro"))
            for g in range(2):
                for kc in range(KC):
                    ps = banks.take(("ht", 1, g, kc), "dve")
                    dve.wait_ge(x_high1, KC * g + kc + 1)
                    dve.wait_ge(*banks.filled(("ht", 1, g, KC - 1)))
                    V.tensor_tensor(z_HTl[:, g, kc, :], ps, z_HTh[:, g, kc, :].bitcast(F32), ALU.subtract).then_inc(emptied["dve"], 1)
            ended(dve, 0)

            for g in range(8):
                copy_out(("xwo", g), x_woT[:, 2 * g:2 * g + 2, :])
            dve.wait_ge(*banks.emptied(("wqr", 5)))
            V.tensor_copy(*wqr_half(0)).then_inc(wqr_shift, 1)
            dve.wait_ge(w2_cleared, 1)
            for p in range(PAIRS):
                ps = banks.take(("w2", p), "dve")
                dve.wait_ge(*banks.filled(("w2", p)))
                src = ps.rearrange("p (c w) -> p c w", c=2)
                V.tensor_copy(W2[:, p, :, 0:64], src[:, :, 0:64])
                V.tensor_copy(W2[0:64, p, :, 64:128], src[0:64, :, 64:128])
                V.tensor_copy(W2[64:128, p, :, 128:192], src[64:128, :, 128:192])
                V.tensor_copy(W2[:, p, :, 192:256], src[:, :, 192:256]).then_inc(emptied["dve"], 1)
            ended(dve, 1)
            dve.wait_ge(rope_loaded, 32)

            def rotate(n):
                p, half, s = n // 2, n % 2, n % 2
                for j in range(3):
                    key = ("z", p, half, j)
                    ps = banks.take(key, "dve")
                    dve.wait_ge(*banks.filled(key))
                    if n >= 2:
                        dve.wait_ge(*banks.filled(("q", (n - 2) // 2, n % 2)))
                    V.tensor_tensor(zc[:, s, j, :], ps, cosq[:, j, :], ALU.mult)
                    V.tensor_tensor(zs[:, s, j, :], ps, sinq[:, j, :], ALU.mult).then_inc(emptied["dve"], 1)

            def lows(n):
                p, half, s = n // 2, n % 2, n % 2
                ps = banks.take(("q", p, half), "dve")
                dve.wait_ge(q_high, 2 * (n + 1))
                if n >= 2:
                    dve.wait_ge(q_moved[s], 32 * (n // 2))
                for i in range(2):
                    rows = slice(i * D, (i + 1) * D)
                    hi = QALL[rows, p, 2 * half:2 * half + 2, i, :].bitcast(F32)
                    ins = V.tensor_tensor(qlo[s][rows, :].rearrange("p (b t) -> p b t", b=2),
                                          ps[rows, :].rearrange("p (b t) -> p b t", b=2), hi, ALU.subtract)
                ins.then_inc(emptied["dve"], 1)

            rotate(0)
            for n in range(2 * PAIRS):
                if n + 1 < 2 * PAIRS:
                    rotate(n + 1)
                lows(n)
            ended(dve, 2)
            def keys(b):
                for g in range(4):
                    dve.wait_ge(kh_ready, 4 * b + g + 1)
                    w = min(HALF, L - g * HALF)
                    cols = slice(g * HALF, g * HALF + w)
                    V.tensor_tensor(KL[b % 2][:, cols], turn_bank(g)[:, 0:w], KH[b % 2][:, cols].bitcast(F32), ALU.subtract).then_inc(kl_ready, 1)

            def scores_out(b, v, st, hd):
                n = 2 * (16 * b + v) + hd
                for half, (a, z) in enumerate(((0, 1024), (1024, L))):
                    dve.wait_ge(sc_full, 2 * n + half + 1)
                    if half == 0 and (not isinstance(v, int) or 16 * b + v >= 2):
                        dve.wait_ge(t_full, 8 * (16 * b + v - 2) + 4 * hd + 4)
                    if half == 1:
                        dve.wait_ge(sc_out, 2 * n + 1)
                    V.tensor_scalar(SC[st][hd][:, a:z], PS[:, a:z], -1.0, mx[:, st, hd, 0:1] if half else None,
                                    ALU.mult, ALU.min, accum_out=mx[:, st, hd, half:half + 1]).then_inc(sc_out, 1)

            def invert(b, v, st, hd):
                dve.wait_ge(p_exp, 2 * (16 * b + v) + hd + 1)
                V.reciprocal(ri[:, st, hd:hd + 1], sm[:, st, hd:hd + 1]).then_inc(p_rec, 1)

            def turned(b, v, groups):
                for r in groups:
                    dve.wait_ge(t_full, 8 * (16 * b + v) + r + 1)
                    if r == TURNED_BY_DVE[0] and (not isinstance(v, int) or 16 * b + v > 0):
                        dve.wait_ge(av_full, 16 * b + v)
                    rows, lt, n = turned_part(r)
                    V.tensor_copy(PT[0:rows, r // 4, lt:lt + n, :], turn_bank(r)[0:rows, 0:n * P]).then_inc(t_dve, 1)

            def tile(b, v, st):
                last = before(b, v, 1)
                scores_out(b, v, st, 0)
                if last:
                    invert(*last, 1 - st, 1)
                invert(b, v, st, 0)
                if last:
                    turned(*last, TURNED_BY_DVE[:1])
                scores_out(b, v, st, 1)
                if last:
                    turned(*last, TURNED_BY_DVE[1:])

            keys(0)
            for b in range(B):
                tile(b, 0, 0)
                tile(b, 1, 1)
                with dve.Fori(1, PAIRS - 1) as j:
                    tile(b, 2 * j, 0)
                    tile(b, 2 * j + 1, 1)
                tile(b, 14, 0)
                if b + 1 < B:
                    keys(b + 1)
                tile(b, 15, 1)
            invert(B - 1, 15, 1, 1)
            turned(B - 1, 15, TURNED_BY_DVE)
            ended(dve, 3)
            turned_norm(2, added("xo"))
            ended(dve, 4)

            def bcast(a, n):
                return a.unsqueeze(2).to_broadcast([P, a.shape[1], n])

            def first_choice(src, E, dst, m):
                link(V.tensor_reduce(f_mx[:, m, :], src, AX, ALU.max))
                link(V.tensor_tensor(f_v[:, :, 0:E], src, bcast(f_mx[:, m, :], E), ALU.is_equal))
                link(V.tensor_tensor(f_v[:, :, 0:E], f_v[:, :, 0:E], f_rev[:, :, 0:E], ALU.mult))
                link(V.tensor_reduce(f_mx[:, 3, :], f_v[:, :, 0:E], AX, ALU.max))
                link(V.tensor_tensor(dst, f_v[:, :, 0:E], bcast(f_mx[:, 3, :], E), ALU.is_equal))

            for half in range(2):
                for kc in range(KC):
                    cols = slice(half * HALF, (half + 1) * HALF)
                    dve.wait_ge(x_high0, KC * half + kc + 1)
                    V.tensor_tensor(f_HTl[:, kc, cols], HT[2][:, kc, cols], f_HTh[:, kc, cols].bitcast(F32),
                                    ALU.subtract).then_inc(x_low0, 1)

            def weights_low(e):
                for i, (w, wl) in enumerate(((f_w1, f_w1l), (f_w2, f_w2l))):
                    dve.wait_ge(w_high0, 2 * e + i + 1)
                    V.tensor_tensor(expert(wl, e), expert(w, e), f_wh[:, e % 3, i, :].bitcast(F32),
                                    ALU.subtract).then_inc(w_low0, 1)

            lg = f_l[:, :, 0:E0]
            dve.wait_ge(moe0_loaded, 16 * 5)
            weights_low(0)
            weights_low(1)
            copy_out("logits0", lg, lambda ps: ps[:, 0:NT * E0].rearrange("p (t e) -> p t e", t=NT))
            dve.wait_ge(*banks.emptied("logits0"))
            first_choice(lg, E0, f_oh[:, :, 0:E0], 0)
            V.tensor_tensor(f_b[:, :, 0:E0], lg, bcast(f_mx[:, 0, :], E0), ALU.subtract).then_inc(e_shift, 1)
            link(V.memset(f_pre[:, 0, :], 0.0))
            for t in range(1, NT):
                dve.wait_ge(mask_ready, t - 1) if t > 1 else None
                V.tensor_tensor(f_pre[:, t, 0:E0], f_pre[:, t - 1, 0:E0], f_oh[:, t - 1, 0:E0], ALU.add).then_inc(mask_ready, 1)
            dve.wait_ge(e_exp, 1)
            link(V.tensor_reduce(f_mx[:, 1, :], f_e[:, :, 0:E0], AX, ALU.add))
            link(V.reciprocal(f_mx[:, 2, :], f_mx[:, 1, :]))
            ps = banks.take("rank0", "dve")
            dve.wait_ge(*banks.filled("rank0"))
            V.scalar_tensor_tensor(f_comb[:, :, 0:E0], ps[:, 0:NT * E0].rearrange("p (t e) -> p t e", t=NT), float(CAP0),
                                   f_oh[:, :, 0:E0], ALU.is_lt, ALU.mult).then_inc(emptied["dve"], 1)
            dve.wait_ge(*banks.emptied("rank0"))
            link(V.tensor_tensor(f_comb[:, :, 0:E0], f_comb[:, :, 0:E0], bcast(f_mx[:, 2, :], E0), ALU.mult))

            def weigh(key, n, e):
                ps = banks.take(key, "dve")
                dve.wait_ge(*banks.filled(key))
                if n >= 2:
                    dve.wait_ge(*banks.emptied((key[0], n - 2, key[2])))
                for tt in range(2):
                    t = 4 * (n % 2) + 2 * key[2] + tt
                    ins = V.scalar_tensor_tensor(X[:, t, :], ps[:, tt * C:(tt + 1) * C], f_comb[:, t, e:e + 1], X[:, t, :],
                                                 ALU.mult, ALU.add)
                ins.then_inc(emptied["dve"], 1)

            def centre(kc):
                for g in range(5):
                    dve.wait_ge(*banks.emptied(("awT", kc, g)))
                for h in (0, 10):
                    qk = a_wT[:, kc, h * P:(h + 10) * P].rearrange("p (h d) -> p h d", d=P)
                    mu = a_mu[:, kc, h:h + 10]
                    link(V.tensor_reduce(mu, qk, AX, ALU.add))
                    link(V.tensor_scalar(mu, mu, 1.0 / P, None, ALU.mult))
                    link(V.tensor_tensor(qk, qk, mu.unsqueeze(2).to_broadcast([P, 10, P]), ALU.subtract))
                    yield

            for n in range(2 * E0 - 1):
                if n % 2 == 0 and n // 2 + 2 < E0:
                    weights_low(n // 2 + 2)
                for i in range(2):
                    weigh(("d0", n, i), n, n // 2)
                if n == 4:
                    centring = [centre(0), centre(1)]
                if n in (4, 6, 8, 10):
                    next(centring[(n - 4) // 4])
            dve.wait_ge(*banks.emptied(("d0", 2 * E0 - 2, 1)))
            normalise(3, 0)
            for i in range(2):
                weigh(("d0", 2 * E0 - 1, i), 2 * E0 - 1, E0 - 1)
            dve.wait_ge(*banks.emptied(("d0", 2 * E0 - 1, 1)))
            normalise(3, 1)
            ht_out(3)
            ended(dve, 5)

            def table(a):
                return a.unsqueeze(1).to_broadcast([P, 4, a.shape[1]])

            def m1_of(n):
                return a_m1[:, n % 6, :].rearrange("p (h d) -> p h d", h=4)

            def parts(n):
                i, s = n % 5 // 4, n // 5 % 2
                key = ("qkv", n // 5, n % 5)
                ps = banks.take(key, "dve")
                dve.wait_ge(*banks.filled(key))
                dve.wait_ge(sq_ready, n + 1)
                src, m1, m2 = ps.rearrange("p (h d) -> p h d", h=4), m1_of(n), a_m2[:, n % 2, :].rearrange("p (h d) -> p h d", h=4)
                if n >= 2:
                    dve.wait_ge(m_sum, n - 1)
                if n >= 6:
                    dve.wait_ge(*banks.filled(("qkT", n - 6)))
                V.tensor_tensor(m1, src, table(a_gc[:, i, s, :]), ALU.mult)
                V.tensor_tensor(m2[:, :, 0:64], src[:, :, 64:128], table(a_gs[:, i, s, 0:64]), ALU.mult)
                V.tensor_tensor(m2[:, :, 64:128], src[:, :, 0:64], table(a_gs[:, i, s, 64:128]), ALU.mult).then_inc(m_part, 1)
                V.tensor_reduce(a_ss[:, n % 4, :], a_sq[:, n % 2, :].rearrange("p (h d) -> p h d", h=4), AX,
                                ALU.add).then_inc(emptied["dve"], 1)
                dve.wait_ge(*banks.emptied(key))
                V.tensor_scalar(a_ss[:, n % 4, :], a_ss[:, n % 4, :], 1.0 / P, LN_EPS, ALU.mult, ALU.add).then_inc(hvar_ready, 1)

            dve.wait_ge(tables_ready, 4)
            for n in range(5 * NT + 1):
                if n < 5 * NT:
                    parts(n)
                if n >= 1:
                    dve.wait_ge(hstd_ready, n)
                    V.reciprocal(a_ss[:, (n - 1) % 4, :], a_ss[:, (n - 1) % 4, :]).then_inc(hinv_ready, 1)
            dve.wait_ge(masks_loaded, 16)
            V.tensor_copy(s_maskb[:, :], s_mask[:, :])
            V.tensor_copy(s_identb[:, :], ident[:, :]).then_inc(mask_set, 1)
            ended(dve, 6)

            def softmax_units(tag, units, base_n, scale, after):
                for k in range(len(units) + 4):
                    if k < len(units):
                        st = units[k][-1]
                        per = 4 // (st + 1)
                        for i in range(st + 1):
                            key = (tag, "s", k, i)
                            dve.wait_ge(*banks.filled(key))
                            ins = V.tensor_reduce(s_mx[:, k % 3, i * per:(i + 1) * per],
                                                  banks.bank(key).rearrange("p (h k) -> p h k", h=per), AX, ALU.max)
                        link(ins)
                        V.tensor_scalar(s_nb[:, k % 3, :], s_mx[:, k % 3, :], -scale, None, ALU.mult).then_inc(sh_ready, 1)
                    if 1 <= k < len(units) + 1:
                        m = k - 1
                        dve.wait_ge(*banks.emptied((tag, "s", m, units[m][-1])))
                        V.reciprocal(s_ri[:, m % 4, :], s_sm[:, m % 3, :]).then_inc(si_ready, 1)
                    if 3 <= k < len(units) + 3 and units[k - 3][-1]:
                        m = k - 3
                        if m >= 2:
                            dve.wait_ge(*banks.filled((tag, "o", m - 2)))
                        copy_out((tag, "pt", m, 1), s_pt[:, m % 2, 1, :])
                    if k >= 4:
                        after(k - 4, units[k - 4])

            def a_after(n, unit):
                b, g, st = unit
                copy_out(("a", "o", n), QKT[:, 4 * g:4 * g + 4, (2 * b + st) * P:(2 * b + st + 1) * P])

            softmax_units("a", A_UNITS, 0, float(P) ** -0.5, a_after)
            turned_norm(4, added("ao"))
            ended(dve, 7)

            def y_after(n, unit):
                b, ct, hg, st = unit
                copy_out(("y", "o", n), y_ax[ct][:, hg, (2 * b + st) * P:(2 * b + st + 1) * P], lambda ps: ps[:, 0:P])

            softmax_units("y", Y_UNITS, len(A_UNITS), 0.25, y_after)
            turned_norm(5, added("yo"))
            ended(dve, 8)

            for half in range(2):
                for kc in range(KC):
                    cols = slice(half * HALF, (half + 1) * HALF)
                    dve.wait_ge(x_high, KC * half + kc + 1)
                    V.tensor_tensor(m_HTl[:, kc, cols], HT[5][:, kc, cols], m_HTh[:, kc, cols].bitcast(F32),
                                    ALU.subtract).then_inc(x_low, 1)
            dve.wait_ge(moe1_loaded, 16 * 11)

            def hidden(n):
                key = ("g1", n)
                ps = banks.take(key, "dve")
                dve.wait_ge(*banks.filled(key))
                dve.wait_ge(*banks.emptied(("u1", n)))
                if n >= 3:
                    dve.wait_ge(h_low, n - 2)
                V.tensor_tensor(m_h[:, n % 3, :], m_su[:, n % 2, :], ps, ALU.mult).then_inc(emptied["dve"], 1)

            copy_out("logits1", f_l[:, :, :], lambda ps: ps[:, 0:NT * E1].rearrange("p (t e) -> p t e", t=NT))
            dve.wait_ge(*banks.emptied("logits1"))
            link(V.tensor_reduce(f_mx[:, 0, :], f_l[:, :, :], AX, ALU.max))
            V.tensor_tensor(f_e[:, :, :], f_l[:, :, :], bcast(f_mx[:, 0, :], E1), ALU.subtract).then_inc(e_shift, 1)
            link(V.tensor_tensor(f_b[:, :, :], f_l[:, :, :], m_rb[:, :].unsqueeze(1).to_broadcast([P, NT, E1]), ALU.add))
            first_choice(f_b[:, :, :], E1, f_oh[:, :, :], 1)
            hidden(0)
            link(V.scalar_tensor_tensor(f_b[:, :, :], f_oh[:, :, :], NEG, f_b[:, :, :], ALU.mult, ALU.add))
            first_choice(f_b[:, :, :], E1, f_oh2[:, :, :], 1)
            link(V.tensor_tensor(f_oh[:, :, :], f_oh[:, :, :], f_oh2[:, :, :], ALU.add))
            dve.wait_ge(e_exp, 2)
            link(V.tensor_tensor(f_v[:, :, :], f_oh[:, :, :], f_e[:, :, :], ALU.mult))
            link(V.tensor_reduce(f_mx[:, 1, :], f_v[:, :, :], AX, ALU.add))
            link(V.reciprocal(f_mx[:, 2, :], f_mx[:, 1, :]))
            link(V.memset(f_comb[:, :, E1:E1X], 1.0))
            link(V.tensor_tensor(f_comb[:, :, 0:E1], f_v[:, :, :], bcast(f_mx[:, 2, :], E1), ALU.mult))
            for n in range(1, 2 * E1X + 2):
                if n < 2 * E1X:
                    hidden(n)
                if n >= 2:
                    for i in range(2):
                        weigh(("d1", n - 2, i), n - 2, (n - 2) // 2)
            ended(dve, 9)

        @block.gpsimd
        def _(pool):
            G = nc.gpsimd
            steps = [0]

            def link(ins):
                steps[0] += 1
                ins.then_inc(pool_step, 1)
                pool.wait_ge(pool_step, steps[0])

            link(G.memset(r_ones[:, :], 1.0))
            G.memset(ones[:, :], 1.0).then_inc(ones_set, 1)
            G.memset(KVR[:, :, LT - 1, :], 0.0).then_inc(kv_cleared, 1)
            pool.wait_ge(kv_loaded, 16 * (2 * B + 2))
            for b in range(B):
                r, half = KVR[:, b, :, :], D // 2
                G.tensor_tensor(kt1[:, :, :], r, cosk[:, :, :], ALU.mult)
                G.tensor_tensor(kt2[:, :, 0:half], r[:, :, half:D], sink[:, :, 0:half], ALU.mult)
                link(G.tensor_tensor(kt2[:, :, half:D], r[:, :, 0:half], sink[:, :, half:D], ALU.mult))
                link(G.tensor_tensor(r, kt1[:, :, :], kt2[:, :, :], ALU.add))
            pool.drain().then_inc(kv_roped, 1)
            ended(pool, 0)

            G.memset(W2[:, :, :, :], 0.0).then_inc(w2_cleared, 1)

            def split(p):
                w = W1[:, :, 3 * P * p:3 * P * (p + 1)]
                link(G.tensor_copy(z_w[p][0][:, :, :], w))
                G.tensor_tensor(z_w[p][1][:, :, :], w, z_w[p][0][:, :, :].bitcast(F32), ALU.subtract).then_inc(w1_split, 1)

            split(0)
            ended(pool, 1)
            split(1)
            def doubled(b):
                for s in range(2):
                    G.tensor_copy(DUP[:, :, s * D:(s + 1) * D], KVR[:, b, :, :]).then_inc(dup_ready, 1)

            doubled(0)
            for p in range(2, PAIRS):
                if p == PAIRS - 1:
                    pool.wait_ge(*banks.filled(("z", 0, 1, 2)))
                split(p)
            ended(pool, 2)
            for k in (*KH, *KL):
                link(G.memset(k[:, L:L + 1].bitcast(F32), 0.0))

            def query(b, j, v, st):
                if not isinstance(v, int) or 16 * b + v >= 2:
                    pool.wait_ge(sc_full, 4 * (16 * b + v - 1))
                G.tensor_copy(QC[st][:, :, :], QALL[:, j, b, :, st * P:(st + 1) * P]).then_inc(qc_ready, 1)

            def norm(b, v, st, hd):
                pool.wait_ge(p_rec, 2 * (16 * b + v) + hd + 1)
                G.tensor_tensor(pool_tick[:, 2 * st + hd:2 * st + hd + 1], ones[:, 0:1], ones[:, 0:1], ALU.mult)
                G.tensor_scalar(SC[st][hd][:, :], SC[st][hd][:, :], ri[:, st, hd:hd + 1], 1.0,
                                ALU.mult, ALU.mult).then_inc(p_norm, 1)

            def tile(b, j, v, st):
                norm(b, v, st, 0)
                if not isinstance(v, int):
                    query(b, j, v + 2, st)
                elif b + 1 < B:
                    query(b + 1, 0, v - 14, st)
                norm(b, v, st, 1)

            pool.wait_ge(q_moved[0], 32 * PAIRS)
            pool.wait_ge(q_moved[1], 32 * PAIRS)
            query(0, 0, 0, 0)
            query(0, 0, 1, 1)
            for b in range(B):
                if b + 1 < B:
                    pool.wait_ge(kt_full, 4 * (b + 1))
                    doubled(b + 1)
                with pool.Fori(0, PAIRS - 1) as j:
                    tile(b, bass.ds(j + 1, 1), 2 * j, 0)
                    tile(b, bass.ds(j + 1, 1), 2 * j + 1, 1)
                tile(b, None, 14, 0)
                tile(b, None, 15, 1)
            ended(pool, 3)
            ended(pool, 4)
            def head_tables(i, s):
                pool.wait_ge(gqa_bcast, 16 * 6)
                gain, bias = a_gb[:, 2 * i, :], a_gb[:, 2 * i + 1, :]
                link(G.tensor_tensor(a_gc[:, i, s, :], a_cos[:, s, :], gain, ALU.mult))
                link(G.tensor_tensor(a_gs[:, i, s, 0:64], a_sin[:, s, 0:64], gain[:, 64:128], ALU.mult))
                link(G.tensor_tensor(a_gs[:, i, s, 64:128], a_sin[:, s, 64:128], gain[:, 0:64], ALU.mult))
                link(G.tensor_tensor(a_bt[:, i, s, :], a_cos[:, s, :], bias, ALU.mult))
                link(G.tensor_tensor(a_tmp[:, s, 0:64], a_sin[:, s, 0:64], bias[:, 64:128], ALU.mult))
                link(G.tensor_tensor(a_tmp[:, s, 64:128], a_sin[:, s, 64:128], bias[:, 0:64], ALU.mult))
                link(G.tensor_tensor(a_bt[:, i, s, :], a_bt[:, i, s, :], a_tmp[:, s, :], ALU.add))
                pool.drain().then_inc(tables_ready, 1)

            for n in range(2 * E0):
                if n < 4:
                    head_tables(n // 2, n % 2)
                pool.wait_ge(h_high0, n + 1)
                G.tensor_tensor(f_hl[:, n % 3, :, :], f_h[:, n % 3, :, :], f_hh[:, n % 3, :, :].bitcast(F32),
                                ALU.subtract).then_inc(h_low0, 1)
            ended(pool, 5)

            def rotated(n):
                pool.wait_ge(m_part, n + 1)
                G.tensor_tensor(a_m1[:, n % 6, :], a_m1[:, n % 6, :], a_m2[:, n % 2, :], ALU.add).then_inc(m_sum, 1)

            def biased(n):
                i, s = n % 5 // 4, n // 5 % 2
                m1 = a_m1[:, n % 6, :].rearrange("p (h d) -> p h d", h=4)
                pool.wait_ge(m_scaled, n + 1)
                G.tensor_tensor(m1, m1, a_bt[:, i, s, :].unsqueeze(1).to_broadcast([P, 4, P]), ALU.add).then_inc(qk_ready, 1)

            for n in range(5 * NT + 2):
                if n < 5 * NT:
                    rotated(n)
                if n >= 2:
                    biased(n - 2)
            ended(pool, 6)
            G.memset(y_v[:, :, :, :, :], 0.0).then_inc(v_cleared, 1)

            def over_sums(n, unit, base_n):
                nk = P * (unit[-1] + 1)
                pool.wait_ge(si_ready, base_n + n + 1)
                for h in range(4):
                    ins = G.tensor_scalar(s_sc[:, n % 4, h, 0:nk], s_sc[:, n % 4, h, 0:nk], s_ri[:, n % 4, h:h + 1], 1.0,
                                          ALU.mult, ALU.mult)
                ins.then_inc(sn_ready, 1)

            for n, unit in enumerate(A_UNITS):
                over_sums(n, unit, 0)
            ended(pool, 7)
            def masked_keys(k, heads=range(8)):
                ct, b = k // B, k % B
                for h in heads:
                    ins = G.tensor_scalar(y_km[:, b, ct, h, :], y_kr[:, ct, b * T:(b + 1) * T], y_hm[:, h:h + 1], 1.0,
                                          ALU.mult, ALU.mult)
                    if h % 4 == 3:
                        ins.then_inc(km_ready, 1)

            masked_keys(0)
            masked_keys(1)
            for n, unit in enumerate(Y_UNITS):
                over_sums(n, unit, len(A_UNITS))
                if n // 4 + 2 < KC * B:
                    masked_keys(n // 4 + 2, range(2 * (n % 4), 2 * (n % 4) + 2))
            link(G.memset(y_wop[:, :, :, :], 0.0))
            for ot in range(KC):
                G.tensor_copy(y_wop[:, ot, :, 0:16], y_wo[:, ot, :].rearrange("p (h d) -> p h d", h=H)).then_inc(wo_padded, 1)
            ended(pool, 8)
            pool.wait_ge(moe1_loaded, 16 * 11)

            def weights_low(e):
                for i, w in enumerate((m_wu, m_wg, m_wd)):
                    pool.wait_ge(w_high, 3 * e + i + 1)
                    G.tensor_tensor(m_wl[:, e % 3, i, :], expert(w, e), m_wh[:, e % 3, i, :].bitcast(F32),
                                    ALU.subtract).then_inc(w_low, 1)

            weights_low(0)
            for n in range(2 * E1X):
                if n % 2 == 0 and n // 2 + 1 < E1X:
                    weights_low(n // 2 + 1)
                pool.wait_ge(h_high, n + 1)
                G.tensor_tensor(m_hl[:, n % 3, :], m_h[:, n % 3, :], m_hh[:, n % 3, :].bitcast(F32), ALU.subtract).then_inc(h_low, 1)
            ended(pool, 9)

        @block.sync
        def _(sp):
            xv = x.rearrange("b (t p) c -> (b t) p c", p=P)
            ov = out.rearrange("b (t p) c -> (b t) p c", p=P)
            sp.dma_start(ident[:, :], ident_c).then_inc(consts_loaded, 16)
            for t in range(NT):
                sp.dma_start(X[:, t, :], xv[t]).then_inc(x_loaded[t // 4], 16)
            for w, a in enumerate((L0_attn_Wk, L0_attn_Wv, L0_attn_Wr, L0_attn_Wo)):
                sp.dma_start(r_nat[:, w, :, :], a.rearrange("(o p) i -> p o i", p=P)).then_inc(rwkv_loaded, 16)
            for dst, a in ((r_td, L0_attn_time_decay), (r_tf, L0_attn_time_first)):
                sp.dma_start(dst[:, :], a.rearrange("(k h) s -> (h s) k", k=KC)).then_inc(rwkv_loaded, 16)
            sp.dma_start(cosk[:, :, :], cosk_c).then_inc(kv_loaded, 16)
            sp.dma_start(sink[:, :, :], sink_c).then_inc(kv_loaded, 16)
            sp.wait_ge(kv_cleared, 1)
            for b in range(B):
                whole = (LT - 1) * P
                sp.dma_start(KVR[:, b, 0:LT - 1, :], ctx_512[b, 0:whole, :].rearrange("(t p) d -> p t d", p=P)).then_inc(kv_loaded, 16)
                sp.dma_start(KVR[0:LREST, b, LT - 1, :], ctx_512[b, whole:L, :]).then_inc(kv_loaded, 16)

            sp.dma_start(x_wq[:, :, :], L0_xattn_Wq.rearrange("(h k) c -> k h c", k=P)).then_inc(w1_loaded, 16)
            sp.dma_start(x_kcq[:, :, :], L0_xattn_w_kc_q.rearrange("h k q -> k h q")).then_inc(w1_loaded, 16)
            sp.dma_start(x_wqr[:, :, :], L0_xattn_W_qr.rearrange("h q r -> (h q) r").rearrange("(t p) r -> p t r", p=P)).then_inc(xattn_loaded, 16)
            sp.dma_start(x_wkr[:, :, :], L0_xattn_W_kr.rearrange("h d r -> (h d) r").rearrange("(t p) r -> p t r", p=P)).then_inc(xattn_loaded, 16)
            for ot in range(KC):
                sp.dma_start(x_wo[ot][:, :], L0_xattn_Wo[ot * P:(ot + 1) * P, :]).then_inc(xattn_loaded, 16)
            sp.wait_ge(kv_roped, 1)
            sp.dma_start(x_kckv[:, :, :], L0_xattn_w_kc_kv.rearrange("h k d -> k h d")).then_inc(kckv_loaded, 16)
            sp.dma_start(cosq[:, :, :], cosq_c).then_inc(rope_loaded, 16)
            sp.dma_start(sinq[:, :, :], sinq_c).then_inc(rope_loaded, 16)
            for n in range(2 * PAIRS):
                p, half, s = n // 2, n % 2, n % 2
                sp.wait_ge(*banks.emptied(("q", p, half)))
                for i in range(2):
                    o = slice((1 - i) * D, (2 - i) * D)
                    sp.dma_start(QALL[o, p, 2 * half:2 * half + 2, i, :].bitcast(F32),
                                 qlo[s][i * D:(i + 1) * D, :].bitcast(F32).rearrange("p (b t) -> p b t", b=2)).then_inc(q_moved[s], 16)
            sp.wait_ge(phase_ended, 4 * 4)
            sp.dma_start(g_nat[:, :], L0_ffn_gate_weight).then_inc(moe0_loaded, 16)
            sp.dma_start(f_rev[:, :, :], rev_c).then_inc(moe0_loaded, 16)
            sp.dma_start(f_tri[:, :], tri_c).then_inc(moe0_loaded, 16)
            sp.dma_start(f_w1[:, :, :, :], L0_ffn_w1.rearrange("e (k p) i -> p e k i", p=P)).then_inc(moe0_loaded, 16)
            sp.dma_start(f_w2[:, :, :, :], L0_ffn_w2.rearrange("e (k p) i -> p e k i", p=P)).then_inc(moe0_loaded, 16)
            sp.dma_start(a_nat[:, :, :], L1_attn_w_qkv.rearrange("(o p) c -> p o c", p=P)).then_inc(gqa_loaded, 16)
            sp.dma_start(a_wo[:, :, :], L1_attn_w_o.rearrange("(o p) k -> p o k", p=P)).then_inc(gqa_loaded, 16)
            sp.wait_ge(phase_ended, 4 * 5)
            sp.dma_start(a_cos[:, :, :], cos1_c).then_inc(gqa_bcast, 16)
            sp.dma_start(a_sin[:, :, :], sin1_c).then_inc(gqa_bcast, 16)
            for i, a in enumerate((L1_attn_qn_g, L1_attn_qn_b, L1_attn_kn_g, L1_attn_kn_b)):
                sp.dma_start(a_gb[:, i, :], a.partition_broadcast(P)).then_inc(gqa_bcast, 16)
            sp.wait_ge(phase_ended, 4 * 6)
            sp.dma_start(s_mask[:, :], mask_c).then_inc(masks_loaded, 16)
            sp.wait_ge(*banks.filled(("a", "o", len(A_UNITS) - 1)))
            sp.dma_start(y_wq[:, :, :], L1_xattn_Wq.rearrange("(o p) i -> p o i", p=P)).then_inc(lat_loaded, 16)
            sp.dma_start(y_wo[:, :, :], L1_xattn_Wout.rearrange("(o p) i -> p o i", p=P)).then_inc(lat_loaded, 16)
            sp.dma_start(y_wkv[:, :, :], L1_xattn_Wkv_expand.rearrange("(o p) i -> p o i", p=P)).then_inc(lat_loaded, 16)
            for b in range(B):
                sp.dma_start(y_lat[:, 2 * b:2 * b + 2, :], ctx_512[b, 0:T, :].rearrange("(t p) d -> p t d", p=P)).then_inc(lat_loaded, 16)
            sp.dma_start(y_hm[:, :], hmask_c).then_inc(lat_loaded, 16)
            sp.wait_ge(km_ready, 2 * KC * B)
            sp.dma_start(m_rw[:, :], L1_ffn_router_w).then_inc(moe1_loaded, 16)
            sp.dma_start(m_rb[:, :], L1_ffn_router_bias.partition_broadcast(P)).then_inc(moe1_loaded, 16)
            sp.dma_start(m_wg[:, 0:E1, :, :], L1_ffn_Wg.rearrange("e (k p) i -> p e k i", p=P)).then_inc(moe1_loaded, 16)
            sp.dma_start(m_wd[:, 0:E1, :], L1_ffn_Wd.rearrange("e i c -> i e c")).then_inc(moe1_loaded, 16)
            for it in range(2):
                sp.dma_start(m_wg[:, E1 + it, :, :], L1_ffn_Sg[0, :, it * P:(it + 1) * P].rearrange("(k p) i -> p k i", p=P)).then_inc(moe1_loaded, 16)
            sp.dma_start(m_wd[:, E1:E1X, :], L1_ffn_Sd[0].rearrange("(s i) c -> i s c", i=P)).then_inc(moe1_loaded, 16)
            sp.wait_ge(*banks.filled(("y", "s", len(Y_UNITS) - 1, 1)))
            sp.dma_start(m_wu[:, 0:E1, :, :], L1_ffn_Wu.rearrange("e (k p) i -> p e k i", p=P)).then_inc(moe1_loaded, 16)
            for it in range(2):
                sp.dma_start(m_wu[:, E1 + it, :, :], L1_ffn_Su[0, :, it * P:(it + 1) * P].rearrange("(k p) i -> p k i", p=P)).then_inc(moe1_loaded, 16)
            sp.dma_start(f_rev[:, :, :], rev_c).then_inc(moe1_loaded, 16)
            sp.wait_ge(phase_ended, 4 * 10)
            for t in range(NT):
                sp.dma_start(ov[t], X[:, t, :]).then_inc(stored, 16)
            sp.wait_ge(stored, 16 * NT)


def shape_constants():
    f = np.float32

    def angles(n, dim, base):
        inv = f(1.0) / np.power(f(base), np.arange(0, dim, 2, dtype=f) / f(dim), dtype=f)
        return np.arange(n, dtype=f)[:, None] * inv[None, :]

    c = {"ident_c": np.eye(P, dtype=f)}
    a = np.repeat(angles(T, QW, 10000.0), 2, axis=-1)
    cos, sin = np.cos(a), np.sin(a)
    half = QW // 2
    other = np.concatenate([sin[:, half:], -sin[:, :half]], axis=-1)
    pair = lambda t: np.tile(np.concatenate([t, t], -1).T.reshape(3, P, T).transpose(1, 0, 2), (1, 1, 2))
    c["cosq_c"], c["sinq_c"] = pair(cos), pair(other)
    a = np.zeros((LT * P, D), f)
    a[:L] = np.repeat(angles(L, D, 10000.0), 2, axis=-1)
    sign = np.concatenate([-np.ones(D // 2, f), np.ones(D // 2, f)])
    rows = lambda t: t.reshape(LT, P, D).transpose(1, 0, 2)
    c["cosk_c"], c["sink_c"] = rows(np.cos(a)), rows(np.sin(a) * sign)
    rev = np.arange(E1, 0, -1, dtype=f)
    c["rev_c"] = np.broadcast_to(rev, (P, NT, E1))
    c["tri_c"] = np.triu(np.ones((P, P), f), 1)
    a = angles(T, P, 1000000.0)
    rows = lambda t: np.concatenate([t, t], -1).reshape(2, P, P).transpose(1, 0, 2)
    sign = np.concatenate([-np.ones(P // 2, f), np.ones(P // 2, f)])
    c["cos1_c"], c["sin1_c"] = rows(np.cos(a)), rows(np.sin(a)) * sign
    tri = np.where(np.arange(P)[None, :] > np.arange(P)[:, None], f(NEG), f(0.0))
    c["mask_c"] = tri
    c["hmask_c"] = (np.arange(P)[:, None] // 16 == np.arange(8)[None, :]).astype(f)
    return {k: np.ascontiguousarray(v, dtype=f) for k, v in c.items()}


_INS = ['x', 'ctx_512', 'L0_attn_Wk', 'L0_attn_Wv', 'L0_attn_Wr', 'L0_attn_Wo', 'L0_attn_time_decay', 'L0_attn_time_first',
        'L0_xattn_Wq', 'L0_xattn_w_kc_q', 'L0_xattn_w_kc_kv', 'L0_xattn_W_qr', 'L0_xattn_W_kr', 'L0_xattn_Wo',
        'L0_ffn_gate_weight', 'L0_ffn_w1', 'L0_ffn_w2', 'L1_attn_w_qkv', 'L1_attn_w_o', 'L1_attn_qn_g', 'L1_attn_qn_b',
        'L1_attn_kn_g', 'L1_attn_kn_b', 'L1_xattn_Wq', 'L1_xattn_Wkv_expand', 'L1_xattn_Wout', 'L1_ffn_router_w',
        'L1_ffn_router_bias', 'L1_ffn_Wu', 'L1_ffn_Wg', 'L1_ffn_Wd', 'L1_ffn_Su', 'L1_ffn_Sg', 'L1_ffn_Sd']
_CONSTS = ['ident_c', 'cosq_c', 'sinq_c', 'cosk_c', 'sink_c', 'rev_c', 'tri_c', 'cos1_c', 'sin1_c', 'mask_c', 'hmask_c']
_OUTS = [((4, 256, 256), 'float32')]


def kernel(**inputs):
    import numpy as _np
    import concourse.bacc as _bacc
    from concourse import mybir as _mybir
    from concourse.bass_utils import run_bass_kernel_spmd as _run

    nc = _bacc.Bacc("TRN2", target_bir_lowering=False, num_devices=1)
    arrays, args = {}, []
    consts = shape_constants()
    for name in _INS + _CONSTS:
        a = _np.ascontiguousarray(inputs[name] if name in inputs else consts[name])
        arrays[f"in_{name}_dram"] = a
        args.append(nc.dram_tensor(f"in_{name}_dram", a.shape, _mybir.dt.from_np(a.dtype), kind="ExternalInput").ap())
    for i, (shape, dtype) in enumerate(_OUTS):
        dt = _mybir.dt.from_np(_np.dtype(dtype))
        args.append(nc.dram_tensor(f"out_{i}_dram", shape, dt, kind="ExternalOutput").ap())
    decoder(nc, *args)
    r = _run(nc, [arrays], core_ids=[0])
    got = tuple(r.results[0][f"out_{i}_dram"] for i in range(len(_OUTS)))
    return got[0]
```
